# Optimizing a Trainium2 kernel written in Bass

```python
import numpy as np
import jax
import jax.numpy as jnp

def _softmax(x, axis=-1):
    return jax.nn.softmax(x, axis=axis)

def _gelu(x):
    return jax.nn.gelu(x, approximate=True)

def _silu(x):
    return jax.nn.silu(x)

def _sigmoid(x):
    return jax.nn.sigmoid(x)

def _layernorm(x, axis=-1, eps=1e-05):
    m = jnp.mean(x, axis=axis, keepdims=True)
    v = jnp.var(x, axis=axis, keepdims=True)
    return (x - m) / jnp.sqrt(v + eps)

def _scatter_add(tgt, idx, src, axis=0):
    return tgt.at[idx].add(src)

def _segment_sum(src, seg, n):
    return jax.ops.segment_sum(src, seg, n)
kernel_name = 'mk_gnn_preln_d2_gnn_r16_b816f7'

def setup_inputs(seed: int=0):
    np.random.seed(seed)
    _w = jnp.asarray

    def _rec_inputs():
        import jax
        import jax.numpy as jnp
        _gk = jax.random.key(seed)
        x = -0.000202 + 1 * jax.random.normal(jax.random.fold_in(_gk, 1), (6250, 128), jnp.float32)
        _s = jax.random.randint(jax.random.fold_in(_gk, 2), (100000,), 0, 6250, jnp.int32)
        _d = jax.random.randint(jax.random.fold_in(_gk, 3), (100000,), 0, 6250, jnp.int32)
        _loop = jnp.arange(6250, dtype=jnp.int32)
        src = jnp.concatenate([_s, _d, _loop])
        dst = jnp.concatenate([_d, _s, _loop])
        _o = jnp.argsort(dst, stable=True)
        src = src[_o]
        dst = dst[_o]
        return (x, src, dst)
    x, src, dst = _rec_inputs()

    def _L0_gnn_setup():
        import jax, jax.numpy as jnp
        import numpy as np
        N = 3125
        E = 50000
        D = 128
        L = 2
        EPS = 1e-05

        def _layer_norm(y, g, b):
            mu = jnp.mean(y, axis=-1, keepdims=True)
            var = jnp.mean((y - mu) ** 2, axis=-1, keepdims=True)
            return (y - mu) * jax.lax.rsqrt(var + EPS) * g + b
        key = jax.random.key(seed)
        ks = jax.random.split(key, 16)
        x = jax.random.normal(ks[0], (N, D), dtype=jnp.float32)
        edge_index = jax.random.randint(ks[1], (2, E), 0, N, dtype=jnp.int64)
        s = 1.0 / np.sqrt(D)
        s2 = 1.0 / np.sqrt(2 * D)
        return {'x': x, 'edge_index': edge_index, 'W_enc': jax.random.normal(ks[2], (D, D), jnp.float32) * s, 'b_enc': jnp.zeros((D,), jnp.float32), 'msg_W1': jax.random.normal(ks[3], (L, D, 2 * D), jnp.float32) * s2, 'msg_b1': jnp.zeros((L, D), jnp.float32), 'msg_W2': jax.random.normal(ks[4], (L, D, D), jnp.float32) * s, 'msg_b2': jnp.zeros((L, D), jnp.float32), 'upd_W': jax.random.normal(ks[5], (L, D, 2 * D), jnp.float32) * s2, 'upd_b': jnp.zeros((L, D), jnp.float32), 'ln_g': jnp.ones((L, D), jnp.float32), 'ln_b': jnp.zeros((L, D), jnp.float32), 'W_out': jax.random.normal(ks[6], (D, D), jnp.float32) * s, 'b_out': jnp.zeros((D,), jnp.float32)}
    _L0_gnn_all = _L0_gnn_setup()
    _L0_gnn_in = {k: v for k, v in _L0_gnn_all.items() if k in ('W_enc', 'b_enc', 'msg_W1', 'msg_b1', 'msg_W2', 'msg_b2', 'upd_W', 'upd_b', 'ln_g', 'ln_b', 'W_out', 'b_out')}
    del _L0_gnn_all

    def _L1_gnn_setup():
        import jax, jax.numpy as jnp
        import numpy as np
        NUM_LAYERS = 3
        HIDDEN = 128
        N_NODES = 3125
        N_EDGES = 37500
        key = jax.random.key(seed)
        ks = jax.random.split(key, 5)
        x = jax.random.normal(ks[0], (N_NODES, HIDDEN), dtype=jnp.float32)
        edge_index = jax.random.randint(ks[1], (2, N_EDGES), 0, N_NODES, dtype=jnp.int32)
        scale = 1.0 / np.sqrt(HIDDEN)
        Wl = jax.random.uniform(ks[2], (NUM_LAYERS, HIDDEN, HIDDEN), jnp.float32, -scale, scale)
        bl = jnp.zeros((NUM_LAYERS, HIDDEN), dtype=jnp.float32)
        Wr = jax.random.uniform(ks[3], (NUM_LAYERS, HIDDEN, HIDDEN), jnp.float32, -scale, scale)
        return {'x': x, 'edge_index': edge_index, 'Wl': Wl, 'bl': bl, 'Wr': Wr}
    _L1_gnn_all = _L1_gnn_setup()
    _L1_gnn_in = {k: v for k, v in _L1_gnn_all.items() if k in ('Wl', 'bl', 'Wr')}
    del _L1_gnn_all
    return {'x': x, 'src': src, 'dst': dst, 'L0_gnn_W_enc': _L0_gnn_in['W_enc'], 'L0_gnn_b_enc': _L0_gnn_in['b_enc'], 'L0_gnn_msg_W1': _L0_gnn_in['msg_W1'], 'L0_gnn_msg_b1': _L0_gnn_in['msg_b1'], 'L0_gnn_msg_W2': _L0_gnn_in['msg_W2'], 'L0_gnn_msg_b2': _L0_gnn_in['msg_b2'], 'L0_gnn_upd_W': _L0_gnn_in['upd_W'], 'L0_gnn_upd_b': _L0_gnn_in['upd_b'], 'L0_gnn_ln_g': _L0_gnn_in['ln_g'], 'L0_gnn_ln_b': _L0_gnn_in['ln_b'], 'L0_gnn_W_out': _L0_gnn_in['W_out'], 'L0_gnn_b_out': _L0_gnn_in['b_out'], 'L1_gnn_Wl': _L1_gnn_in['Wl'], 'L1_gnn_bl': _L1_gnn_in['bl'], 'L1_gnn_Wr': _L1_gnn_in['Wr']}

def reference(x, src, dst, L0_gnn_W_enc, L0_gnn_b_enc, L0_gnn_msg_W1, L0_gnn_msg_b1, L0_gnn_msg_W2, L0_gnn_msg_b2, L0_gnn_upd_W, L0_gnn_upd_b, L0_gnn_ln_g, L0_gnn_ln_b, L0_gnn_W_out, L0_gnn_b_out, L1_gnn_Wl, L1_gnn_bl, L1_gnn_Wr):
    import jax
    import jax.numpy as jnp

    def _L0_gnn_ref(x, edge_index, W_enc, b_enc, msg_W1, msg_b1, msg_W2, msg_b2, upd_W, upd_b, ln_g, ln_b, W_out, b_out):
        import jax, jax.numpy as jnp
        import numpy as np
        N = 3125
        E = 50000
        D = 128
        L = 2
        EPS = 1e-05

        def _layer_norm(y, g, b):
            mu = jnp.mean(y, axis=-1, keepdims=True)
            var = jnp.mean((y - mu) ** 2, axis=-1, keepdims=True)
            return (y - mu) * jax.lax.rsqrt(var + EPS) * g + b
        h = x @ W_enc.T + b_enc
        row, col = (edge_index[0], edge_index[1])
        n_layers = msg_W1.shape[0]
        for l in range(n_layers):
            m = jnp.concatenate([h[row], h[col]], axis=-1)
            m = jax.nn.relu(m @ msg_W1[l].T + msg_b1[l])
            m = m @ msg_W2[l].T + msg_b2[l]
            agg = jax.ops.segment_sum(m, col, num_segments=h.shape[0])
            upd = jnp.concatenate([h, agg], axis=-1) @ upd_W[l].T + upd_b[l]
            h = _layer_norm(h + upd, ln_g[l], ln_b[l])
        return h @ W_out.T + b_out

    def _L1_gnn_ref(x, edge_index, Wl, bl, Wr):
        import jax, jax.numpy as jnp
        import numpy as np
        NUM_LAYERS = 3
        HIDDEN = 128
        N_NODES = 3125
        N_EDGES = 37500
        src = edge_index[0]
        dst = edge_index[1]
        n = x.shape[0]
        deg = jax.ops.segment_sum(jnp.ones(src.shape[0], dtype=x.dtype), dst, num_segments=n)
        inv_deg = (1.0 / jnp.maximum(deg, 1.0))[:, None]
        h = x
        for i in range(NUM_LAYERS):
            agg = jax.ops.segment_sum(h[src], dst, num_segments=n) * inv_deg
            h = agg @ Wl[i].T + bl[i] + h @ Wr[i].T
            if i < NUM_LAYERS - 1:
                h = jax.nn.relu(h)
        return h
    edge_index = jnp.stack([src, dst])
    h = jnp.maximum(_layernorm(x, axis=-1), 0.0)
    x = x + _L0_gnn_ref(h, edge_index, L0_gnn_W_enc, L0_gnn_b_enc, L0_gnn_msg_W1, L0_gnn_msg_b1, L0_gnn_msg_W2, L0_gnn_msg_b2, L0_gnn_upd_W, L0_gnn_upd_b, L0_gnn_ln_g, L0_gnn_ln_b, L0_gnn_W_out, L0_gnn_b_out)
    h = jnp.maximum(_layernorm(x, axis=-1), 0.0)
    x = x + _L1_gnn_ref(h, edge_index, L1_gnn_Wl, L1_gnn_bl, L1_gnn_Wr)
    return x

_drawn_inputs = setup_inputs


def setup_inputs(seed=0):
    import zlib

    import numpy as np

    out = dict(_drawn_inputs(seed))
    spreads = {'L0_gnn_b_enc': (0.0, 0.1),
     'L0_gnn_msg_b1': (0.0, 0.1),
     'L0_gnn_msg_b2': (0.0, 0.1),
     'L0_gnn_upd_b': (0.0, 0.8),
     'L0_gnn_ln_g': (1.0, 0.2),
     'L0_gnn_ln_b': (0.0, 0.1),
     'L0_gnn_b_out': (0.0, 0.1),
     'L1_gnn_bl': (0.0, 0.1)}
    factors = {}
    for name, (base, spread) in spreads.items():
        noise = np.random.default_rng([zlib.crc32(name.encode()), seed]).standard_normal(out[name].shape)
        drawn = base * np.exp(spread * noise) if base else spread * noise
        out[name] = jnp.asarray(drawn.astype(out[name].dtype))
    for name, factor in factors.items():
        out[name] = (out[name] * factor).astype(out[name].dtype)
    return out
```

```python
from contextlib import ExitStack

import concourse.bass as bass
from concourse import mybir

F32 = mybir.dt.float32
BF16 = mybir.dt.bfloat16
I32 = mybir.dt.int32
ALU = mybir.AluOpType
ACT = mybir.ActivationFunctionType
AX = mybir.AxisListType.X

N = 6250
E = 206250
D = 128
P = 125
NT = N // P
ET = E // P
PAIRS = ET // 2
L0 = 2
L1 = 3
EPS = 1e-5
PARTS = 3
ROW = PARTS * D
W = D + 1

CELL = 128
MORE = 2
CELLS = NT + MORE
GROUP = 4
GROUPS = CELLS // GROUP
BANKS = 4
BODY = 2 * GROUPS
CHUNKS = [(0, 3), (3, 2), (5, 2), (7, 2), (9, 2), (11, 2)]
SAMPLE = 33
COLS = 36
WIN = 128 * COLS
RG = 4
RK = COLS // RG
MAGIC = 1.5 * 2.0 ** 23

assert CELLS % GROUP == 0 and RG * RK == COLS and ET % SAMPLE == 0 and sum(n for _, n in CHUNKS) == GROUPS

assert NT * P == N and ET * P == E and NT % 2 == 0 and ET % 2 == 0

ENC, MSG, UPD_H, UPD_M, OUT, LIN_L, LIN_R = 0, 1, 5, 7, 9, 10, 13
NW = 16
B_ENC, B_1, B_UPD, LN_G, LN_B, B_OUT, B_LIN = 0, 1, 3, 5, 7, 9, 10
NB = 13
LOADS = NW + 2 * L0 + NB
STAGES = ["enc", "ab0", "upd0", "ab1", "upd1", "out", "lin0", "lin1", "lin2"]
STAGE0 = {name: 2 + NT * k for k, name in enumerate(STAGES)}
EDGE = ["ab0", "ab1", "lin0", "lin1", "lin2"]
AGG_STAGES = ["upd0", "upd1", "lin0", "lin1", "lin2"]
HI0 = [0, NT, 2 * NT, 2 * NT + 1, 2 * NT + 2]


class Steps:

    def __init__(self, eng, sem):
        self.eng, self.sem, self.base, self.k, self.i, self.per = eng, sem, 0, 0, None, 0

    def now(self):
        return self.base + self.k if self.i is None else self.i * self.per + (self.base + self.k)

    def did(self, ins):
        ins.then_inc(self.sem, 1)
        self.k += 1
        return self.now()

    def after(self, value):
        self.eng.wait_ge(self.sem, value)

    def last(self):
        self.after(self.now())

    def enter(self, i, per):
        self.base, self.k, self.i, self.per = self.base + self.k, 0, i, per

    def leave(self, times):
        assert self.k == self.per, (self.k, self.per)
        self.base, self.k, self.i = self.base + times * self.per, 0, None


def build(nc, x, src, dst, W_enc, b_enc, msg_W1, msg_b1, msg_W2, msg_b2, upd_W, upd_b, ln_g, ln_b,
          W_out, b_out, Wl, bl, Wr, out):
    with ExitStack() as ctx:
        def sb(name, shape, dt=F32):
            return ctx.enter_context(nc.sbuf_tensor(name, shape, dt))

        def sem(name):
            return ctx.enter_context(nc.semaphore(name))

        table_dram = [nc.dram_tensor(f"table_{n}", [N, ROW], BF16, kind="Internal").ap() for n in "ab"]
        sums_dram = [nc.dram_tensor(f"sums_{u}", [N + P, W], F32, kind="Internal").ap() for u in range(2)]

        slots_dram = nc.dram_tensor("slots_turned", [NT, 2, CELLS, CELL], BF16, kind="Internal").ap()

        Hf = sb("Hf", [128, NT * D])
        H = Hf[0:P, :].rearrange("p (t d) -> p t d", d=D)
        AGGf = sb("AGGf", [128, NT * W])
        AGG = AGGf[0:P, :].rearrange("p (t d) -> p t d", d=W)
        half = NT * ROW // 2
        tabf = sb("tabf", [128, 2 * half])
        TAB = tabf[0:P, :].bitcast(BF16).rearrange("p (n t c d) -> p n t c d", n=2, t=NT, c=PARTS)
        wnat = tabf[:, 0:(NW + L0) * D].rearrange("p (w d) -> p w d", d=D)
        AGG1 = tabf[0:P, 0:NT * W].rearrange("p (t d) -> p t d", d=W)
        X = tabf[0:P, half:half + NT * D].rearrange("p (t d) -> p t d", d=D)
        wT = sb("wT", [D, NW, D])
        wM = sb("wM", [D, L0, D])
        bias = sb("bias", [P, NB, D])
        b2col = sb("b2col", [D, L0])
        b2rep = sb("b2rep", [D, L0, P])
        b2upd = sb("b2upd", [P, L0, D])
        abias = sb("abias", [P, L0, 2, D])
        ident = sb("ident", [128, 128])
        before = sb("before", [P, P])
        ones = sb("ones", [128, 128])
        eps = sb("eps", [P, 1])
        stats = sb("stats", [P, NT, 6])
        mean = sb("mean", [P, NT])
        var = sb("var", [P, NT])
        std = sb("std", [P, NT])
        rstd = sb("rstd", [P, NT])
        sq = sb("sq", [P, NT])
        degc = sb("degc", [P, NT])
        invdeg = sb("invdeg", [P, NT])
        ones_bf = sb("ones_bf", [128, 128], BF16)
        ident_bf = sb("ident_bf", [128, 128], BF16)
        below_bf = sb("below_bf", [128, 128], BF16)
        col0 = sb("col0", [128, 128], BF16)
        col1 = sb("col1", [128, 128], BF16)
        row1 = sb("row1", [128, 1])
        tilec = sb("tilec", [128, 3, NT + 2])
        junk = sb("junk", [P, 1])
        zrow = sb("zrow", [P, W])
        msg = sb("msg", [P, 2, W])
        slots = sb("slots", [128, 2, NT + 1, CELLS], BF16)
        lo = sb("lo", [1, NT + 2])
        loi = sb("loi", [1, NT + 2], I32)
        placed = sb("placed", [128, 1])
        missing = sb("missing", [1, 2])
        missingi = sb("missingi", [1, 1], I32)

        arena_words = 10740
        arena = sb("arena", [128, arena_words])

        def carver(memory, words):
            at = [0]

            def carve(shape, dt=F32):
                n = 1
                for k in shape[1:]:
                    n *= k
                size = (n + 1) // 2 if dt == BF16 else n
                a = memory[0:shape[0], at[0]:at[0] + size]
                at[0] += size
                assert at[0] <= words, (at[0], words)
                if dt != F32:
                    a = a.bitcast(dt)[:, 0:n]
                dims = " ".join(f"d{k}" for k in range(1, len(shape)))
                return a.rearrange(f"p ({dims}) -> p {dims}", **{f"d{k}": shape[k] for k in range(1, len(shape))})
            return carve

        carve = carver(arena, arena_words)
        tile_in = carve([P, 2, 2, D])
        hT = carve([128, 2, 2, 128])
        raw = carve([P, 2, 2, D])
        rest = carve([P, 2, 2, D])
        tmp = carve([P, 2, 2, D])
        carve = carver(arena, arena_words)
        srci = carve([P, ET], I32)
        dsti = carve([P, ET], I32)
        sidx = carve([P, 2], I32)
        didx = carve([P, 2], I32)
        widx = carve([P, 2], I32)
        dcol = carve([P, 2])
        drep = carve([P, 2, P])
        same = carve([P, 2, P])
        earlier = carve([P, 2, P])
        nearl = carve([P, 2])
        wsel = carve([P, 2, 2])
        rows = carve([P, 2, 2, PARTS, D], BF16)
        part = carve([P, 2, 2, D])
        msum = carve([P, 2, W])
        carve = carver(arena, arena_words)
        slist = [carve([P, 2, n * GROUP * CELL], BF16) for _, n in (CHUNKS[0], CHUNKS[1])]
        toN = carve([P, 4, 2, GROUP * CELL], BF16)
        toE = carve([128, 4, GROUP, 126], BF16)
        mparts = carve([128, 4, PARTS, GROUP, W + 1], BF16)
        mrest = carve([128, 2, GROUP, D])
        cur = carve([P, 2, 2, ROW], BF16)
        curS = carve([128, 2, CELLS, 2], BF16)
        carve = carver(arena, arena_words)
        oneE = carve([128, 4, GROUP, 2, 126], BF16)
        cells = carve([P, 4, GROUP, 126], BF16)
        cur2 = carve([P, 2, ROW], BF16)
        curS2 = carve([128, 2, CELLS, 2, 2], BF16)
        carve = carver(Hf, NT * D)
        one_cell = carve([128, 2, COLS, NT], BF16)
        payload = carve([128, 2, COLS, 2, CELLS], BF16)
        carve = carver(AGGf, NT * W)
        one_slot = carve([128, COLS, CELL], BF16)
        prod = carve([128, RG, RK * NT])
        carve = carver(Hf, NT * D)
        dstl = carve([P, ET], I32)
        samp = carve([P, NT])
        less = carve([P, NT + 1, NT])
        nless = carve([P, NT + 1])
        carve = carver(arena, arena_words)
        win = carve([128, 2, 2, COLS], I32)
        node = carve([128, 2, 2, COLS])
        off1 = carve([128, 2, 2, COLS])
        srct = carve([128, 2, 3, COLS])
        inside = carve([128, 2, 2, COLS])
        q1 = carve([128, 2, COLS, 2], BF16)
        rank = carve([128, 2, COLS])
        over = carve([128, 3, COLS])
        ondiag = carve([128, COLS])
        step3 = carve([128, 3, COLS])
        keep = carve([128, 3, COLS])
        pay = carve([128, 2, 2, 3, COLS])
        slot = carve([128, 2, COLS, 2], BF16)
        pay2 = carve([128, 2, COLS, 2], BF16)
        rtot = carve([128, 2, RG, NT], BF16)
        Sb = carve([128, 2, 2 * CELLS], BF16)
        STb = carve([2 * CELLS, 2, CELL], BF16)
        filled = carve([128, NT, CELLS])
        counti = carve([128, 128], I32)
        rowi = carve([128, 1], I32)
        tilei = carve([128, 3, NT + 2], I32)
        junki = carve([P, 1], I32)

        psum = ctx.enter_context(nc.psum_tensor("psum", [128, 8, 512], F32))
        bank = [psum[:, k, :] for k in range(8)]
        psRank = psum[:, 0:RG, 0:RK * NT]
        psTot, psSlot, psTurn, psCount = bank[4], bank[5], bank[6], bank[7]
        psMsg, psA = bank[0:BANKS], bank[4:6]
        psT = [bank[0], bank[1]]
        psO = [bank[2], bank[3]]
        psD = [bank[4], bank[5]]
        psM = [bank[6], bank[7]]

        s_w = sem("weights_loaded")
        s_x = sem("x_loaded")
        s_e = sem("edges_loaded")
        s_const = sem("constants_ready")
        s_wT = sem("weight_transposed")
        s_wTc = sem("weight_copied")
        s_b2 = sem("b2_spread")
        s_comp = sem("composed_ready")
        s_compc = sem("composed_copied")
        s_in = sem("tile_staged")
        s_tT = sem("tile_transposed")
        s_tC = sem("tile_copied")
        s_tO = sem("tile_product_ready")
        s_tE = sem("tile_finished")
        s_raw = sem("raw_ready")
        s_hi = sem("high_part_ready")
        s_rest = sem("rest_ready")
        s_mid = sem("middle_part_ready")
        s_dve = sem("vector_step")
        s_var = sem("variance_ready")
        s_std = sem("std_ready")
        s_h = sem("hidden_ready")
        s_tab = sem("linear_table_ready")
        s_agg = sem("aggregate_ready")
        s_fin = sem("result_ready")
        s_out = sem("result_stored")
        s_pset = sem("constant_step")
        gate = {e: sem(f"gate_{e}") for e in ("act", "dve", "pool")}
        g_tab = sem("general_table_stored")
        g_zero = sem("general_sums_cleared")
        g_idx = sem("general_indices_copied")
        g_rows = [[sem(f"general_rows_gathered{k}_{u}") for u in range(2)] for k in range(len(EDGE))]
        g_drep = sem("general_destinations_spread")
        g_dT = sem("general_destinations_turned")
        g_same = sem("general_equal_destinations_found")
        g_widx = sem("general_write_rows_ready")
        g_msg = sem("general_messages_ready")
        g_sum = sem("general_messages_summed")
        g_cp = sem("general_sums_copied")
        g_add = [[sem(f"general_sums_added{k}_{u}") for u in range(2)] for k in range(len(EDGE))]
        g_back = sem("general_sums_loaded")
        g_dve = sem("general_vector_step")

        o_dst = sem("sort_destinations_loaded")
        o_less = sem("sort_samples_counted")
        o_nless = sem("sort_starts_summed")
        o_lo = sem("sort_starts_ready")
        o_win = [sem(f"sort_window_loaded{u}") for u in range(2)]
        o_read = sem("sort_window_read")
        o_cell = sem("sort_cells_ready")
        o_tot = sem("sort_totals_ready")
        o_totc = sem("sort_totals_copied")
        o_rank = sem("sort_ranks_ready")
        o_prod = sem("sort_ranks_picked")
        o_pay = sem("sort_payload_ready")
        o_mul = sem("sort_payload_placed")
        o_mulv = sem("sort_sources_placed")
        o_slot = sem("sort_slots_ready")
        o_perm = sem("sort_slots_filled")
        o_S = sem("sort_slots_copied")
        o_turn = sem("sort_slots_turned")
        o_ST = sem("sort_turned_copied")
        o_store = [sem(f"sort_slots_stored{u}") for u in range(2)]
        o_dve = sem("sort_vector_step")
        o_fill = sem("sort_fill_counted")
        o_sum = sem("sort_fill_summed")
        o_flag = sem("sort_flag_ready")
        f_list = [sem(f"cells_slot_list_loaded{b}") for b in range(2)]
        f_cur = [sem(f"cells_tile_rows_copied{u}") for u in range(2)]
        f_own = sem("cells_tile_slots_copied")
        f_one = sem("cells_count_column_set")
        f_toN = sem("cells_node_onehots_ready")
        f_toE = sem("cells_slot_onehots_ready")
        f_gat = sem("cells_rows_gathered")
        f_hi = sem("cells_high_part_ready")
        f_rest = sem("cells_rest_ready")
        f_mid = sem("cells_middle_part_ready")
        f_lo = sem("cells_low_part_ready")
        f_sca = sem("cells_messages_summed")
        f_agg = sem("cells_aggregate_copied")
        l_cur = [sem(f"linear_tile_rows_copied{u}") for u in range(2)]
        l_own = sem("linear_tile_slots_copied")
        l_from = sem("linear_onehots_ready")
        l_C = sem("linear_counts_ready")
        l_Cc = sem("linear_counts_copied")
        l_sum = sem("linear_rows_summed")
        l_agg = sem("linear_aggregate_copied")

        def hold(eng, name, s, value):
            eng.wait_ge(s, value)
            eng.sem_inc(gate[name], 1)

        def load_flag(eng):
            eng.wait_ge(o_flag, 1)
            return eng.value_load(missingi[0:1, 0:1], min_val=0, max_val=1)

        def edge_sp(sp, k, miss):
            with sp.If(miss < 1):
                cells_sp(sp, k) if k < L0 else linear_sp(sp, k - L0)
            with sp.If(miss > 0):
                general_sp(sp, k)

        def edge_pool(pool, k, miss):
            with pool.If(miss < 1):
                cells_pool(pool, k) if k < L0 else linear_pool(pool, k - L0)
            with pool.If(miss > 0):
                general_pool(pool, k)

        def edge_pe(pe, k, miss):
            with pe.If(miss < 1):
                cells_pe(pe, k) if k < L0 else linear_pe(pe, k - L0)
            with pe.If(miss > 0):
                general_pe(pe, k)

        def edge_act(act, k, miss):
            with act.If(miss < 1):
                cells_act(act, k) if k < L0 else linear_act(act, k - L0)
            with act.If(miss > 0):
                general_act(act, k)

        def edge_dve(dve, step, k, miss):
            with dve.If(miss < 1):
                cells_dve(dve, k) if k < L0 else counts_dve(dve, k - L0)
            with dve.If(miss > 0):
                general_dve(dve, step, k)

        def pairs(a):
            return a.rearrange("p c (n e) -> p c n e", e=2)

        def columns(numbers, width, count):
            a = numbers[:, 0:width].rearrange("p (o n e) -> p o n e", o=1, e=2)
            return a.to_broadcast([128, count, width // 2, 2])

        def along(values, width):
            c = values.shape[1]
            return values.rearrange("p c (o e) -> p c o e", o=1).to_broadcast([128, c, width // 2, 2])

        def twice(a):
            return a.rearrange("p (t o) -> p t o", o=1).to_broadcast([128, COLS, 2])

        def sort_sp(sp):
            sp.dma_start(dstl, dst.rearrange("(p t) -> p t", p=P)).then_inc(o_dst, 16)
            sp.wait_ge(o_lo, 1)

            def window(t, u):
                start = sp.value_load(loi[0:1, t], min_val=0, max_val=E - WIN)
                for n, ends in enumerate((src, dst)):
                    sp.dma_start(win[:, u, n, :], ends[bass.ds(start, WIN)].rearrange("(p t) -> p t", p=128)
                                 ).then_inc(o_win[u], 16)

            window(slice(0, 1), 0)
            with sp.Fori(0, NT // 2) as i:
                for u in range(2):
                    sp.wait_ge(o_read, i * 2 + (u + 2))
                    window(bass.ds(i * 2 + (u + 1), 1), 1 - u)

        def sort_pool(pool):
            with pool.Fori(0, NT // 2) as i:
                for u in range(2):
                    hold(pool, "pool", o_pay, i * 2 + (u + 3))
                    hold(pool, "pool", o_perm, i * 2 + (u + 1))
                    pool.tensor_copy(payload[:, u, :, :, NT:CELLS], pay[:, u, :, 1:3, :].rearrange("p n m t -> p t n m"))
                    pool.tensor_tensor(payload[:, u, :, 1, 0:NT], one_cell[:, u],
                                       pay[:, u, 1, 0, :].rearrange("p (t o) -> p t o", o=1).to_broadcast([128, COLS, NT]),
                                       ALU.mult).then_inc(o_mul, 1)

        def sort_pe(pe):
            pe.wait_ge(o_less, 1)
            pe.matmul(psCount[0:1, 0:NT + 1], ones[0:P, 0:1], nless, start=True, stop=True).then_inc(o_nless, 1)

            def ranks(n, u):
                pe.wait_ge(o_cell, n + 3)
                pe.wait_ge(o_totc, n + 2)
                cell = one_cell[:, u].rearrange("p (g k) c -> p g k c", g=RG)
                for k in range(RK):
                    m = pe.matmul(psTot[:, 0:RG * NT].rearrange("p (g c) -> p g c", g=RG), ident_bf[:], cell[:, :, k, :],
                                  start=k == 0, stop=k == RK - 1)
                m.then_inc(o_tot, 1)
                pe.wait_ge(o_prod, n + 2)
                pe.wait_ge(o_totc, n + 3)
                for g in range(RG):
                    bk = psRank[:, g, :].rearrange("p (k c) -> p k c", k=RK)
                    all_k = [128, RK, NT]
                    pe.matmul(bk, below_bf[:], rtot[:, u, g:g + 1, :].to_broadcast(all_k), start=True, stop=False)
                    for e in range(g):
                        pe.matmul(bk, ones_bf[:], rtot[:, u, e:e + 1, :].to_broadcast(all_k), start=False, stop=False)
                    for k in range(RK - 1):
                        m = pe.matmul(bk[:, k + 1:RK, :], ident_bf[:], cell[:, g, k:k + 1, :].to_broadcast([128, RK - 1 - k, NT]),
                                      start=False, stop=k == RK - 2)
                m.then_inc(o_rank, 1)

            def fill(n, u):
                pe.wait_ge(o_slot, n + 3)
                pe.wait_ge(o_mul, n + 3)
                pe.wait_ge(o_mulv, n + 3)
                pe.wait_ge(o_S, n + 2)
                for t in range(COLS):
                    m = pe.matmul(psSlot[:, 0:2 * CELLS], one_slot[:, t, :],
                                  payload[:, u, t].rearrange("p n c -> p (n c)"), start=t == 0, stop=t == COLS - 1)
                m.then_inc(o_perm, 1)
                pe.wait_ge(o_ST, n + 2)
                pe.wait_ge(o_S, n + 3)
                pe.transpose(psTurn[0:2 * CELLS, 0:CELL // 2].bitcast(BF16), Sb[:, u, :], ident_bf[:]).then_inc(o_turn, 1)

            ranks(0, 0)
            with pe.Fori(0, NT // 2) as i:
                for u in range(2):
                    ranks(i * 2 + (u + 1), 1 - u)
                    fill(i * 2 + u, u)
            pe.wait_ge(o_fill, 1)
            pe.matmul(psCount[0:1, 64:65], ones[:, 0:1], placed[:], start=True, stop=True).then_inc(o_sum, 1)

        def sort_act(act):
            def totals(n, u):
                act.wait_ge(o_tot, n + 3)
                act.wait_ge(o_rank, n + 2)
                act.copy(rtot[:, u], psTot[:, 0:RG * NT].rearrange("p (g c) -> p g c", g=RG)).then_inc(o_totc, 1)

            totals(0, 0)
            with act.Fori(0, NT // 2) as i:
                for u in range(2):
                    totals(i * 2 + (u + 1), 1 - u)
                    hold(act, "act", o_turn, i * 2 + (u + 1))
                    hold(act, "act", o_perm, i * 2 + (u + 3))
                    act.copy(slots[:, :, bass.ds(i * 2 + u, 1), :], psSlot[:, 0:2 * CELLS].rearrange("p (n o c) -> p n o c", n=2, o=1))
                    act.copy(Sb[:, u, :], psSlot[:, 0:2 * CELLS]).then_inc(o_S, 1)
                    act.wait_ge(o_turn, i * 2 + (u + 3))
                    act.wait_ge(o_store[u], i * 16 + 16)
                    act.copy(STb[:, u, :], psTurn[0:2 * CELLS, 0:CELL // 2].bitcast(BF16)).then_inc(o_ST, 1)
                    act.wait_ge(o_ST, i * 2 + (u + 3))
                    act.dma_start(slots_dram[bass.ds(i * 2 + u, 1)].rearrange("o n c e -> (o n c) e"), STb[:, u, :]
                                  ).then_inc(o_store[u], 16)
            for u in range(2):
                act.wait_ge(o_store[u], 16 + 16 * (NT // 2))

        def sort_dve(dve):
            step = Steps(dve, o_dve)
            dve.wait_ge(o_dst, 16)
            step.did(dve.tensor_copy(samp, dstl[:, 0:ET:SAMPLE]))
            step.last()
            grid = [P, NT + 1, NT]
            step.did(dve.tensor_tensor(less, samp.rearrange("p (o t) -> p o t", o=1).to_broadcast(grid),
                                       tilec[0:P, 0, 0:NT + 1].rearrange("p (t o) -> p t o", o=1).to_broadcast(grid), ALU.is_lt))
            step.last()
            dve.tensor_reduce(nless, less, AX, ALU.add).then_inc(o_less, 1)
            dve.wait_ge(o_nless, 1)
            step.did(dve.tensor_scalar(lo[:, 0:NT + 1], psCount[0:1, 0:NT + 1], float(SAMPLE), float(1 - SAMPLE), ALU.mult, ALU.add))
            step.last()
            dve.tensor_scalar(loi[:, 0:NT + 1], lo[:, 0:NT + 1], 0.0, float(E - WIN), ALU.max, ALU.min).then_inc(o_lo, 1)

            def find_cells(n, u, loaded, tile):
                dve.wait_ge(o_win[u], loaded)
                a = step.did(dve.tensor_copy(node[:, u], win[:, u]))
                step.after(a)
                dve.sem_inc(o_read, 1)
                t = [srct[:, u, k, :] for k in range(3)]
                a = step.did(dve.tensor_scalar(t[0], node[:, u, 0, :], 1.0 / P, -((P - 1) / 2) / P, ALU.mult, ALU.add))
                hold(dve, "dve", o_dve, a)
                b = step.did(dve.tensor_scalar(off1[:, u, 1, :], node[:, u, 1, :], tilec[:, 1, tile], None, ALU.subtract))
                a = step.did(dve.tensor_scalar(t[1], t[0], MAGIC, None, ALU.add))
                step.after(b)
                b = step.did(dve.tensor_scalar(inside[:, u, 0, :], off1[:, u, 1, :], 1.0, None, ALU.is_ge))
                step.after(a)
                a = step.did(dve.tensor_scalar(t[2], t[1], MAGIC, None, ALU.subtract))
                step.after(b)
                b = step.did(dve.scalar_tensor_tensor(out=inside[:, u, 1, :], in0=off1[:, u, 1, :], scalar=float(P),
                                                      in1=inside[:, u, 0, :], op0=ALU.is_le, op1=ALU.mult))
                step.after(b)
                b = step.did(dve.scalar_tensor_tensor(out=q1[:, u], in0=twice(t[2]), scalar=1.0, in1=twice(inside[:, u, 1, :]),
                                                      op0=ALU.add, op1=ALU.mult))
                a = step.did(dve.scalar_tensor_tensor(out=t[0], in0=t[2], scalar=-float(P), in1=node[:, u, 0, :],
                                                      op0=ALU.mult, op1=ALU.add))
                step.after(a)
                a = step.did(dve.tensor_scalar(off1[:, u, 0, :], t[0], 1.0, None, ALU.add))
                step.after(b)
                dve.wait_ge(o_mul, n + 1)
                dve.wait_ge(o_mulv, n + 1)
                dve.tensor_tensor(pairs(one_cell[:, u]), columns(col1, NT, COLS), along(q1[:, u], NT), ALU.is_equal).then_inc(o_cell, 1)
                return a

            def find_slots(n, u, tile):
                dve.wait_ge(o_rank, n + 3)
                p = step.did(dve.tensor_tensor(prod, one_cell[:, u].rearrange("p (g k) c -> p g (k c)", g=RG), psRank, ALU.mult))
                step.after(p)
                dve.sem_inc(o_prod, 1)
                a = step.did(dve.tensor_reduce(rank[:, u, :], prod.rearrange("p g (k c) -> p (g k) c", c=NT), AX, ALU.add))
                hold(dve, "dve", o_dve, a)
                d = step.did(dve.tensor_scalar(ondiag, q1[:, u, :, 0], tilec[:, 2, tile], None, ALU.is_equal))
                for m in range(3):
                    b = step.did(dve.tensor_scalar(over[:, m, :], rank[:, u, :], float(CELL * (m + 1)), None, ALU.is_ge))
                step.after(b)
                a = step.did(dve.scalar_tensor_tensor(out=step3[:, 2, :], in0=over[:, 0, :], scalar=-float(CELL), in1=rank[:, u, :],
                                                      op0=ALU.mult, op1=ALU.add))
                b = step.did(dve.tensor_tensor(step3[:, 0:2, :], over[:, 0:2, :], over[:, 1:3, :], ALU.subtract))
                c = step.did(dve.tensor_scalar(keep[:, 0, :], over[:, 0, :], -1.0, 1.0, ALU.mult, ALU.add))
                step.after(b)
                b = step.did(dve.tensor_tensor(keep[:, 1:3, :], step3[:, 0:2, :],
                                               ondiag.rearrange("p (o t) -> p o t", o=1).to_broadcast([128, 2, COLS]), ALU.mult))
                a = step.did(dve.scalar_tensor_tensor(out=slot[:, u], in0=twice(over[:, 1, :]), scalar=-float(CELL), in1=twice(step3[:, 2, :]),
                                                      op0=ALU.mult, op1=ALU.add))
                step.after(b)
                for m in range(2):
                    b = step.did(dve.tensor_tensor(pay[:, u, m], keep, off1[:, u, m:m + 1, :].to_broadcast([128, 3, COLS]), ALU.mult))
                a = step.did(dve.tensor_tensor(pay2[:, u], twice(keep[:, 0, :]), twice(off1[:, u, 0, :]), ALU.mult))
                step.after(b)
                dve.sem_inc(o_pay, 1)
                dve.wait_ge(o_perm, n + 2)
                dve.tensor_tensor(pairs(one_slot), columns(col0, CELL, COLS), along(slot[:, u], CELL), ALU.is_equal).then_inc(o_slot, 1)
                step.after(a)
                dve.tensor_tensor(pairs(payload[:, u, :, 0, 0:NT]), pairs(one_cell[:, u]), along(pay2[:, u], NT), ALU.mult
                                  ).then_inc(o_mulv, 1)

            find_cells(0, 0, 32, slice(0, 1))
            with dve.Fori(0, NT // 2) as i:
                step.enter(i, 2 * (10 + 14))
                for u in range(2):
                    find_cells(i * 2 + (u + 1), 1 - u, i * 32 + (32 if u == 0 else 64), bass.ds(i * 2 + (u + 1), 1))
                    find_slots(i * 2 + u, u, bass.ds(i * 2 + u, 1))
                step.leave(NT // 2)
            dve.wait_ge(o_S, NT + 2)
            step.did(dve.tensor_scalar(filled, slots[:, 1, 0:NT], 0.0, None, ALU.is_gt))
            step.last()
            dve.tensor_reduce(placed[:], filled.rearrange("p t c -> p (t c)"), AX, ALU.add).then_inc(o_fill, 1)
            dve.wait_ge(o_sum, 1)
            step.did(dve.tensor_scalar(missing[:, 0:1], psCount[0:1, 64:65], -1.0, float(E), ALU.mult, ALU.add))
            step.last()
            dve.tensor_scalar(missingi[:], missing[:, 0:1], 0.0, None, ALU.is_gt).then_inc(o_flag, 1)

        def group_done(i, k, pos):
            return i * BODY + (BODY + k * (NT // 2) * BODY + pos + 1)

        def before_it(i, k, pos, buffers):
            if pos >= buffers:
                return group_done(i, k, pos - buffers)
            return group_done(i, k, max(q for q in range(BODY) if q % buffers == pos) - BODY)

        def cells_sp(sp, k):
            sp.wait_ge(s_tE, STAGE0[EDGE[k]] + NT)
            for u in range(2):
                sp.wait_ge(o_store[u], 16 + 16 * (NT // 2))
            with sp.Fori(0, NT // 2) as i:
                for u in range(2):
                    sp.wait_ge(f_gat, group_done(i, k, (u - 1) * GROUPS - 1))
                    sp.dma_start(cur[:, u], TAB[:, :, bass.ds(i * 2 + u, 1)].rearrange("p n o c d -> p n (o c d)")).then_inc(f_cur[u], 16)
                    for c, (g0, n) in enumerate(CHUNKS):
                        g1, n1 = CHUNKS[c - 2]
                        pos = u * GROUPS + g1 + n1 - 1 - (GROUPS if c < 2 else 0)
                        sp.wait_ge(f_toN, group_done(i, k, pos))
                        for a in range(2):
                            sp.dma_start(slist[c % 2][:, a, 0:n * GROUP * CELL],
                                         slots_dram[bass.ds(i * 2 + u, 1), a, g0 * GROUP:(g0 + n) * GROUP, :]
                                         .rearrange("o c e -> o (c e)").to_broadcast([P, n * GROUP * CELL])
                                         ).then_inc(f_list[c % 2], 16)

        def cells_pool(pool, k):
            hold(pool, "pool", s_tE, STAGE0[EDGE[k]] + NT)
            pool.memset(mparts[:, :, 0, :, D:W], 1.0).then_inc(f_one, 1)
            hold(pool, "pool", f_one, k + 1)

            def own_slots(tile, u):
                pool.tensor_copy(curS[:, u], slots[:, 1, tile, :].rearrange("p o c -> p c o").to_broadcast([128, CELLS, 2])
                                 ).then_inc(f_own, 1)

            own_slots(slice(0, 1), 0)
            with pool.Fori(0, NT // 2) as i:
                hold(pool, "pool", f_toE, group_done(i, k, -1))
                own_slots(bass.ds(i * 2 + 1, 1), 1)
                for pos in range(BODY):
                    hold(pool, "pool", f_mid, group_done(i, k, pos))
                    pool.tensor_tensor(mparts[:, pos % 4, 2, :, 0:D], mrest[:, pos % 2], mparts[:, pos % 4, 1, :, 0:D], ALU.subtract
                                       ).then_inc(f_lo, 1)
                    if pos == GROUPS + 3:
                        hold(pool, "pool", f_toE, group_done(i, k, GROUPS - 1))
                        own_slots(bass.ds(i * 2 + 2, 1), 0)

        def cells_pe(pe, k):
            def gather(i, pos):
                u, g = divmod(pos, GROUPS)
                if g == 0:
                    pe.wait_ge(f_cur[u], i * 16 + (k * (NT // 2) + 1) * 16)
                pe.wait_ge(f_toN, group_done(i, k, pos))
                pe.wait_ge(f_rest, before_it(i, k, pos, BANKS))
                for c in range(GROUP):
                    t = g * GROUP + c
                    to = psMsg[pos % BANKS][:, c * D:(c + 1) * D]
                    for p in range(PARTS):
                        row = TAB[:, 0, t, p, :] if t < NT else cur[:, u, 0, p * D:(p + 1) * D]
                        pe.matmul(to, toN[:, pos % 4, 0, c * CELL:(c + 1) * CELL], row, start=p == 0, stop=False)
                    for p in range(PARTS):
                        m = pe.matmul(to, toN[:, pos % 4, 1, c * CELL:(c + 1) * CELL], cur[:, u, 1, p * D:(p + 1) * D],
                                      start=False, stop=p == PARTS - 1)
                m.then_inc(f_gat, 1)

            def scatter(i, pos):
                u, g = divmod(pos, GROUPS)
                pe.wait_ge(f_toE, group_done(i, k, pos))
                pe.wait_ge(f_lo, group_done(i, k, pos))
                if g == 0:
                    pe.wait_ge(f_agg, i * 2 + (k * NT + u + 1))
                for c in range(GROUP):
                    for p in range(PARTS):
                        w = W if p == 0 else D
                        m = pe.matmul(psA[u][0:P, 0:w], toE[:, pos % 4, c, 0:P], mparts[:, pos % 4, p, c, 0:w],
                                      start=g == 0 and c == 0 and p == 0, stop=g == GROUPS - 1 and c == GROUP - 1 and p == PARTS - 1,
                                      skip_group_check=True)
                m.then_inc(f_sca, 1)

            with pe.Fori(0, NT // 2) as i:
                for pos in range(BODY):
                    gather(i, pos)
                    if pos >= 2:
                        scatter(i, pos - 2)
                for pos in range(BODY - 2, BODY):
                    scatter(i, pos)

        def cells_act(act, k):
            with act.Fori(0, NT // 2) as i:
                def high(pos):
                    act.wait_ge(f_gat, group_done(i, k, pos))
                    act.wait_ge(f_sca, before_it(i, k, pos, 4))
                    act.activation(mparts[:, pos % 4, 0, :, 0:D], psMsg[pos % BANKS].rearrange("p (c d) -> p c d", d=D), ACT.Relu
                                   ).then_inc(f_hi, 1)

                def middle(pos):
                    act.wait_ge(f_rest, group_done(i, k, pos))
                    act.copy(mparts[:, pos % 4, 1, :, 0:D], mrest[:, pos % 2]).then_inc(f_mid, 1)

                def sums(u):
                    hold(act, "act", f_sca, group_done(i, k, (u + 1) * GROUPS - 1))
                    act.copy(AGG[:, bass.ds(i * 2 + u, 1), :], psA[u][0:P, 0:W].rearrange("p (o d) -> p o d", o=1)).then_inc(f_agg, 1)

                for pos in range(BODY):
                    if pos:
                        middle(pos - 1)
                    high(pos)
                    if pos == GROUPS + 3:
                        sums(0)
                middle(BODY - 1)
                sums(1)

        def cells_dve(dve, k):
            with dve.Fori(0, NT // 2) as i:
                def by_node(pos):
                    u, g = divmod(pos, GROUPS)
                    c = max(n for n, (g0, _) in enumerate(CHUNKS) if g0 <= g)
                    at = (g - CHUNKS[c][0]) * GROUP * CELL
                    per = len(CHUNKS) // 2
                    n = u * per + c // 2
                    dve.wait_ge(f_list[c % 2], i * (2 * per * 32) + (k * NT * per * 32 + 32 * (n + 1)))
                    dve.wait_ge(f_gat, before_it(i, k, pos, 4))
                    dve.tensor_scalar(toN[:, pos % 4], slist[c % 2][:, :, at:at + GROUP * CELL], row1[0:P, :], None, ALU.is_equal
                                      ).then_inc(f_toN, 1)

                def by_slot(pos):
                    u, g = divmod(pos, GROUPS)
                    if g == 0:
                        dve.wait_ge(f_own, i * 2 + (k * (NT + 1) + u + 1))
                    dve.wait_ge(f_sca, before_it(i, k, pos, 4))
                    dve.tensor_tensor(pairs(toE[:, pos % 4]), columns(col1, 126, GROUP),
                                      along(curS[:, u, g * GROUP:(g + 1) * GROUP], 126), ALU.is_equal).then_inc(f_toE, 1)

                def rest_of(pos):
                    dve.wait_ge(f_hi, group_done(i, k, pos))
                    dve.wait_ge(f_lo, before_it(i, k, pos, 2))
                    dve.scalar_tensor_tensor(out=mrest[:, pos % 2], in0=psMsg[pos % BANKS].rearrange("p (c d) -> p c d", d=D), scalar=0.0,
                                             in1=mparts[:, pos % 4, 0, :, 0:D], op0=ALU.max, op1=ALU.subtract).then_inc(f_rest, 1)

                for pos in range(3):
                    by_node(pos)
                by_slot(0)
                for pos in range(BODY):
                    rest_of(pos)
                    if pos + 3 < BODY:
                        by_node(pos + 3)
                    if pos + 1 < BODY:
                        by_slot(pos + 1)
            dve.wait_ge(f_agg, 2 + NT * (k + 1))
            dve.sem_inc(s_agg, 1)

        def linear_sp(sp, l):
            sp.wait_ge(s_tab, l + 1)
            with sp.Fori(0, NT // 2) as i:
                for u in range(2):
                    sp.wait_ge(l_sum, group_done(i, l, (u - 1) * GROUPS - 1))
                    sp.dma_start(cur2[:, u], TAB[:, 0, bass.ds(i * 2 + u, 1)].rearrange("p o c d -> p (o c d)")).then_inc(l_cur[u], 16)

        def linear_pool(pool, l):
            hold(pool, "pool", s_tab, l + 1)

            def own_slots(tile, u):
                for a in range(2):
                    o = pool.tensor_copy(curS2[:, u, :, a, :], slots[:, a, tile, :].rearrange("p o c -> p c o").to_broadcast([128, CELLS, 2]))
                o.then_inc(l_own, 1)

            own_slots(slice(0, 1), 0)
            with pool.Fori(0, NT // 2) as i:
                hold(pool, "pool", l_from, group_done(i, l, -1))
                own_slots(bass.ds(i * 2 + 1, 1), 1)
                hold(pool, "pool", l_from, group_done(i, l, GROUPS - 1))
                own_slots(bass.ds(i * 2 + 2, 1), 0)

        def linear_pe(pe, l):
            def count(i, pos):
                pe.wait_ge(l_from, group_done(i, l, pos))
                pe.wait_ge(l_Cc, before_it(i, l, pos, BANKS))
                for c in range(GROUP):
                    m = pe.matmul(psMsg[pos % BANKS][0:P, c * P:(c + 1) * P], oneE[:, pos % 4, c, 0, 0:P], oneE[:, pos % 4, c, 1, 0:P],
                                  start=True, stop=True, skip_group_check=True)
                m.then_inc(l_C, 1)

            def total(i, pos):
                u, g = divmod(pos, GROUPS)
                pe.wait_ge(l_Cc, group_done(i, l, pos))
                if g == 0:
                    pe.wait_ge(l_cur[u], i * 16 + (l * (NT // 2) + 1) * 16)
                    pe.wait_ge(l_agg, i * 2 + (l * NT + u + 1))
                for c in range(GROUP):
                    t = g * GROUP + c
                    for p in range(PARTS):
                        row = TAB[:, 0, t, p, :] if t < NT else cur2[:, u, p * D:(p + 1) * D]
                        m = pe.matmul(psA[u][0:P, 0:D], cells[:, pos % 4, c, 0:P], row, start=g == 0 and c == 0 and p == 0,
                                      stop=g == GROUPS - 1 and c == GROUP - 1 and p == PARTS - 1)
                m.then_inc(l_sum, 1)

            with pe.Fori(0, NT // 2) as i:
                for pos in range(BODY):
                    count(i, pos)
                    if pos >= 2:
                        total(i, pos - 2)
                for pos in range(BODY - 2, BODY):
                    total(i, pos)

        def linear_act(act, l):
            with act.Fori(0, NT // 2) as i:
                def sums(u):
                    hold(act, "act", l_sum, group_done(i, l, (u + 1) * GROUPS - 1))
                    act.copy(AGG[:, bass.ds(i * 2 + u, 1), 0:D], psA[u][0:P, 0:D].rearrange("p (o d) -> p o d", o=1)).then_inc(l_agg, 1)

                for pos in range(BODY):
                    act.wait_ge(l_C, group_done(i, l, pos))
                    act.wait_ge(l_sum, before_it(i, l, pos, 4))
                    act.copy(cells[:, pos % 4, :, 0:P], psMsg[pos % BANKS][0:P, 0:GROUP * P].rearrange("p (c d) -> p c d", d=P)
                             ).then_inc(l_Cc, 1)
                    if pos == GROUPS + 3:
                        sums(0)
                sums(1)

        def counts_dve(dve, l):
            with dve.Fori(0, NT // 2) as i:
                for pos in range(BODY):
                    u, g = divmod(pos, GROUPS)
                    if g == 0:
                        dve.wait_ge(l_own, i * 2 + (l * (NT + 1) + u + 1))
                    dve.wait_ge(l_C, before_it(i, l, pos, 4))
                    dve.tensor_tensor(pairs(oneE[:, pos % 4].rearrange("p c a n -> p (c a) n")), columns(col1, 126, 2 * GROUP),
                                      along(curS2[:, u, g * GROUP:(g + 1) * GROUP].rearrange("p c a e -> p (c a) e"), 126),
                                      ALU.is_equal).then_inc(l_from, 1)
            dve.wait_ge(l_agg, 2 + NT * (l + 1))
            dve.sem_inc(s_agg, 1)

        def general_sp(sp, k):
            if k < L0:
                sp.wait_ge(s_tE, STAGE0[EDGE[k]] + NT)
            else:
                sp.wait_ge(s_tab, k - L0 + 1)
            sp.dma_start(srci, src.rearrange("(p t) -> p t", p=P)).then_inc(s_e, 16)
            sp.dma_start(dsti, dst.rearrange("(p t) -> p t", p=P)).then_inc(s_e, 16)
            sp.wait_ge(s_const, 1)
            if k:
                sp.wait_ge(g_back, 32 * k)
            for u in range(2):
                sp.dma_start(sums_dram[u][0:N, :].rearrange("(t p) d -> p t d", p=P),
                             zrow[:].rearrange("p (o d) -> p o d", o=1).to_broadcast([P, NT, W])
                             ).then_inc(g_zero, 16)
            tables = 2 if k < L0 else 1
            for n in range(tables):
                sp.dma_start(table_dram[n].rearrange("(t p) d -> p t d", p=P),
                             TAB[:, n].rearrange("p t c d -> p t (c d)")).then_inc(g_tab, 16)
            for u in range(2):
                sp.wait_ge(g_add[k][u], 16 * PAIRS + 16)
            for u, to in enumerate((AGG, AGG1)):
                sp.dma_start(to, sums_dram[u][0:N, :].rearrange("(t p) d -> p t d", p=P)).then_inc(g_back, 16)

        def stage_pool(pool, name, ready, value):
            base = STAGE0[name]
            hold(pool, "pool", ready, value)
            with pool.Fori(0, NT // 2) as i:
                for u in range(2):
                    hold(pool, "pool", s_tT, i * 2 + (base + u - 1))
                    copies = [pool.tensor_copy(tile_in[:, u, 0, :], H[:, bass.ds(i * 2 + u, 1), :])]
                    if name in AGG_STAGES:
                        copies.append(pool.tensor_copy(tile_in[:, u, 1, :], AGG[:, bass.ds(i * 2 + u, 1), 0:D]))
                    copies[-1].then_inc(s_in, 1)

        def general_pool(pool, k):
            hold(pool, "pool", s_e, 32 * (k + 1))
            hold(pool, "pool", g_tab, 16 * (2 * min(k + 1, L0) + max(k + 1 - L0, 0)))
            hold(pool, "pool", g_zero, 32 * (k + 1))
            for u in range(2):
                pool.dma_start(sums_dram[u][N:N + P, :], zrow[:]).then_inc(g_add[k][u], 16)
            tables = 2 if k < L0 else 1
            done = 2 * PAIRS * k + 2
            with pool.Fori(0, PAIRS) as i:
                hold(pool, "pool", g_msg, i * 2 + done)
                hold(pool, "pool", g_widx, i * 2 + done)
                for u in range(2):
                    pool.tensor_copy(sidx[:, u:u + 1], srci[:, bass.ds(i * 2 + u, 1)])
                    pool.tensor_copy(didx[:, u:u + 1], dsti[:, bass.ds(i * 2 + u, 1)]).then_inc(g_idx, 1)
                hold(pool, "pool", g_idx, i * 2 + done)
                for u in range(2):
                    for n in range(tables):
                        pool.indirect_dma_start(rows[:, u, n].rearrange("p c d -> p (c d)"), None, table_dram[n],
                                                bass.IndirectOffsetOnAxis(ap=(sidx, didx)[n][:, u:u + 1], axis=0)
                                                ).then_inc(g_rows[k][u], 16)
                for u in range(2):
                    hold(pool, "pool", g_cp, i * 2 + (u + 1 + done))
                    hold(pool, "pool", g_add[k][u], i * 16 + 16)
                    pool.indirect_dma_start(sums_dram[u], bass.IndirectOffsetOnAxis(ap=widx[:, u:u + 1], axis=0),
                                            msum[:, u, :], None, compute_op=ALU.add).then_inc(g_add[k][u], 16)

        def stage_pe(pe, name, products):
            base = STAGE0[name]
            with pe.Fori(0, NT // 2) as i:
                for u in range(2):
                    pe.wait_ge(s_in, i * 2 + (base + u + 1))
                    pe.wait_ge(s_tC, i * 2 + (base + u - 1))
                    t = pe.transpose(psT[u][:, 0:P], tile_in[:, u, 0, :], ident[0:P, 0:P])
                    if name in AGG_STAGES:
                        t = pe.transpose(psT[u][:, 128:128 + P], tile_in[:, u, 1, :], ident[0:P, 0:P])
                    t.then_inc(s_tT, 1)
                for u in range(2):
                    pe.wait_ge(s_tC, i * 2 + (base + u + 1))
                    pe.wait_ge(s_tE, i * 2 + (base + u - 1))
                    for n, (which, rhs, at, stop) in enumerate(products):
                        start = n == 0 or products[n - 1][3]
                        m = pe.matmul(psO[u][0:P, at:at + rhs.shape[1]], hT[:, u, which, 0:P], rhs, start=start, stop=stop)
                    m.then_inc(s_tO, 1)

        def general_pe(pe, k):
            done = 2 * PAIRS * k + 2
            with pe.Fori(0, PAIRS) as i:
                for u in range(2):
                    pe.wait_ge(g_drep, i * 2 + (u - 1 + done))
                    pe.wait_ge(g_same, i * 2 + done)
                    pe.transpose(psD[u][0:P, 0:P], drep[:, u, :], ident[0:P, 0:P]).then_inc(g_dT, 1)
                for u in range(2):
                    pe.wait_ge(g_same, i * 2 + (u + 1 + done))
                    pe.wait_ge(g_msg, i * 2 + (u + 1 + done))
                    pe.wait_ge(g_cp, i * 2 + done)
                    pe.matmul(psM[u][0:P, 0:W], same[:, u, :], msg[:, u, :], start=True, stop=True).then_inc(g_sum, 1)

        def norm_act(act, n):
            act.wait_ge(s_var, n + 1)
            act.activation(std[:], var[:], ACT.Sqrt, bias=eps[:]).then_inc(s_std, 1)

        def stage_act(act, name, split=None):
            base = STAGE0[name]
            with act.Fori(0, NT // 2) as i:
                for u in range(2):
                    act.wait_ge(s_tT, i * 2 + (base + u + 1))
                    act.wait_ge(s_tO, i * 2 + (base + u - 1))
                    n = 2 if name in AGG_STAGES else 1
                    act.copy(hT[:, u, 0:n, 0:P], psT[u][:, 0:n * 128].rearrange("k (n p) -> k n p", n=n)[:, :, 0:P]
                             ).then_inc(s_tC, 1)
                if split is not None:
                    for u in range(2):
                        hold(act, "act", s_raw, i * 2 + (u + 1 + split * NT))
                        act.copy(TAB[:, :, bass.ds(i * 2 + u, 1), 0, :], raw[:, u].rearrange("p n (o d) -> p n o d", o=1)).then_inc(s_hi, 1)
                    for u in range(2):
                        hold(act, "act", s_rest, i * 2 + (u + 1 + split * NT))
                        act.copy(TAB[:, :, bass.ds(i * 2 + u, 1), 1, :], rest[:, u].rearrange("p n (o d) -> p n o d", o=1)).then_inc(s_mid, 1)

        def general_act(act, k):
            done = 2 * PAIRS * k + 2
            with act.Fori(0, PAIRS) as i:
                for u in range(2):
                    act.wait_ge(g_sum, i * 2 + (u + 1 + done))
                    act.wait_ge(g_add[k][u], i * 16 + 16)
                    act.copy(msum[:, u, :], psM[u][0:P, 0:W]).then_inc(g_cp, 1)

        def norm_dve(dve, step, n, source, l=None):
            even, odd = stats[:, :, 0:3], stats[:, :, 3:6]
            step.last()
            a = step.did(dve.tensor_tensor(mean[:], even[:, :, 1], odd[:, :, 1], ALU.add))
            b = step.did(dve.tensor_tensor(sq[:], even[:, :, 1], odd[:, :, 1], ALU.subtract))
            c = step.did(dve.tensor_tensor(var[:], even[:, :, 2], odd[:, :, 2], ALU.add))
            step.after(c)
            d = step.did(dve.tensor_scalar(mean[:], mean[:], 0.5, None, ALU.mult))
            e = step.did(dve.tensor_tensor(sq[:], sq[:], sq[:], ALU.mult))
            f = step.did(dve.tensor_scalar(var[:], var[:], 1.0 / D, None, ALU.mult))
            step.after(f)
            dve.scalar_tensor_tensor(out=var[:], in0=sq[:], scalar=0.25, in1=var[:], op0=ALU.mult, op1=ALU.add
                                     ).then_inc(s_var, 1)
            per_tile = [P, NT, D]
            step.did(dve.tensor_tensor(H, source, mean[:].rearrange("p (t o) -> p t o", o=1).to_broadcast(per_tile), ALU.subtract))
            dve.wait_ge(s_std, n + 1)
            step.did(dve.reciprocal(rstd[:], std[:]))
            step.last()
            step.did(dve.tensor_tensor(H, H, rstd[:].rearrange("p (t o) -> p t o", o=1).to_broadcast(per_tile), ALU.mult))
            if l is not None:
                step.last()
                step.did(dve.tensor_tensor(H, H, bias[:, LN_G + l:LN_G + l + 1, :].to_broadcast(per_tile), ALU.mult))
                step.last()
                dve.tensor_tensor(H, H, bias[:, LN_B + l:LN_B + l + 1, :].to_broadcast(per_tile), ALU.add).then_inc(s_h, 1)

        def split_dve(dve, l):
            base, done = STAGE0[f"ab{l}"], l * NT
            with dve.Fori(0, NT // 2) as i:
                for u in range(2):
                    dve.wait_ge(s_tO, i * 2 + (base + u + 1))
                    dve.tensor_tensor(raw[:, u], psO[u][0:P, 0:2 * D].rearrange("p (n d) -> p n d", n=2), abias[:, l], ALU.add
                                      ).then_inc(s_raw, 1)
                for u in range(2):
                    hold(dve, "dve", s_hi, i * 2 + (done + u + 1))
                    dve.tensor_tensor(rest[:, u].rearrange("p n (o d) -> p n o d", o=1), raw[:, u].rearrange("p n (o d) -> p n o d", o=1),
                                      TAB[:, :, bass.ds(i * 2 + u, 1), 0, :], ALU.subtract).then_inc(s_rest, 1)
                for u in range(2):
                    hold(dve, "dve", s_rest, i * 2 + (done + u + 1))
                    hold(dve, "dve", s_mid, i * 2 + (done + u + 1))
                    dve.tensor_tensor(TAB[:, :, bass.ds(i * 2 + u, 1), 2, :], rest[:, u].rearrange("p n (o d) -> p n o d", o=1),
                                      TAB[:, :, bass.ds(i * 2 + u, 1), 1, :], ALU.subtract).then_inc(s_tE, 1)

        def update_dve(dve, step, l):
            base = STAGE0[f"upd{l}"]
            with dve.Fori(0, NT // 2) as i:
                step.enter(i, 8)
                now = [0, 0]
                tile = [H[:, bass.ds(i * 2 + u, 1), :] for u in range(2)]
                for u in range(2):
                    hold(dve, "dve", s_tO, i * 2 + (base + u + 1))
                    now[u] = step.did(dve.scalar_tensor_tensor(
                        out=tmp[:, u, 0, :], in0=b2upd[:, l, :], scalar=degc[:, bass.ds(i * 2 + u, 1)],
                        in1=psO[u][0:P, 0:D], op0=ALU.mult, op1=ALU.add))
                for u in range(2):
                    dve.wait_ge(s_dve, now[u])
                    now[u] = step.did(dve.tensor_tensor(tmp[:, u, 1, :], tmp[:, u, 0, :], bias[:, B_UPD + l, :], ALU.add))
                for u in range(2):
                    hold(dve, "dve", s_dve, now[u])
                    now[u] = step.did(dve.tensor_tensor(tile[u], tmp[:, u, 1:2, :], tile[u], ALU.add))
                for u in range(2):
                    hold(dve, "dve", s_dve, now[u])
                    step.did(dve.bn_stats(stats[:, bass.ds(i * 2 + u, 1), :], tile[u]))
                    dve.sem_inc(s_tE, 1)
                step.leave(NT // 2)

        def linear_dve(dve, step, l):
            base = STAGE0[f"lin{l}"]
            with dve.Fori(0, NT // 2) as i:
                step.enter(i, 6 if l < L1 - 1 else 8)
                now = [0, 0]
                for u in range(2):
                    hold(dve, "dve", s_tO, i * 2 + (base + u + 1))
                    now[u] = step.did(dve.tensor_scalar(tmp[:, u, 0, :], psO[u][0:P, 0:D], invdeg[:, bass.ds(i * 2 + u, 1)], None, ALU.mult))
                for u in range(2):
                    dve.wait_ge(s_dve, now[u])
                    now[u] = step.did(dve.tensor_tensor(tmp[:, u, 1, :], tmp[:, u, 0, :], psO[u][0:P, D:2 * D], ALU.add))
                for u in range(2):
                    hold(dve, "dve", s_dve, now[u])
                    dve.sem_inc(s_tE, 1)
                    to = H[:, bass.ds(i * 2 + u, 1), :] if l < L1 - 1 else raw[:, u, 0:1, :]
                    now[u] = step.did(dve.tensor_tensor(to, tmp[:, u, 1:2, :], bias[:, B_LIN + l:B_LIN + l + 1, :], ALU.add))
                if l == L1 - 1:
                    for u in range(2):
                        hold(dve, "dve", s_dve, now[u])
                        tile = X[:, bass.ds(i * 2 + u, 1), :]
                        step.did(dve.tensor_tensor(tile, tile, raw[:, u, 0:1, :], ALU.add))
                step.leave(NT // 2)
            step.last()
            if l < L1 - 1:
                dve.tensor_scalar(H, H, 0.0, None, ALU.max).then_inc(s_h, 1)
            else:
                dve.sem_inc(s_fin, 1)

        def general_dve(dve, step, k):
            tables = 2 if k < L0 else 1
            done = 2 * PAIRS * k + 2
            with dve.Fori(0, PAIRS) as i:
                step.enter(i, 2 * (4 + (3 if k < L0 else 1)))
                now = [0, 0]
                for u in range(2):
                    dve.wait_ge(g_idx, i * 2 + (u - 1 + done))
                    dve.wait_ge(g_sum, i * 2 + done)
                    now[u] = step.did(dve.tensor_copy(dcol[:, u:u + 1], didx[:, u:u + 1]))
                for u in range(2):
                    dve.wait_ge(g_dve, now[u])
                    dve.tensor_scalar(drep[:, u, :], ones[0:P, 0:P], dcol[:, u:u + 1], None, ALU.mult).then_inc(g_drep, 1)
                for u in range(2):
                    dve.wait_ge(g_dT, i * 2 + (u - 1 + done))
                    dve.tensor_scalar(same[:, u, :], psD[u][0:P, 0:P], dcol[:, u:u + 1], None, ALU.is_equal).then_inc(g_same, 1)
                for u in range(2):
                    dve.wait_ge(g_same, i * 2 + (u + 1 + done))
                    now[u] = step.did(dve.tensor_tensor_reduce(earlier[:, u, :], same[:, u, :], before[:], 1.0, 0.0,
                                                               ALU.mult, ALU.add, nearl[:, u:u + 1]))
                for u in range(2):
                    dve.wait_ge(g_dve, now[u])
                    step.did(dve.tensor_scalar(wsel[:, u, 0:1], nearl[:, u:u + 1], 0.0, None, ALU.is_gt))
                    now[u] = step.did(dve.tensor_tensor(wsel[:, u, 1:2], junk[:], dcol[:, u:u + 1], ALU.subtract))
                for u in range(2):
                    dve.wait_ge(g_dve, now[u])
                    dve.wait_ge(g_add[k][u], i * 16 + 16)
                    dve.scalar_tensor_tensor(out=widx[:, u:u + 1], in0=wsel[:, u, 1:2], scalar=wsel[:, u, 0:1],
                                             in1=dcol[:, u:u + 1], op0=ALU.mult, op1=ALU.add).then_inc(g_widx, 1)
                for u in range(2):
                    dve.wait_ge(g_rows[k][u], i * (16 * tables) + 16 * tables)
                    r = rows[:, u, 0:tables]
                    now[u] = step.did(dve.tensor_tensor(part[:, u, 0:tables, :], r[:, :, 0, :], r[:, :, 1, :], ALU.add))
                for u in range(2):
                    dve.wait_ge(g_dve, now[u])
                    r = rows[:, u, 0:tables]
                    if k >= L0:
                        dve.tensor_tensor(msg[:, u, 0:D], part[:, u, 0, :], r[:, 0, 2, :], ALU.add).then_inc(g_msg, 1)
                    else:
                        now[u] = step.did(dve.tensor_tensor(part[:, u], part[:, u], r[:, :, 2, :], ALU.add))
                if k < L0:
                    for u in range(2):
                        dve.wait_ge(g_dve, now[u])
                        now[u] = step.did(dve.tensor_tensor(part[:, u, 0, :], part[:, u, 0, :], part[:, u, 1, :], ALU.add))
                    for u in range(2):
                        dve.wait_ge(g_dve, now[u])
                        dve.tensor_scalar(msg[:, u, 0:D], part[:, u, 0, :], 0.0, None, ALU.max).then_inc(g_msg, 1)
                step.leave(PAIRS)
            dve.wait_ge(g_back, 32 * (k + 1))
            dve.tensor_tensor(AGG[:], AGG, AGG1, ALU.add).then_inc(s_agg, 1)

        block = ctx.enter_context(nc.Block())

        @block.sync
        def _(sp):
            sp.dma_start(X, x.rearrange("(t p) d -> p t d", p=P)).then_inc(s_x, 16)
            loads = [(wnat[:, ENC, :], W_enc), (wnat[:, OUT, :], W_out)]
            for l in range(L0):
                loads += [(wnat[:, MSG + 2 * l, :], msg_W1[l, :, 0:D]),
                          (wnat[:, MSG + 2 * l + 1, :], msg_W1[l, :, D:2 * D]),
                          (wnat[:, UPD_H + l, :], upd_W[l, :, 0:D]),
                          (wnat[:, UPD_M + l, :], upd_W[l, :, D:2 * D]),
                          (wnat[:, NW + l, :], msg_W2[l]),
                          (b2col[:, l:l + 1], msg_b2[l].rearrange("(d o) -> d o", o=1))]
            for l in range(L1):
                loads += [(wnat[:, LIN_L + l, :], Wl[l]), (wnat[:, LIN_R + l, :], Wr[l])]
            rows_of = [b_enc] + [v[l] for v in (msg_b1, upd_b, ln_g, ln_b) for l in range(L0)] \
                + [b_out] + [bl[l] for l in range(L1)]
            for k, b in enumerate(rows_of):
                loads.append((bias[:, k, :], b.rearrange("(o d) -> o d", o=1).to_broadcast([P, D])))
            assert len(loads) == LOADS
            for to, fr in loads:
                sp.dma_start(to, fr).then_inc(s_w, 16)
            sort_sp(sp)
            miss = load_flag(sp)
            for k in range(L0):
                edge_sp(sp, k, miss)
            sp.wait_ge(s_agg, L0)
            sp.dma_start(X, x.rearrange("(t p) d -> p t d", p=P)).then_inc(s_x, 16)
            for k in range(L0, L0 + L1):
                edge_sp(sp, k, miss)
            sp.wait_ge(s_fin, 1)
            sp.dma_start(out.rearrange("(t p) d -> p t d", p=P), X).then_inc(s_out, 16)
            sp.wait_ge(s_out, 16)

        @block.gpsimd
        def _(pool):
            pool.memset(ones[:], 1.0).then_inc(s_pset, 1)
            pool.memset(ident[:], 0.0).then_inc(s_pset, 1)
            pool.memset(zrow[:], 0.0).then_inc(s_pset, 1)
            pool.memset(eps[:], EPS).then_inc(s_pset, 1)
            pool.memset(msg[:, :, D:W], 1.0).then_inc(s_pset, 1)
            pool.memset(abias[:], 0.0).then_inc(s_pset, 1)
            pool.iota(junki, pattern=[[0, 1]], base=N, channel_multiplier=1).then_inc(s_pset, 1)
            pool.iota(counti, pattern=[[1, 128]], base=0, channel_multiplier=0).then_inc(s_pset, 1)
            pool.iota(rowi, pattern=[[0, 1]], base=1, channel_multiplier=1).then_inc(s_pset, 1)
            pool.iota(tilei[:, 0, :], pattern=[[P, NT + 2]], base=0, channel_multiplier=0).then_inc(s_pset, 1)
            pool.iota(tilei[:, 1, :], pattern=[[P, NT + 2]], base=-1, channel_multiplier=0).then_inc(s_pset, 1)
            pool.iota(tilei[:, 2, :], pattern=[[1, NT + 2]], base=1, channel_multiplier=0).then_inc(s_pset, 1)
            pool.memset(ones_bf[:], 1.0).then_inc(s_pset, 1)
            pool.wait_ge(s_pset, 13)
            pool.tensor_copy(col0[:], counti).then_inc(s_pset, 1)
            pool.tensor_scalar(col1[:], counti, 1.0, None, ALU.add).then_inc(s_pset, 1)
            pool.tensor_copy(row1[:], rowi).then_inc(s_pset, 1)
            pool.tensor_copy(tilec[:], tilei).then_inc(s_pset, 1)
            pool.affine_select(out=below_bf[:], in_=ones_bf[:], compare_op=ALU.is_gt, fill=0.0, base=0,
                               pattern=[[1, 128]], channel_multiplier=-1).then_inc(s_pset, 1)
            pool.tensor_copy(junk[:], junki).then_inc(s_pset, 1)
            pool.affine_select(out=ident[:], in_=ident[:], compare_op=ALU.not_equal, fill=1.0, base=0,
                               pattern=[[-1, 128]], channel_multiplier=1).then_inc(s_pset, 1)
            pool.affine_select(out=before[:], in_=ones[0:P, 0:P], compare_op=ALU.is_gt, fill=0.0, base=0,
                               pattern=[[-1, P]], channel_multiplier=1).then_inc(s_pset, 1)
            pool.wait_ge(s_pset, 21)
            pool.tensor_copy(ident_bf[:], ident[:]).then_inc(s_pset, 1)
            pool.wait_ge(s_pset, 22)
            pool.sem_inc(s_const, 1)
            for empty in (s_in, s_tT, s_tC, s_tO, s_tE, g_msg, g_widx, g_same, g_cp, g_sum,
                          o_read, o_tot, o_totc, o_rank, o_prod, o_pay, o_mul, o_mulv, o_slot, o_perm, o_S, o_turn, o_ST, o_cell, f_agg, l_agg):
                pool.sem_inc(empty, 2)
            for empty in (f_toN, f_toE, f_gat, f_hi, f_rest, f_mid, f_lo, f_sca, l_from, l_C, l_Cc, l_sum):
                pool.sem_inc(empty, BODY)
            for stored in o_store:
                pool.sem_inc(stored, 16)
            pool.memset(slots[:, :, NT, :], 0.0)
            sort_pool(pool)
            miss = load_flag(pool)
            stage_pool(pool, "enc", s_h, 1)
            for l in range(L0):
                if l == 0:
                    stage_pool(pool, "ab0", s_tE, STAGE0["enc"] + NT)
                else:
                    stage_pool(pool, f"ab{l}", s_h, l + 1)
                edge_pool(pool, l, miss)
                stage_pool(pool, f"upd{l}", s_agg, l + 1)
            stage_pool(pool, "out", s_h, L0 + 1)
            for l in range(L1):
                edge_pool(pool, L0 + l, miss)
                stage_pool(pool, f"lin{l}", s_agg, L0 + l + 1)

        @block.tensor
        def _(pe):
            pe.wait_ge(s_w, 16 * LOADS)
            pe.wait_ge(s_const, 1)
            for w in range(NW):
                if w >= 2:
                    pe.wait_ge(s_wTc, w - 1)
                pe.transpose(psT[w % 2][:, 0:D], wnat[:, w, :], ident[:]).then_inc(s_wT, 1)
            pe.wait_ge(s_wTc, NW)
            pe.wait_ge(s_b2, L0)
            for l in range(L0):
                pe.matmul(psO[l][:, 0:D], wnat[:, NW + l, :], wT[:, UPD_M + l, :], start=True, stop=True)
                pe.matmul(psO[l][0:P, D:2 * D], b2rep[:, l, :], wT[:, UPD_M + l, :], start=True, stop=True
                          ).then_inc(s_comp, 1)
            pe.wait_ge(s_compc, 2 * L0)
            sort_pe(pe)
            miss = load_flag(pe)
            stage_pe(pe, "enc", [(0, wT[:, ENC, :], 0, True)])
            for l in range(L0):
                stage_pe(pe, f"ab{l}", [(0, wT[:, MSG + 2 * l:MSG + 2 * l + 2, :].rearrange("k w d -> k (w d)"), 0, True)])
                edge_pe(pe, l, miss)
                stage_pe(pe, f"upd{l}", [(0, wT[:, UPD_H + l, :], 0, False), (1, wM[:, l, :], 0, True)])
            stage_pe(pe, "out", [(0, wT[:, OUT, :], 0, True)])
            for l in range(L1):
                edge_pe(pe, L0 + l, miss)
                stage_pe(pe, f"lin{l}", [(0, wT[:, LIN_R + l, :], D, True), (1, wT[:, LIN_L + l, :], 0, True)])

        @block.scalar
        def _(act):
            for w in range(NW):
                act.wait_ge(s_wT, w + 1)
                act.copy(wT[:, w, :], psT[w % 2][:, 0:D]).then_inc(s_wTc, 1)
            for l in range(L0):
                act.wait_ge(s_comp, l + 1)
                act.copy(wM[:, l, :], psO[l][:, 0:D]).then_inc(s_compc, 1)
                act.copy(b2upd[:, l, :], psO[l][0:P, D:2 * D]).then_inc(s_compc, 1)
            sort_act(act)
            miss = load_flag(act)
            norm_act(act, 0)
            stage_act(act, "enc")
            for l in range(L0):
                stage_act(act, f"ab{l}", split=l)
                edge_act(act, l, miss)
                stage_act(act, f"upd{l}")
                norm_act(act, l + 1)
            stage_act(act, "out")
            norm_act(act, L0 + 1)
            for l in range(L1):
                act.wait_ge(s_h, L0 + 2 + l)
                act.copy(TAB[:, 0, :, 0, :], H).then_inc(s_hi, 1)
                act.wait_ge(s_rest, 2 * NT + l + 1)
                act.copy(TAB[:, 0, :, 1, :], AGG[:, :, 0:D]).then_inc(s_mid, 1)
                edge_act(act, L0 + l, miss)
                stage_act(act, f"lin{l}")

        @block.vector
        def _(dve):
            step = Steps(dve, s_dve)
            gstep = Steps(dve, g_dve)
            dve.wait_ge(s_const, 1)
            dve.wait_ge(s_w, 16 * LOADS)
            for l in range(L0):
                dve.tensor_scalar(b2rep[:, l, :], ones[:, 0:P], b2col[:, l:l + 1], None, ALU.mult).then_inc(s_b2, 1)
                step.did(dve.tensor_copy(abias[:, l, 1, :], bias[:, B_1 + l, :]))
            sort_dve(dve)
            miss = load_flag(dve)
            dve.wait_ge(s_x, 16)
            with dve.Fori(0, NT // 2) as i:
                step.enter(i, 2)
                for u in range(2):
                    step.did(dve.bn_stats(stats[:, bass.ds(i * 2 + u, 1), :], X[:, bass.ds(i * 2 + u, 1), :]))
                step.leave(NT // 2)
            norm_dve(dve, step, 0, X)
            step.last()
            dve.tensor_scalar(H, H, 0.0, None, ALU.max).then_inc(s_h, 1)
            with dve.Fori(0, NT // 2) as i:
                for u in range(2):
                    hold(dve, "dve", s_tO, i * 2 + (STAGE0["enc"] + u + 1))
                    dve.tensor_tensor(H[:, bass.ds(i * 2 + u, 1), :], psO[u][0:P, 0:D].rearrange("p (o d) -> p o d", o=1),
                                      bias[:, B_ENC:B_ENC + 1, :], ALU.add).then_inc(s_tE, 1)
            for l in range(L0):
                split_dve(dve, l)
                edge_dve(dve, gstep, l, miss)
                if l == 0:
                    dve.wait_ge(s_agg, 1)
                    step.did(dve.tensor_copy(degc[:], AGG[:, :, D]))
                    step.last()
                    step.did(dve.tensor_scalar(sq[:], degc[:], 1.0, None, ALU.max))
                    step.last()
                    step.did(dve.reciprocal(invdeg[:], sq[:]))
                update_dve(dve, step, l)
                norm_dve(dve, step, l + 1, H, l)
            dve.wait_ge(s_x, 32)
            with dve.Fori(0, NT // 2) as i:
                step.enter(i, 6)
                now = [0, 0]
                tile = [X[:, bass.ds(i * 2 + u, 1), :] for u in range(2)]
                for u in range(2):
                    hold(dve, "dve", s_tO, i * 2 + (STAGE0["out"] + u + 1))
                    now[u] = step.did(dve.tensor_tensor(tmp[:, u, 0, :], psO[u][0:P, 0:D], bias[:, B_OUT, :], ALU.add))
                for u in range(2):
                    hold(dve, "dve", s_dve, now[u])
                    now[u] = step.did(dve.tensor_tensor(tile[u], tmp[:, u, 0:1, :], tile[u], ALU.add))
                for u in range(2):
                    hold(dve, "dve", s_dve, now[u])
                    step.did(dve.bn_stats(stats[:, bass.ds(i * 2 + u, 1), :], tile[u]))
                    dve.sem_inc(s_tE, 1)
                step.leave(NT // 2)
            norm_dve(dve, step, L0 + 1, X)
            step.last()
            dve.tensor_scalar(H, H, 0.0, None, ALU.max).then_inc(s_h, 1)
            for l in range(L1):
                dve.wait_ge(s_h, L0 + 2 + l)
                dve.wait_ge(s_hi, 2 * NT + l + 1)
                dve.tensor_tensor(AGG[:, :, 0:D], H, TAB[:, 0, :, 0, :], ALU.subtract).then_inc(s_rest, 1)
                dve.wait_ge(s_rest, 2 * NT + l + 1)
                dve.wait_ge(s_mid, 2 * NT + l + 1)
                dve.tensor_tensor(TAB[:, 0, :, 2, :], AGG[:, :, 0:D], TAB[:, 0, :, 1, :], ALU.subtract).then_inc(s_tab, 1)
                dve.wait_ge(s_tab, l + 1)
                edge_dve(dve, gstep, L0 + l, miss)
                linear_dve(dve, step, l)


_INS = ["x", "src", "dst", "L0_gnn_W_enc", "L0_gnn_b_enc", "L0_gnn_msg_W1", "L0_gnn_msg_b1", "L0_gnn_msg_W2",
        "L0_gnn_msg_b2", "L0_gnn_upd_W", "L0_gnn_upd_b", "L0_gnn_ln_g", "L0_gnn_ln_b", "L0_gnn_W_out",
        "L0_gnn_b_out", "L1_gnn_Wl", "L1_gnn_bl", "L1_gnn_Wr"]


def kernel(**inputs):
    import numpy as np
    import concourse.bacc as bacc
    from concourse.bass_utils import run_bass_kernel_spmd as run

    nc = bacc.Bacc("TRN2", target_bir_lowering=False, num_devices=1)
    arrays, args = {}, []
    for name in _INS:
        a = np.ascontiguousarray(inputs[name])
        arrays[f"in_{name}"] = a
        args.append(nc.dram_tensor(f"in_{name}", a.shape, mybir.dt.from_np(a.dtype), kind="ExternalInput").ap())
    args.append(nc.dram_tensor("out_0", (N, D), F32, kind="ExternalOutput").ap())
    build(nc, *args)
    return run(nc, [arrays], core_ids=[0]).results[0]["out_0"]
```

```python
from contextlib import ExitStack

import concourse.bass as bass
from concourse import mybir

F32 = mybir.dt.float32
BF16 = mybir.dt.bfloat16
I32 = mybir.dt.int32
ALU = mybir.AluOpType
ACT = mybir.ActivationFunctionType
AX = mybir.AxisListType.X

N = 6250
E = 206250
D = 128
P = 125
NT = N // P
ET = E // P
PAIRS = ET // 2
L0 = 2
L1 = 3
EPS = 1e-5
PARTS = 3
ROW = PARTS * D
W = D + 1

CELL = 128
GROUP = 4
PAIRED = NT // 2
BODY = 2 * NT // GROUP
FIRST = [0, NT // GROUP]
LAST = [(NT - 1) // GROUP, BODY - 1]
RING = 5
CHUNKS = [(0, 3)] + [(g, 2) for g in range(3, BODY, 2)]
OWN = [0, 5]
PAY = 2 * NT + 2
SAMPLE = 33
COLS = 36
WIN = 128 * COLS
RG = 4
RK = COLS // RG
MAGIC = 1.5 * 2.0 ** 23

assert RG * RK == COLS and ET % SAMPLE == 0 and sum(n for _, n in CHUNKS) == BODY and len(CHUNKS) % 2 == 0 and BODY % RING == 0

assert NT * P == N and ET * P == E and NT % 2 == 0 and ET % 2 == 0

ENC, MSG, UPD_H, UPD_M, OUT, LIN_L, LIN_R = 0, 1, 5, 7, 9, 10, 13
NW = 16
B_ENC, B_1, B_UPD, LN_G, LN_B, B_OUT, B_LIN = 0, 1, 3, 5, 7, 9, 10
NB = 13
LOADS = NW + 2 * L0 + NB
STAGES = ["enc", "ab0", "upd0", "ab1", "upd1", "out", "lin0", "lin1", "lin2"]
STAGE0 = {name: 2 + NT * k for k, name in enumerate(STAGES)}
EDGE = ["ab0", "ab1", "lin0", "lin1", "lin2"]
AGG_STAGES = ["upd0", "upd1", "lin0", "lin1", "lin2"]
HI0 = [0, NT, 2 * NT, 2 * NT + 1, 2 * NT + 2]


class Steps:

    def __init__(self, eng, sem):
        self.eng, self.sem, self.base, self.k, self.i, self.per = eng, sem, 0, 0, None, 0

    def now(self):
        return self.base + self.k if self.i is None else self.i * self.per + (self.base + self.k)

    def did(self, ins):
        ins.then_inc(self.sem, 1)
        self.k += 1
        return self.now()

    def after(self, value):
        self.eng.wait_ge(self.sem, value)

    def last(self):
        self.after(self.now())

    def enter(self, i, per):
        self.base, self.k, self.i, self.per = self.base + self.k, 0, i, per

    def leave(self, times):
        assert self.k == self.per, (self.k, self.per)
        self.base, self.k, self.i = self.base + times * self.per, 0, None


def build(nc, x, src, dst, W_enc, b_enc, msg_W1, msg_b1, msg_W2, msg_b2, upd_W, upd_b, ln_g, ln_b,
          W_out, b_out, Wl, bl, Wr, out):
    with ExitStack() as ctx:
        def sb(name, shape, dt=F32):
            return ctx.enter_context(nc.sbuf_tensor(name, shape, dt))

        def sem(name):
            return ctx.enter_context(nc.semaphore(name))

        table_dram = [nc.dram_tensor(f"table_{n}", [N, ROW], BF16, kind="Internal").ap() for n in "ab"]
        sums_dram = [nc.dram_tensor(f"sums_{u}", [N + P, W], F32, kind="Internal").ap() for u in range(2)]

        slots_dram = nc.dram_tensor("slots_turned", [PAIRED, 2, 2 * NT, CELL], BF16, kind="Internal").ap()

        Hf = sb("Hf", [128, (NT + 1) * D])
        Hs = Hf[0:P, :].rearrange("p (t d) -> p t d", d=D)
        H = Hs[:, 1:NT + 1, :]
        AGGf = sb("AGGf", [128, (NT + 1) * W])
        AGGs = AGGf[0:P, :].rearrange("p (t d) -> p t d", d=W)
        AGG = AGGs[:, 1:NT + 1, :]
        selfs = sb("selfs", [128, NT + 1])
        half = NT * ROW // 2
        tabf = sb("tabf", [128, 2 * half])
        TAB = tabf[0:P, :].bitcast(BF16).rearrange("p (n t c d) -> p n t c d", n=2, t=NT, c=PARTS)
        wnat = tabf[:, 0:(NW + L0) * D].rearrange("p (w d) -> p w d", d=D)
        AGG1 = tabf[0:P, 0:NT * W].rearrange("p (t d) -> p t d", d=W)
        X = tabf[0:P, half:half + NT * D].rearrange("p (t d) -> p t d", d=D)
        wT = sb("wT", [D, NW, D])
        wM = sb("wM", [D, L0, D])
        bias = sb("bias", [P, NB, D])
        b2col = sb("b2col", [D, L0])
        b2upd = sb("b2upd", [P, L0, D])
        abias = sb("abias", [P, L0, 2, D])
        ident = sb("ident", [128, 128])
        before = sb("before", [P, P])
        ones = sb("ones", [128, 128])
        eps = sb("eps", [P, 1])
        stats = sb("stats", [P, NT, 6])
        mean = sb("mean", [P, NT])
        var = sb("var", [P, NT])
        std = sb("std", [P, NT])
        rstd = sb("rstd", [P, NT])
        sq = sb("sq", [P, NT])
        degc = sb("degc", [P, NT])
        invdeg = sb("invdeg", [P, NT])
        ones_bf = sb("ones_bf", [128, 128], BF16)
        ident_bf = sb("ident_bf", [128, 128], BF16)
        below_bf = sb("below_bf", [128, 128], BF16)
        col1 = sb("col1", [128, 128], BF16)
        row1 = sb("row1", [128, 1])
        tilec = sb("tilec", [128, 2, NT + 2])
        junk = sb("junk", [P, 1])
        zrow = sb("zrow", [P, W])
        slots = sb("slots", [128, 2, NT + 1, NT], BF16)
        lo = sb("lo", [1, NT + 2])
        loi = sb("loi", [1, NT + 2], I32)
        placed = sb("placed", [128, 2])
        missing = sb("missing", [1, 2])
        missingi = sb("missingi", [1, 1], I32)

        arena_words = 11790
        arena = sb("arena", [128, arena_words])

        def carver(memory, words):
            at = [0]

            def carve(shape, dt=F32):
                n = 1
                for k in shape[1:]:
                    n *= k
                size = (n + 1) // 2 if dt == BF16 else n
                a = memory[0:shape[0], at[0]:at[0] + size]
                at[0] += size
                assert at[0] <= words, (at[0], words)
                if dt != F32:
                    a = a.bitcast(dt)[:, 0:n]
                dims = " ".join(f"d{k}" for k in range(1, len(shape)))
                return a.rearrange(f"p ({dims}) -> p {dims}", **{f"d{k}": shape[k] for k in range(1, len(shape))})
            return carve

        carve = carver(arena, arena_words)
        tile_in = carve([P, 2, 2, D])
        hT = carve([128, 2, 2, 128])
        raw = carve([P, 2, 2, D])
        rest = carve([P, 2, 2, D])
        tmp = carve([P, 2, 2, D])
        carve = carver(arena, arena_words)
        srci = carve([P, ET], I32)
        dsti = carve([P, ET], I32)
        sidx = carve([P, 2], I32)
        didx = carve([P, 2], I32)
        widx = carve([P, 2], I32)
        dcol = carve([P, 2])
        drep = carve([P, 2, P])
        same = carve([P, 2, P])
        earlier = carve([P, 2, P])
        nearl = carve([P, 2])
        wsel = carve([P, 2, 2])
        rows = carve([P, 2, 2, PARTS, D], BF16)
        part = carve([P, 2, 2, D])
        msum = carve([P, 2, W])
        msg = carve([P, 2, W])
        carve = carver(arena, arena_words)
        slist = [carve([P, 2, n * GROUP * CELL], BF16) for _, n in (CHUNKS[0], CHUNKS[1])]
        toN = carve([P, RING, 2, GROUP * CELL], BF16)
        toE = carve([128, RING, GROUP, 126], BF16)
        mparts = carve([128, RING, PARTS, GROUP, W + 1], BF16)
        mrest = carve([128, 2, GROUP, D])
        cur = carve([P, 2, ROW], BF16)
        curS = carve([128, 2 * NT, 2], BF16)
        carve = carver(arena, arena_words)
        oneE = carve([128, RING, GROUP, 2, 126], BF16)
        cells = carve([P, RING, GROUP, 126], BF16)
        curS2 = carve([128, 2 * NT, 2, 2], BF16)
        carve = carver(Hf, NT * D)
        one_cell = carve([128, 2, COLS, NT], BF16)
        payload = carve([128, 2, COLS, PAY], BF16)
        carve = carver(AGGf, NT * W)
        one_slot = carve([128, COLS, CELL], BF16)
        prod = carve([128, RG, RK * NT])
        carve = carver(Hf, NT * D)
        dstl = carve([P, ET], I32)
        samp = carve([P, NT])
        less = carve([P, NT + 1, NT])
        nless = carve([P, NT + 1])
        carve = carver(arena, arena_words)
        win = carve([128, 2, 2, COLS], I32)
        node = carve([128, 2, 2, COLS])
        off1 = carve([128, 2, 2, COLS])
        srct = carve([128, 2, 3, COLS])
        inside = carve([128, 2, 2, COLS])
        q1 = carve([128, 2, COLS, 2], BF16)
        rank = carve([128, 2, COLS])
        loops = carve([128, 2, COLS])
        selfe = carve([128, 2, COLS])
        others = carve([128, 2, COLS])
        selfto = carve([128, 2, COLS])
        slot0 = carve([128, 2, COLS])
        keep = carve([128, COLS])
        pay = carve([128, 2, COLS])
        pay2 = carve([128, 2, COLS, 2], BF16)
        slot1 = carve([128, 2, COLS, 2], BF16)
        rtot = carve([128, 2, RG, NT], BF16)
        Sb = carve([128, 2, 2 * NT], BF16)
        STb = carve([2 * NT, 2, CELL], BF16)
        filled = carve([128, NT, NT])
        b2rep = carve([D, L0, P])
        counti = carve([128, 128], I32)
        rowi = carve([128, 1], I32)
        tilei = carve([128, 2, NT + 2], I32)
        junki = carve([P, 1], I32)

        psum = ctx.enter_context(nc.psum_tensor("psum", [128, 8, 512], F32))
        bank = [psum[:, k, :] for k in range(8)]
        psRank = psum[:, 0:RG, 0:RK * NT]
        psTot, psSlot, psTurn, psCount = bank[4], bank[5], bank[6], bank[7]
        psMsg, psA = [bank[1]] + bank[4:8], bank[2:4]
        psT = [bank[0], bank[1]]
        psO = [bank[2], bank[3]]
        psD = [bank[4], bank[5]]
        psM = [bank[6], bank[7]]

        s_w = sem("weights_loaded")
        s_x = sem("x_loaded")
        s_e = sem("edges_loaded")
        s_const = sem("constants_ready")
        s_wT = sem("weight_transposed")
        s_wTc = sem("weight_copied")
        s_b2 = sem("b2_spread")
        s_comp = sem("composed_ready")
        s_compc = sem("composed_copied")
        s_in = sem("tile_staged")
        s_tT = sem("tile_transposed")
        s_tC = sem("tile_copied")
        s_tO = sem("tile_product_ready")
        s_tE = sem("tile_finished")
        s_raw = sem("raw_ready")
        s_hi = sem("high_part_ready")
        s_rest = sem("rest_ready")
        s_mid = sem("middle_part_ready")
        s_dve = sem("vector_step")
        s_var = sem("variance_ready")
        s_std = sem("std_ready")
        s_h = sem("hidden_ready")
        s_tab = sem("linear_table_ready")
        s_agg = sem("aggregate_ready")
        s_fin = sem("result_ready")
        s_out = sem("result_stored")
        s_pset = sem("constant_step")
        gate = {e: sem(f"gate_{e}") for e in ("act", "dve", "pool")}
        g_tab = sem("general_table_stored")
        g_zero = sem("general_sums_cleared")
        g_idx = sem("general_indices_copied")
        g_rows = [[sem(f"general_rows_gathered{k}_{u}") for u in range(2)] for k in range(len(EDGE))]
        g_drep = sem("general_destinations_spread")
        g_dT = sem("general_destinations_turned")
        g_same = sem("general_equal_destinations_found")
        g_widx = sem("general_write_rows_ready")
        g_msg = sem("general_messages_ready")
        g_sum = sem("general_messages_summed")
        g_cp = sem("general_sums_copied")
        g_add = [[sem(f"general_sums_added{k}_{u}") for u in range(2)] for k in range(len(EDGE))]
        g_back = sem("general_sums_loaded")
        g_dve = sem("general_vector_step")

        o_dst = sem("sort_destinations_loaded")
        o_less = sem("sort_samples_counted")
        o_nless = sem("sort_starts_summed")
        o_lo = sem("sort_starts_ready")
        o_win = [sem(f"sort_window_loaded{u}") for u in range(2)]
        o_read = sem("sort_window_read")
        o_cell = sem("sort_cells_ready")
        o_tot = sem("sort_totals_ready")
        o_totc = sem("sort_totals_copied")
        o_rank = sem("sort_ranks_ready")
        o_prod = sem("sort_ranks_picked")
        o_pay = sem("sort_payload_ready")
        o_mul = sem("sort_payload_placed")
        o_mulv = sem("sort_sources_placed")
        o_slot = sem("sort_slots_ready")
        o_perm = sem("sort_slots_filled")
        o_S = sem("sort_slots_copied")
        o_turn = sem("sort_slots_turned")
        o_ST = sem("sort_turned_copied")
        o_store = [sem(f"sort_slots_stored{u}") for u in range(2)]
        o_dve = sem("sort_vector_step")
        o_fill = sem("sort_fill_counted")
        o_sum = sem("sort_fill_summed")
        o_flag = sem("sort_flag_ready")
        f_list = [sem(f"cells_slot_list_loaded{b}") for b in range(2)]
        f_cur = [sem(f"cells_tile_rows_copied{u}") for u in range(2)]
        f_own = sem("cells_tile_slots_copied")
        f_one = sem("cells_count_column_set")
        f_toN = sem("cells_node_onehots_ready")
        f_toE = sem("cells_slot_onehots_ready")
        f_gat = sem("cells_rows_gathered")
        f_hi = sem("cells_high_part_ready")
        f_rest = sem("cells_rest_ready")
        f_mid = sem("cells_middle_part_ready")
        f_lo = sem("cells_low_part_ready")
        f_sca = sem("cells_messages_summed")
        f_agg = sem("cells_aggregate_copied")
        l_own = sem("linear_tile_slots_copied")
        l_from = sem("linear_onehots_ready")
        l_C = sem("linear_counts_ready")
        l_Cc = sem("linear_counts_copied")
        l_sum = sem("linear_rows_summed")
        l_agg = sem("linear_aggregate_copied")

        def hold(eng, name, s, value):
            eng.wait_ge(s, value)
            eng.sem_inc(gate[name], 1)

        def load_flag(eng):
            eng.wait_ge(o_flag, 1)
            return eng.value_load(missingi[0:1, 0:1], min_val=0, max_val=1)

        def edge_sp(sp, k, miss):
            with sp.If(miss < 1):
                if k < L0:
                    cells_sp(sp, k)
            with sp.If(miss > 0):
                general_sp(sp, k)

        def edge_pool(pool, k, miss):
            with pool.If(miss < 1):
                cells_pool(pool, k) if k < L0 else linear_pool(pool, k - L0)
            with pool.If(miss > 0):
                general_pool(pool, k)

        def edge_pe(pe, k, miss):
            with pe.If(miss < 1):
                cells_pe(pe, k) if k < L0 else linear_pe(pe, k - L0)
            with pe.If(miss > 0):
                general_pe(pe, k)

        def edge_act(act, k, miss):
            with act.If(miss < 1):
                cells_act(act, k) if k < L0 else linear_act(act, k - L0)
            with act.If(miss > 0):
                general_act(act, k)

        def edge_dve(dve, step, k, miss):
            with dve.If(miss < 1):
                cells_dve(dve, k) if k < L0 else counts_dve(dve, k - L0)
            with dve.If(miss > 0):
                general_dve(dve, step, k)

        def pairs(a):
            return a.rearrange("p c (n e) -> p c n e", e=2)

        def columns(numbers, width, count):
            a = numbers[:, 0:width].rearrange("p (o n e) -> p o n e", o=1, e=2)
            return a.to_broadcast([128, count, width // 2, 2])

        def along(values, width):
            c = values.shape[1]
            return values.rearrange("p c (o e) -> p c o e", o=1).to_broadcast([128, c, width // 2, 2])

        def twice(a):
            return a.rearrange("p (t o) -> p t o", o=1).to_broadcast([128, COLS, 2])

        def sort_sp(sp):
            sp.dma_start(dstl, dst.rearrange("(p t) -> p t", p=P)).then_inc(o_dst, 16)
            sp.wait_ge(o_lo, 1)

            def window(t, u):
                start = sp.value_load(loi[0:1, t], min_val=0, max_val=E - WIN)
                for n, ends in enumerate((src, dst)):
                    sp.dma_start(win[:, u, n, :], ends[bass.ds(start, WIN)].rearrange("(p t) -> p t", p=128)
                                 ).then_inc(o_win[u], 16)

            window(slice(0, 1), 0)
            with sp.Fori(0, NT // 2) as i:
                for u in range(2):
                    sp.wait_ge(o_read, i * 2 + (u + 2))
                    window(bass.ds(i * 2 + (u + 1), 1), 1 - u)

        def sort_pool(pool):
            with pool.Fori(0, NT // 2) as i:
                for u in range(2):
                    hold(pool, "pool", o_pay, i * 2 + (u + 3))
                    hold(pool, "pool", o_perm, i * 2 + (u + 1))
                    pool.tensor_tensor(payload[:, u, :, NT:2 * NT], one_cell[:, u],
                                       pay[:, u, :].rearrange("p (t o) -> p t o", o=1).to_broadcast([128, COLS, NT]),
                                       ALU.mult).then_inc(o_mul, 1)

        def sort_pe(pe):
            pe.wait_ge(o_less, 1)
            pe.matmul(psCount[0:1, 0:NT + 1], ones[0:P, 0:1], nless, start=True, stop=True).then_inc(o_nless, 1)

            def ranks(n, u):
                pe.wait_ge(o_cell, n + 3)
                pe.wait_ge(o_totc, n + 2)
                cell = one_cell[:, u].rearrange("p (g k) c -> p g k c", g=RG)
                for k in range(RK):
                    m = pe.matmul(psTot[:, 0:RG * NT].rearrange("p (g c) -> p g c", g=RG), ident_bf[:], cell[:, :, k, :],
                                  start=k == 0, stop=k == RK - 1)
                m.then_inc(o_tot, 1)
                pe.wait_ge(o_prod, n + 2)
                pe.wait_ge(o_totc, n + 3)
                for g in range(RG):
                    bk = psRank[:, g, :].rearrange("p (k c) -> p k c", k=RK)
                    all_k = [128, RK, NT]
                    pe.matmul(bk, below_bf[:], rtot[:, u, g:g + 1, :].to_broadcast(all_k), start=True, stop=False)
                    for e in range(g):
                        pe.matmul(bk, ones_bf[:], rtot[:, u, e:e + 1, :].to_broadcast(all_k), start=False, stop=False)
                    for k in range(RK - 1):
                        m = pe.matmul(bk[:, k + 1:RK, :], ident_bf[:], cell[:, g, k:k + 1, :].to_broadcast([128, RK - 1 - k, NT]),
                                      start=False, stop=k == RK - 2)
                m.then_inc(o_rank, 1)

            def fill(n, u):
                pe.wait_ge(o_slot, n + 3)
                pe.wait_ge(o_mul, n + 3)
                pe.wait_ge(o_mulv, n + 3)
                pe.wait_ge(o_S, n + 2)
                for t in range(COLS):
                    m = pe.matmul(psSlot[:, 0:PAY], one_slot[:, t, :], payload[:, u, t, :], start=t == 0, stop=t == COLS - 1)
                m.then_inc(o_perm, 1)
                pe.wait_ge(o_ST, n + 2)
                pe.wait_ge(o_S, n + 3)
                pe.transpose(psTurn[0:2 * NT, 0:CELL // 2].bitcast(BF16), Sb[:, u, :], ident_bf[:]).then_inc(o_turn, 1)

            ranks(0, 0)
            with pe.Fori(0, NT // 2) as i:
                for u in range(2):
                    ranks(i * 2 + (u + 1), 1 - u)
                    fill(i * 2 + u, u)
            pe.wait_ge(o_fill, 1)
            for n in range(2):
                m = pe.matmul(psCount[0:1, 64:65], ones[:, 0:1], placed[:, n:n + 1], start=n == 0, stop=n == 1)
            m.then_inc(o_sum, 1)

        def sort_act(act):
            def totals(n, u):
                act.wait_ge(o_tot, n + 3)
                act.wait_ge(o_rank, n + 2)
                act.copy(rtot[:, u], psTot[:, 0:RG * NT].rearrange("p (g c) -> p g c", g=RG)).then_inc(o_totc, 1)

            totals(0, 0)
            with act.Fori(0, NT // 2) as i:
                for u in range(2):
                    totals(i * 2 + (u + 1), 1 - u)
                    hold(act, "act", o_turn, i * 2 + (u + 1))
                    hold(act, "act", o_perm, i * 2 + (u + 3))
                    act.copy(slots[:, :, bass.ds(i * 2 + u, 1), :], psSlot[:, 0:2 * NT].rearrange("p (n o c) -> p n o c", n=2, o=1))
                    act.copy(selfs[:, bass.ds(i * 2 + (u + 1), 1)], psSlot[:, 2 * NT:2 * NT + 1])
                    act.copy(Sb[:, u, :], psSlot[:, 0:2 * NT]).then_inc(o_S, 1)
                    act.wait_ge(o_turn, i * 2 + (u + 3))
                    act.wait_ge(o_store[u], i * 32 + 32)
                    act.copy(STb[:, u, :], psTurn[0:2 * NT, 0:CELL // 2].bitcast(BF16)).then_inc(o_ST, 1)
                    act.wait_ge(o_ST, i * 2 + (u + 3))
                    for n in range(2):
                        act.dma_start(slots_dram[bass.ds(i, 1), n, u * NT:(u + 1) * NT, :].rearrange("o c e -> (o c) e"),
                                      STb[n * NT:(n + 1) * NT, u, :]).then_inc(o_store[u], 16)
            for u in range(2):
                act.wait_ge(o_store[u], 32 + 32 * (NT // 2))

        def sort_dve(dve):
            step = Steps(dve, o_dve)
            dve.wait_ge(o_dst, 16)
            step.did(dve.tensor_copy(samp, dstl[:, 0:ET:SAMPLE]))
            step.last()
            grid = [P, NT + 1, NT]
            step.did(dve.tensor_tensor(less, samp.rearrange("p (o t) -> p o t", o=1).to_broadcast(grid),
                                       tilec[0:P, 0, 0:NT + 1].rearrange("p (t o) -> p t o", o=1).to_broadcast(grid), ALU.is_lt))
            step.last()
            dve.tensor_reduce(nless, less, AX, ALU.add).then_inc(o_less, 1)
            dve.wait_ge(o_nless, 1)
            step.did(dve.tensor_scalar(lo[:, 0:NT + 1], psCount[0:1, 0:NT + 1], float(SAMPLE), float(1 - SAMPLE), ALU.mult, ALU.add))
            step.last()
            dve.tensor_scalar(loi[:, 0:NT + 1], lo[:, 0:NT + 1], 0.0, float(E - WIN), ALU.max, ALU.min).then_inc(o_lo, 1)

            def find_cells(n, u, loaded, tile):
                dve.wait_ge(o_win[u], loaded)
                a = step.did(dve.tensor_copy(node[:, u], win[:, u]))
                step.after(a)
                dve.sem_inc(o_read, 1)
                t = [srct[:, u, k, :] for k in range(3)]
                to1 = off1[:, u, 1, :]
                a = step.did(dve.tensor_scalar(t[0], node[:, u, 0, :], 1.0 / P, -((P - 1) / 2) / P, ALU.mult, ALU.add))
                hold(dve, "dve", o_dve, a)
                b = step.did(dve.tensor_scalar(to1, node[:, u, 1, :], tilec[:, 1, tile], None, ALU.subtract))
                step.did(dve.tensor_tensor(loops[:, u], node[:, u, 0, :], node[:, u, 1, :], ALU.is_equal))
                a = step.did(dve.tensor_scalar(t[1], t[0], MAGIC, None, ALU.add))
                step.after(b)
                b = step.did(dve.tensor_scalar(inside[:, u, 0, :], to1, 1.0, None, ALU.is_ge))
                step.after(a)
                a = step.did(dve.tensor_scalar(t[2], t[1], MAGIC, None, ALU.subtract))
                step.after(b)
                b = step.did(dve.scalar_tensor_tensor(out=inside[:, u, 1, :], in0=to1, scalar=float(P),
                                                      in1=inside[:, u, 0, :], op0=ALU.is_le, op1=ALU.mult))
                step.after(b)
                b = step.did(dve.tensor_tensor(selfe[:, u], loops[:, u], inside[:, u, 1, :], ALU.mult))
                a = step.did(dve.scalar_tensor_tensor(out=t[0], in0=t[2], scalar=-float(P), in1=node[:, u, 0, :],
                                                      op0=ALU.mult, op1=ALU.add))
                step.after(b)
                b = step.did(dve.tensor_tensor(others[:, u], inside[:, u, 1, :], selfe[:, u], ALU.subtract))
                c = step.did(dve.tensor_tensor(selfto[:, u], selfe[:, u], to1, ALU.mult))
                step.after(a)
                step.did(dve.tensor_scalar(off1[:, u, 0, :], t[0], 1.0, None, ALU.add))
                step.after(b)
                step.did(dve.scalar_tensor_tensor(out=q1[:, u], in0=twice(t[2]), scalar=1.0, in1=twice(others[:, u]),
                                                  op0=ALU.add, op1=ALU.mult))
                step.after(c)
                a = step.did(dve.tensor_tensor(slot0[:, u], others[:, u], selfto[:, u], ALU.add))
                step.after(a)
                dve.wait_ge(o_mul, n + 1)
                dve.wait_ge(o_mulv, n + 1)
                dve.tensor_tensor(pairs(one_cell[:, u]), columns(col1, NT, COLS), along(q1[:, u], NT), ALU.is_equal).then_inc(o_cell, 1)

            def find_slots(n, u, tile):
                dve.wait_ge(o_rank, n + 3)
                p = step.did(dve.tensor_tensor(prod, one_cell[:, u].rearrange("p (g k) c -> p g (k c)", g=RG), psRank, ALU.mult))
                step.after(p)
                dve.sem_inc(o_prod, 1)
                a = step.did(dve.tensor_reduce(rank[:, u, :], prod.rearrange("p g (k c) -> p (g k) c", c=NT), AX, ALU.add))
                step.after(a)
                step.did(dve.tensor_scalar(keep, rank[:, u, :], float(CELL), None, ALU.is_lt))
                a = step.did(dve.tensor_tensor(slot1[:, u], twice(rank[:, u, :]), twice(slot0[:, u]), ALU.add))
                step.after(a)
                a = step.did(dve.tensor_tensor(pay[:, u], keep, off1[:, u, 1, :], ALU.mult))
                b = step.did(dve.tensor_tensor(pay2[:, u], twice(keep), twice(off1[:, u, 0, :]), ALU.mult))
                step.after(a)
                dve.sem_inc(o_pay, 1)
                dve.wait_ge(o_perm, n + 2)
                step.did(dve.tensor_copy(payload[:, u, :, 2 * NT:PAY], twice(selfe[:, u])))
                dve.tensor_tensor(pairs(one_slot), columns(col1, CELL, COLS), along(slot1[:, u], CELL), ALU.is_equal).then_inc(o_slot, 1)
                step.after(b)
                dve.tensor_tensor(pairs(payload[:, u, :, 0:NT]), pairs(one_cell[:, u]), along(pay2[:, u], NT), ALU.mult
                                  ).then_inc(o_mulv, 1)

            find_cells(0, 0, 32, slice(0, 1))
            with dve.Fori(0, NT // 2) as i:
                step.enter(i, 2 * (15 + 7))
                for u in range(2):
                    find_cells(i * 2 + (u + 1), 1 - u, i * 32 + (32 if u == 0 else 64), bass.ds(i * 2 + (u + 1), 1))
                    find_slots(i * 2 + u, u, bass.ds(i * 2 + u, 1))
                step.leave(NT // 2)
            dve.wait_ge(o_S, NT + 2)
            step.did(dve.tensor_scalar(filled, slots[:, 1, 0:NT], 0.0, None, ALU.is_gt))
            step.last()
            step.did(dve.tensor_reduce(placed[:, 1:2], selfs[:, 1:NT + 1], AX, ALU.add))
            dve.tensor_reduce(placed[:, 0:1], filled.rearrange("p t c -> p (t c)"), AX, ALU.add).then_inc(o_fill, 1)
            dve.wait_ge(o_sum, 1)
            step.did(dve.tensor_scalar(missing[:, 0:1], psCount[0:1, 64:65], -1.0, float(E), ALU.mult, ALU.add))
            step.last()
            dve.tensor_scalar(missingi[:], missing[:, 0:1], 0.0, None, ALU.is_gt).then_inc(o_flag, 1)

        def group_done(i, k, pos, extra=0):
            return i * BODY + (BODY + k * (PAIRED * BODY + extra) + pos + 1)

        def before_it(i, k, pos, buffers, extra=0):
            at = pos % BODY
            last = at - buffers if at >= buffers else max(q for q in range(BODY) if q % buffers == at) - BODY
            return group_done(i, k, pos - at + last, extra)

        def cell(pos, c):
            return divmod(pos % BODY * GROUP + c, NT)

        def cells_sp(sp, k):
            sp.wait_ge(s_tE, STAGE0[EDGE[k]] + NT)
            for u in range(2):
                sp.wait_ge(o_store[u], 32 + 32 * PAIRED)

            def load(i, pair, tile, c):
                g0, n = CHUNKS[c]
                g1, n1 = CHUNKS[c - 2]
                sp.wait_ge(f_toN, group_done(i, k, g1 + n1 - 1 - (BODY if c < 2 else 0), 3))
                for a in range(2):
                    sp.dma_start(slist[c % 2][:, a, 0:n * GROUP * CELL],
                                 slots_dram[pair, a, g0 * GROUP:(g0 + n) * GROUP, :]
                                 .rearrange("o c e -> o (c e)").to_broadcast([P, n * GROUP * CELL])).then_inc(f_list[c % 2], 16)
                if c in OWN:
                    u = OWN.index(c)
                    sp.wait_ge(f_gat, group_done(i, k, LAST[u] - BODY, 2))
                    sp.dma_start(cur[:, u], TAB[:, 1, tile(u)].rearrange("p o c d -> p (o c d)")).then_inc(f_cur[u], 16)

            with sp.Fori(0, PAIRED) as i:
                for c in range(len(CHUNKS)):
                    load(i, bass.ds(i, 1), lambda u: bass.ds(i * 2 + u, 1), c)
            load(PAIRED, slice(0, 1), lambda u: slice(u, u + 1), 0)

        def cells_pool(pool, k):
            hold(pool, "pool", s_tE, STAGE0[EDGE[k]] + NT)
            pool.memset(mparts[:, :, 0, :, D:W], 1.0).then_inc(f_one, 1)
            hold(pool, "pool", f_one, k + 1)

            def own_slots(tile, u):
                pool.tensor_copy(curS[:, u * NT:(u + 1) * NT], slots[:, 1, tile, :].rearrange("p o c -> p c o").to_broadcast([128, NT, 2])
                                 ).then_inc(f_own, 1)

            own_slots(slice(0, 1), 0)
            with pool.Fori(0, PAIRED) as i:
                hold(pool, "pool", f_toE, group_done(i, k, -1, 1))
                own_slots(bass.ds(i * 2 + 1, 1), 1)
                for pos in range(BODY):
                    hold(pool, "pool", f_mid, group_done(i, k, pos))
                    pool.tensor_tensor(mparts[:, pos % RING, 2, :, 0:D], mrest[:, pos % 2], mparts[:, pos % RING, 1, :, 0:D], ALU.subtract
                                       ).then_inc(f_lo, 1)
                    if pos == LAST[0] + 4:
                        hold(pool, "pool", f_toE, group_done(i, k, LAST[0], 1))
                        own_slots(bass.ds(i * 2 + 2, 1), 0)

        def cells_pe(pe, k):
            def gather(i, pos):
                for u in range(2):
                    if pos % BODY == FIRST[u]:
                        pe.wait_ge(f_cur[u], i * 16 + (k * (PAIRED + 1 - u) + pos // BODY + 1) * 16)
                pe.wait_ge(f_toN, group_done(i, k, pos, 3))
                pe.wait_ge(f_rest, before_it(i, k, pos, RING))
                b = pos % BODY % RING
                for c in range(GROUP):
                    u, t = cell(pos, c)
                    to = psMsg[b][:, c * D:(c + 1) * D]
                    for p in range(PARTS):
                        pe.matmul(to, toN[:, b, 0, c * CELL:(c + 1) * CELL], TAB[:, 0, t, p, :], start=p == 0, stop=False)
                    for p in range(PARTS):
                        m = pe.matmul(to, toN[:, b, 1, c * CELL:(c + 1) * CELL], cur[:, u, p * D:(p + 1) * D],
                                      start=False, stop=p == PARTS - 1)
                m.then_inc(f_gat, 1)

            def scatter(i, pos):
                pe.wait_ge(f_toE, group_done(i, k, pos, 1))
                pe.wait_ge(f_lo, group_done(i, k, pos))
                for u in range(2):
                    if pos == FIRST[u]:
                        pe.wait_ge(f_agg, i * 2 + (k * (NT + 1) + u + 2))
                for c in range(GROUP):
                    u, t = cell(pos, c)
                    for p in range(PARTS):
                        w = W if p == 0 else D
                        m = pe.matmul(psA[u][0:P, 0:w], toE[:, pos % RING, c, 0:P], mparts[:, pos % RING, p, c, 0:w],
                                      start=t == 0 and p == 0, stop=t == NT - 1 and p == PARTS - 1, skip_group_check=True)
                m.then_inc(f_sca, 1)

            for pos in range(2):
                gather(0, pos)
            with pe.Fori(0, PAIRED) as i:
                for pos in range(BODY):
                    gather(i, pos + 2)
                    scatter(i, pos)

        def cells_act(act, k):
            with act.Fori(0, PAIRED) as i:
                def high(pos):
                    act.wait_ge(f_gat, group_done(i, k, pos, 2))
                    act.wait_ge(f_sca, before_it(i, k, pos, RING))
                    act.activation(mparts[:, pos % RING, 0, :, 0:D], psMsg[pos % RING].rearrange("p (c d) -> p c d", d=D), ACT.Relu
                                   ).then_inc(f_hi, 1)

                def middle(pos):
                    act.wait_ge(f_rest, group_done(i, k, pos))
                    act.copy(mparts[:, pos % RING, 1, :, 0:D], mrest[:, pos % 2]).then_inc(f_mid, 1)

                for pos in range(BODY):
                    if pos:
                        middle(pos - 1)
                    high(pos)
                middle(BODY - 1)

        def cells_dve(dve, k):
            def by_node(i, pos):
                g = pos % BODY
                c = max(n for n, (g0, _) in enumerate(CHUNKS) if g0 <= g)
                at = (g - CHUNKS[c][0]) * GROUP * CELL
                per = len(CHUNKS) // 2
                n = pos // BODY * per + c // 2
                dve.wait_ge(f_list[c % 2], i * (per * 32) + (k * (PAIRED * per + 1 - c % 2) * 32 + 32 * (n + 1)))
                dve.wait_ge(f_gat, before_it(i, k, pos, RING, 2))
                dve.tensor_scalar(toN[:, g % RING], slist[c % 2][:, :, at:at + GROUP * CELL], row1[0:P, :], None, ALU.is_equal
                                  ).then_inc(f_toN, 1)

            def by_slot(i, pos):
                g = pos % BODY
                for u in range(2):
                    if g == FIRST[u]:
                        dve.wait_ge(f_own, i * 2 + (k * (NT + 1) + pos // BODY * 2 + u + 1))
                dve.wait_ge(f_sca, before_it(i, k, pos, RING))
                dve.tensor_tensor(pairs(toE[:, g % RING]), columns(col1, 126, GROUP),
                                  along(curS[:, g * GROUP:(g + 1) * GROUP], 126), ALU.is_equal).then_inc(f_toE, 1)

            def rest_of(i, pos):
                dve.wait_ge(f_hi, group_done(i, k, pos))
                dve.wait_ge(f_lo, before_it(i, k, pos, 2))
                dve.scalar_tensor_tensor(out=mrest[:, pos % 2], in0=psMsg[pos % RING].rearrange("p (c d) -> p c d", d=D), scalar=0.0,
                                         in1=mparts[:, pos % RING, 0, :, 0:D], op0=ALU.max, op1=ALU.subtract).then_inc(f_rest, 1)

            def sums(i, at, u, pos):
                hold(dve, "dve", f_sca, group_done(i, k, pos))
                dve.tensor_tensor(AGGs[:, at, :], AGGs[:, at, :], psA[u][0:P, 0:W].rearrange("p (o d) -> p o d", o=1), ALU.add
                                  ).then_inc(f_agg, 1)

            for pos in range(3):
                by_node(0, pos)
            by_slot(0, 0)
            with dve.Fori(0, PAIRED) as i:
                for pos in range(BODY):
                    rest_of(i, pos)
                    by_node(i, pos + 3)
                    by_slot(i, pos + 1)
                    if pos == 2:
                        sums(i, bass.ds(i * 2, 1), 1, -1)
                    if pos == LAST[0] + 3:
                        sums(i, bass.ds(i * 2 + 1, 1), 0, LAST[0])
            sums(PAIRED, slice(NT, NT + 1), 1, -1)
            dve.wait_ge(f_agg, 2 + (NT + 1) * (k + 1))
            dve.sem_inc(s_agg, 1)

        def linear_pool(pool, l):
            hold(pool, "pool", s_tab, l + 1)

            def own_slots(tile, u):
                for a in range(2):
                    o = pool.tensor_copy(curS2[:, u * NT:(u + 1) * NT, a, :], slots[:, a, tile, :].rearrange("p o c -> p c o").to_broadcast([128, NT, 2]))
                o.then_inc(l_own, 1)

            own_slots(slice(0, 1), 0)
            with pool.Fori(0, PAIRED) as i:
                hold(pool, "pool", l_from, group_done(i, l, -1, 2))
                own_slots(bass.ds(i * 2 + 1, 1), 1)
                hold(pool, "pool", l_from, group_done(i, l, LAST[0], 2))
                own_slots(bass.ds(i * 2 + 2, 1), 0)

        def linear_pe(pe, l):
            def count(i, pos):
                b = pos % BODY % RING
                pe.wait_ge(l_from, group_done(i, l, pos, 2))
                pe.wait_ge(l_Cc, before_it(i, l, pos, RING))
                for c in range(GROUP):
                    m = pe.matmul(psMsg[b][0:P, c * P:(c + 1) * P], oneE[:, b, c, 0, 0:P], oneE[:, b, c, 1, 0:P],
                                  start=True, stop=True, skip_group_check=True)
                m.then_inc(l_C, 1)

            def total(i, pos):
                pe.wait_ge(l_Cc, group_done(i, l, pos))
                for u in range(2):
                    if pos == FIRST[u]:
                        pe.wait_ge(l_agg, i * 2 + (l * (NT + 1) + u + 2))
                for c in range(GROUP):
                    u, t = cell(pos, c)
                    for p in range(PARTS):
                        m = pe.matmul(psA[u][0:P, 0:D], cells[:, pos % RING, c, 0:P], TAB[:, 0, t, p, :], start=t == 0 and p == 0,
                                      stop=t == NT - 1 and p == PARTS - 1, skip_group_check=True)
                m.then_inc(l_sum, 1)

            for pos in range(2):
                count(0, pos)
            with pe.Fori(0, PAIRED) as i:
                for pos in range(BODY):
                    count(i, pos + 2)
                    total(i, pos)

        def linear_act(act, l):
            with act.Fori(0, PAIRED) as i:
                for pos in range(BODY):
                    act.wait_ge(l_C, group_done(i, l, pos, 2))
                    act.wait_ge(l_sum, before_it(i, l, pos, RING))
                    act.copy(cells[:, pos % RING, :, 0:P], psMsg[pos % RING][0:P, 0:GROUP * P].rearrange("p (c d) -> p c d", d=P)
                             ).then_inc(l_Cc, 1)

        def counts_dve(dve, l):
            def onehots(i, pos):
                for u in range(2):
                    if pos == FIRST[u]:
                        dve.wait_ge(l_own, i * 2 + (l * (NT + 1) + u + 1))
                dve.wait_ge(l_C, before_it(i, l, pos, RING, 2))
                dve.tensor_tensor(pairs(oneE[:, pos % RING].rearrange("p c a n -> p (c a) n")), columns(col1, 126, 2 * GROUP),
                                  along(curS2[:, pos * GROUP:(pos + 1) * GROUP].rearrange("p c a e -> p (c a) e"), 126),
                                  ALU.is_equal).then_inc(l_from, 1)

            def sums(i, at, u, pos):
                hold(dve, "dve", l_sum, group_done(i, l, pos))
                dve.scalar_tensor_tensor(out=AGGs[:, at, 0:D], in0=Hs[:, at, :], scalar=selfs[0:P, at],
                                         in1=psA[u][0:P, 0:D].rearrange("p (o d) -> p o d", o=1), op0=ALU.mult, op1=ALU.add
                                         ).then_inc(l_agg, 1)

            with dve.Fori(0, PAIRED) as i:
                for pos in range(BODY):
                    onehots(i, pos)
                    if pos == 4:
                        sums(i, bass.ds(i * 2, 1), 1, -1)
                    if pos == LAST[0] + 5:
                        sums(i, bass.ds(i * 2 + 1, 1), 0, LAST[0])
            for pos in range(2):
                onehots(PAIRED, pos)
            sums(PAIRED, slice(NT, NT + 1), 1, -1)
            dve.wait_ge(l_agg, 2 + (NT + 1) * (l + 1))
            dve.sem_inc(s_agg, 1)

        def general_sp(sp, k):
            if k < L0:
                sp.wait_ge(s_tE, STAGE0[EDGE[k]] + NT)
            else:
                sp.wait_ge(s_tab, k - L0 + 1)
            sp.dma_start(srci, src.rearrange("(p t) -> p t", p=P)).then_inc(s_e, 16)
            sp.dma_start(dsti, dst.rearrange("(p t) -> p t", p=P)).then_inc(s_e, 16)
            sp.wait_ge(s_const, 1)
            if k:
                sp.wait_ge(g_back, 32 * k)
            for u in range(2):
                sp.dma_start(sums_dram[u][0:N, :].rearrange("(t p) d -> p t d", p=P),
                             zrow[:].rearrange("p (o d) -> p o d", o=1).to_broadcast([P, NT, W])
                             ).then_inc(g_zero, 16)
            tables = 2 if k < L0 else 1
            for n in range(tables):
                sp.dma_start(table_dram[n].rearrange("(t p) d -> p t d", p=P),
                             TAB[:, n].rearrange("p t c d -> p t (c d)")).then_inc(g_tab, 16)
            for u in range(2):
                sp.wait_ge(g_add[k][u], 16 * PAIRS + 16)
            for u, to in enumerate((AGG, AGG1)):
                sp.dma_start(to, sums_dram[u][0:N, :].rearrange("(t p) d -> p t d", p=P)).then_inc(g_back, 16)

        def stage_pool(pool, name, ready, value):
            base = STAGE0[name]
            hold(pool, "pool", ready, value)
            with pool.Fori(0, NT // 2) as i:
                for u in range(2):
                    hold(pool, "pool", s_tT, i * 2 + (base + u - 1))
                    copies = [pool.tensor_copy(tile_in[:, u, 0, :], H[:, bass.ds(i * 2 + u, 1), :])]
                    if name in AGG_STAGES:
                        copies.append(pool.tensor_copy(tile_in[:, u, 1, :], AGG[:, bass.ds(i * 2 + u, 1), 0:D]))
                    copies[-1].then_inc(s_in, 1)

        def general_pool(pool, k):
            hold(pool, "pool", s_e, 32 * (k + 1))
            pool.memset(msg[:, :, D:W], 1.0)
            hold(pool, "pool", g_tab, 16 * (2 * min(k + 1, L0) + max(k + 1 - L0, 0)))
            hold(pool, "pool", g_zero, 32 * (k + 1))
            for u in range(2):
                pool.dma_start(sums_dram[u][N:N + P, :], zrow[:]).then_inc(g_add[k][u], 16)
            tables = 2 if k < L0 else 1
            done = 2 * PAIRS * k + 2
            with pool.Fori(0, PAIRS) as i:
                hold(pool, "pool", g_msg, i * 2 + done)
                hold(pool, "pool", g_widx, i * 2 + done)
                for u in range(2):
                    pool.tensor_copy(sidx[:, u:u + 1], srci[:, bass.ds(i * 2 + u, 1)])
                    pool.tensor_copy(didx[:, u:u + 1], dsti[:, bass.ds(i * 2 + u, 1)]).then_inc(g_idx, 1)
                hold(pool, "pool", g_idx, i * 2 + done)
                for u in range(2):
                    for n in range(tables):
                        pool.indirect_dma_start(rows[:, u, n].rearrange("p c d -> p (c d)"), None, table_dram[n],
                                                bass.IndirectOffsetOnAxis(ap=(sidx, didx)[n][:, u:u + 1], axis=0)
                                                ).then_inc(g_rows[k][u], 16)
                for u in range(2):
                    hold(pool, "pool", g_cp, i * 2 + (u + 1 + done))
                    hold(pool, "pool", g_add[k][u], i * 16 + 16)
                    pool.indirect_dma_start(sums_dram[u], bass.IndirectOffsetOnAxis(ap=widx[:, u:u + 1], axis=0),
                                            msum[:, u, :], None, compute_op=ALU.add).then_inc(g_add[k][u], 16)

        def stage_pe(pe, name, products):
            base = STAGE0[name]
            with pe.Fori(0, NT // 2) as i:
                for u in range(2):
                    pe.wait_ge(s_in, i * 2 + (base + u + 1))
                    pe.wait_ge(s_tC, i * 2 + (base + u - 1))
                    t = pe.transpose(psT[u][:, 0:P], tile_in[:, u, 0, :], ident[0:P, 0:P])
                    if name in AGG_STAGES:
                        t = pe.transpose(psT[u][:, 128:128 + P], tile_in[:, u, 1, :], ident[0:P, 0:P])
                    t.then_inc(s_tT, 1)
                for u in range(2):
                    pe.wait_ge(s_tC, i * 2 + (base + u + 1))
                    pe.wait_ge(s_tE, i * 2 + (base + u - 1))
                    for n, (which, rhs, at, stop) in enumerate(products):
                        start = n == 0 or products[n - 1][3]
                        m = pe.matmul(psO[u][0:P, at:at + rhs.shape[1]], hT[:, u, which, 0:P], rhs, start=start, stop=stop)
                    m.then_inc(s_tO, 1)

        def general_pe(pe, k):
            done = 2 * PAIRS * k + 2
            with pe.Fori(0, PAIRS) as i:
                for u in range(2):
                    pe.wait_ge(g_drep, i * 2 + (u - 1 + done))
                    pe.wait_ge(g_same, i * 2 + done)
                    pe.transpose(psD[u][0:P, 0:P], drep[:, u, :], ident[0:P, 0:P]).then_inc(g_dT, 1)
                for u in range(2):
                    pe.wait_ge(g_same, i * 2 + (u + 1 + done))
                    pe.wait_ge(g_msg, i * 2 + (u + 1 + done))
                    pe.wait_ge(g_cp, i * 2 + done)
                    pe.matmul(psM[u][0:P, 0:W], same[:, u, :], msg[:, u, :], start=True, stop=True).then_inc(g_sum, 1)

        def norm_act(act, n):
            act.wait_ge(s_var, n + 1)
            act.activation(std[:], var[:], ACT.Sqrt, bias=eps[:]).then_inc(s_std, 1)

        def stage_act(act, name, split=None):
            base = STAGE0[name]
            with act.Fori(0, NT // 2) as i:
                for u in range(2):
                    act.wait_ge(s_tT, i * 2 + (base + u + 1))
                    act.wait_ge(s_tO, i * 2 + (base + u - 1))
                    n = 2 if name in AGG_STAGES else 1
                    act.copy(hT[:, u, 0:n, 0:P], psT[u][:, 0:n * 128].rearrange("k (n p) -> k n p", n=n)[:, :, 0:P]
                             ).then_inc(s_tC, 1)
                if split is not None:
                    for u in range(2):
                        hold(act, "act", s_raw, i * 2 + (u + 1 + split * NT))
                        act.copy(TAB[:, :, bass.ds(i * 2 + u, 1), 0, :], raw[:, u].rearrange("p n (o d) -> p n o d", o=1)).then_inc(s_hi, 1)
                    for u in range(2):
                        hold(act, "act", s_rest, i * 2 + (u + 1 + split * NT))
                        act.copy(TAB[:, :, bass.ds(i * 2 + u, 1), 1, :], rest[:, u].rearrange("p n (o d) -> p n o d", o=1)).then_inc(s_mid, 1)

        def general_act(act, k):
            done = 2 * PAIRS * k + 2
            with act.Fori(0, PAIRS) as i:
                for u in range(2):
                    act.wait_ge(g_sum, i * 2 + (u + 1 + done))
                    act.wait_ge(g_add[k][u], i * 16 + 16)
                    act.copy(msum[:, u, :], psM[u][0:P, 0:W]).then_inc(g_cp, 1)

        def norm_dve(dve, step, n, source, l=None):
            even, odd = stats[:, :, 0:3], stats[:, :, 3:6]
            step.last()
            a = step.did(dve.tensor_tensor(mean[:], even[:, :, 1], odd[:, :, 1], ALU.add))
            b = step.did(dve.tensor_tensor(sq[:], even[:, :, 1], odd[:, :, 1], ALU.subtract))
            c = step.did(dve.tensor_tensor(var[:], even[:, :, 2], odd[:, :, 2], ALU.add))
            step.after(c)
            d = step.did(dve.tensor_scalar(mean[:], mean[:], 0.5, None, ALU.mult))
            e = step.did(dve.tensor_tensor(sq[:], sq[:], sq[:], ALU.mult))
            f = step.did(dve.tensor_scalar(var[:], var[:], 1.0 / D, None, ALU.mult))
            step.after(f)
            dve.scalar_tensor_tensor(out=var[:], in0=sq[:], scalar=0.25, in1=var[:], op0=ALU.mult, op1=ALU.add
                                     ).then_inc(s_var, 1)
            per_tile = [P, NT, D]
            step.did(dve.tensor_tensor(H, source, mean[:].rearrange("p (t o) -> p t o", o=1).to_broadcast(per_tile), ALU.subtract))
            dve.wait_ge(s_std, n + 1)
            step.did(dve.reciprocal(rstd[:], std[:]))
            step.last()
            step.did(dve.tensor_tensor(H, H, rstd[:].rearrange("p (t o) -> p t o", o=1).to_broadcast(per_tile), ALU.mult))
            if l is not None:
                step.last()
                step.did(dve.tensor_tensor(H, H, bias[:, LN_G + l:LN_G + l + 1, :].to_broadcast(per_tile), ALU.mult))
                step.last()
                dve.tensor_tensor(H, H, bias[:, LN_B + l:LN_B + l + 1, :].to_broadcast(per_tile), ALU.add).then_inc(s_h, 1)

        def split_dve(dve, l):
            base, done = STAGE0[f"ab{l}"], l * NT
            dve.tensor_copy(AGG[:, :, D], selfs[0:P, 1:NT + 1])
            with dve.Fori(0, NT // 2) as i:
                for u in range(2):
                    dve.wait_ge(s_tO, i * 2 + (base + u + 1))
                    dve.tensor_tensor(raw[:, u], psO[u][0:P, 0:2 * D].rearrange("p (n d) -> p n d", n=2), abias[:, l], ALU.add
                                      ).then_inc(s_raw, 1)
                for u in range(2):
                    hold(dve, "dve", s_hi, i * 2 + (done + u + 1))
                    dve.tensor_tensor(tmp[:, u, 0, :], raw[:, u, 0, :], raw[:, u, 1, :], ALU.add)
                    dve.tensor_tensor(rest[:, u].rearrange("p n (o d) -> p n o d", o=1), raw[:, u].rearrange("p n (o d) -> p n o d", o=1),
                                      TAB[:, :, bass.ds(i * 2 + u, 1), 0, :], ALU.subtract).then_inc(s_rest, 1)
                for u in range(2):
                    hold(dve, "dve", s_rest, i * 2 + (done + u + 1))
                    hold(dve, "dve", s_mid, i * 2 + (done + u + 1))
                    dve.tensor_scalar(AGG[:, bass.ds(i * 2 + u, 1), 0:D], tmp[:, u, 0:1, :], 0.0, selfs[0:P, bass.ds(i * 2 + (u + 1), 1)],
                                      ALU.max, ALU.mult)
                    dve.tensor_tensor(TAB[:, :, bass.ds(i * 2 + u, 1), 2, :], rest[:, u].rearrange("p n (o d) -> p n o d", o=1),
                                      TAB[:, :, bass.ds(i * 2 + u, 1), 1, :], ALU.subtract).then_inc(s_tE, 1)

        def update_dve(dve, step, l):
            base = STAGE0[f"upd{l}"]
            with dve.Fori(0, NT // 2) as i:
                step.enter(i, 8)
                now = [0, 0]
                tile = [H[:, bass.ds(i * 2 + u, 1), :] for u in range(2)]
                for u in range(2):
                    hold(dve, "dve", s_tO, i * 2 + (base + u + 1))
                    now[u] = step.did(dve.scalar_tensor_tensor(
                        out=tmp[:, u, 0, :], in0=b2upd[:, l, :], scalar=degc[:, bass.ds(i * 2 + u, 1)],
                        in1=psO[u][0:P, 0:D], op0=ALU.mult, op1=ALU.add))
                for u in range(2):
                    dve.wait_ge(s_dve, now[u])
                    now[u] = step.did(dve.tensor_tensor(tmp[:, u, 1, :], tmp[:, u, 0, :], bias[:, B_UPD + l, :], ALU.add))
                for u in range(2):
                    hold(dve, "dve", s_dve, now[u])
                    now[u] = step.did(dve.tensor_tensor(tile[u], tmp[:, u, 1:2, :], tile[u], ALU.add))
                for u in range(2):
                    hold(dve, "dve", s_dve, now[u])
                    step.did(dve.bn_stats(stats[:, bass.ds(i * 2 + u, 1), :], tile[u]))
                    dve.sem_inc(s_tE, 1)
                step.leave(NT // 2)

        def linear_dve(dve, step, l):
            base = STAGE0[f"lin{l}"]
            with dve.Fori(0, NT // 2) as i:
                step.enter(i, 6 if l < L1 - 1 else 8)
                now = [0, 0]
                for u in range(2):
                    hold(dve, "dve", s_tO, i * 2 + (base + u + 1))
                    now[u] = step.did(dve.tensor_scalar(tmp[:, u, 0, :], psO[u][0:P, 0:D], invdeg[:, bass.ds(i * 2 + u, 1)], None, ALU.mult))
                for u in range(2):
                    dve.wait_ge(s_dve, now[u])
                    now[u] = step.did(dve.tensor_tensor(tmp[:, u, 1, :], tmp[:, u, 0, :], psO[u][0:P, D:2 * D], ALU.add))
                for u in range(2):
                    hold(dve, "dve", s_dve, now[u])
                    dve.sem_inc(s_tE, 1)
                    to = H[:, bass.ds(i * 2 + u, 1), :] if l < L1 - 1 else raw[:, u, 0:1, :]
                    now[u] = step.did(dve.tensor_tensor(to, tmp[:, u, 1:2, :], bias[:, B_LIN + l:B_LIN + l + 1, :], ALU.add))
                if l == L1 - 1:
                    for u in range(2):
                        hold(dve, "dve", s_dve, now[u])
                        tile = X[:, bass.ds(i * 2 + u, 1), :]
                        step.did(dve.tensor_tensor(tile, tile, raw[:, u, 0:1, :], ALU.add))
                step.leave(NT // 2)
            step.last()
            if l < L1 - 1:
                dve.tensor_scalar(H, H, 0.0, None, ALU.max).then_inc(s_h, 1)
            else:
                dve.sem_inc(s_fin, 1)

        def general_dve(dve, step, k):
            tables = 2 if k < L0 else 1
            done = 2 * PAIRS * k + 2
            with dve.Fori(0, PAIRS) as i:
                step.enter(i, 2 * (4 + (3 if k < L0 else 1)))
                now = [0, 0]
                for u in range(2):
                    dve.wait_ge(g_idx, i * 2 + (u - 1 + done))
                    dve.wait_ge(g_sum, i * 2 + done)
                    now[u] = step.did(dve.tensor_copy(dcol[:, u:u + 1], didx[:, u:u + 1]))
                for u in range(2):
                    dve.wait_ge(g_dve, now[u])
                    dve.tensor_scalar(drep[:, u, :], ones[0:P, 0:P], dcol[:, u:u + 1], None, ALU.mult).then_inc(g_drep, 1)
                for u in range(2):
                    dve.wait_ge(g_dT, i * 2 + (u - 1 + done))
                    dve.tensor_scalar(same[:, u, :], psD[u][0:P, 0:P], dcol[:, u:u + 1], None, ALU.is_equal).then_inc(g_same, 1)
                for u in range(2):
                    dve.wait_ge(g_same, i * 2 + (u + 1 + done))
                    now[u] = step.did(dve.tensor_tensor_reduce(earlier[:, u, :], same[:, u, :], before[:], 1.0, 0.0,
                                                               ALU.mult, ALU.add, nearl[:, u:u + 1]))
                for u in range(2):
                    dve.wait_ge(g_dve, now[u])
                    step.did(dve.tensor_scalar(wsel[:, u, 0:1], nearl[:, u:u + 1], 0.0, None, ALU.is_gt))
                    now[u] = step.did(dve.tensor_tensor(wsel[:, u, 1:2], junk[:], dcol[:, u:u + 1], ALU.subtract))
                for u in range(2):
                    dve.wait_ge(g_dve, now[u])
                    dve.wait_ge(g_add[k][u], i * 16 + 16)
                    dve.scalar_tensor_tensor(out=widx[:, u:u + 1], in0=wsel[:, u, 1:2], scalar=wsel[:, u, 0:1],
                                             in1=dcol[:, u:u + 1], op0=ALU.mult, op1=ALU.add).then_inc(g_widx, 1)
                for u in range(2):
                    dve.wait_ge(g_rows[k][u], i * (16 * tables) + 16 * tables)
                    r = rows[:, u, 0:tables]
                    now[u] = step.did(dve.tensor_tensor(part[:, u, 0:tables, :], r[:, :, 0, :], r[:, :, 1, :], ALU.add))
                for u in range(2):
                    dve.wait_ge(g_dve, now[u])
                    r = rows[:, u, 0:tables]
                    if k >= L0:
                        dve.tensor_tensor(msg[:, u, 0:D], part[:, u, 0, :], r[:, 0, 2, :], ALU.add).then_inc(g_msg, 1)
                    else:
                        now[u] = step.did(dve.tensor_tensor(part[:, u], part[:, u], r[:, :, 2, :], ALU.add))
                if k < L0:
                    for u in range(2):
                        dve.wait_ge(g_dve, now[u])
                        now[u] = step.did(dve.tensor_tensor(part[:, u, 0, :], part[:, u, 0, :], part[:, u, 1, :], ALU.add))
                    for u in range(2):
                        dve.wait_ge(g_dve, now[u])
                        dve.tensor_scalar(msg[:, u, 0:D], part[:, u, 0, :], 0.0, None, ALU.max).then_inc(g_msg, 1)
                step.leave(PAIRS)
            dve.wait_ge(g_back, 32 * (k + 1))
            dve.tensor_tensor(AGG[:], AGG, AGG1, ALU.add).then_inc(s_agg, 1)

        block = ctx.enter_context(nc.Block())

        @block.sync
        def _(sp):
            sp.dma_start(X, x.rearrange("(t p) d -> p t d", p=P)).then_inc(s_x, 16)
            loads = [(wnat[:, ENC, :], W_enc), (wnat[:, OUT, :], W_out)]
            for l in range(L0):
                loads += [(wnat[:, MSG + 2 * l, :], msg_W1[l, :, 0:D]),
                          (wnat[:, MSG + 2 * l + 1, :], msg_W1[l, :, D:2 * D]),
                          (wnat[:, UPD_H + l, :], upd_W[l, :, 0:D]),
                          (wnat[:, UPD_M + l, :], upd_W[l, :, D:2 * D]),
                          (wnat[:, NW + l, :], msg_W2[l]),
                          (b2col[:, l:l + 1], msg_b2[l].rearrange("(d o) -> d o", o=1))]
            for l in range(L1):
                loads += [(wnat[:, LIN_L + l, :], Wl[l]), (wnat[:, LIN_R + l, :], Wr[l])]
            rows_of = [b_enc] + [v[l] for v in (msg_b1, upd_b, ln_g, ln_b) for l in range(L0)] \
                + [b_out] + [bl[l] for l in range(L1)]
            for k, b in enumerate(rows_of):
                loads.append((bias[:, k, :], b.rearrange("(o d) -> o d", o=1).to_broadcast([P, D])))
            assert len(loads) == LOADS
            for to, fr in loads:
                sp.dma_start(to, fr).then_inc(s_w, 16)
            sort_sp(sp)
            miss = load_flag(sp)
            for k in range(L0):
                edge_sp(sp, k, miss)
            sp.wait_ge(s_agg, L0)
            sp.dma_start(X, x.rearrange("(t p) d -> p t d", p=P)).then_inc(s_x, 16)
            for k in range(L0, L0 + L1):
                edge_sp(sp, k, miss)
            sp.wait_ge(s_fin, 1)
            sp.dma_start(out.rearrange("(t p) d -> p t d", p=P), X).then_inc(s_out, 16)
            sp.wait_ge(s_out, 16)

        @block.gpsimd
        def _(pool):
            pool.memset(ones[:], 1.0).then_inc(s_pset, 1)
            pool.memset(ident[:], 0.0).then_inc(s_pset, 1)
            pool.memset(zrow[:], 0.0).then_inc(s_pset, 1)
            pool.memset(eps[:], EPS).then_inc(s_pset, 1)
            pool.memset(abias[:], 0.0).then_inc(s_pset, 1)
            pool.iota(junki, pattern=[[0, 1]], base=N, channel_multiplier=1).then_inc(s_pset, 1)
            pool.iota(counti, pattern=[[1, 128]], base=0, channel_multiplier=0).then_inc(s_pset, 1)
            pool.iota(rowi, pattern=[[0, 1]], base=1, channel_multiplier=1).then_inc(s_pset, 1)
            pool.iota(tilei[:, 0, :], pattern=[[P, NT + 2]], base=0, channel_multiplier=0).then_inc(s_pset, 1)
            pool.iota(tilei[:, 1, :], pattern=[[P, NT + 2]], base=-1, channel_multiplier=0).then_inc(s_pset, 1)
            pool.memset(ones_bf[:], 1.0).then_inc(s_pset, 1)
            pool.wait_ge(s_pset, 11)
            pool.tensor_scalar(col1[:], counti, 1.0, None, ALU.add).then_inc(s_pset, 1)
            pool.tensor_copy(row1[:], rowi).then_inc(s_pset, 1)
            pool.tensor_copy(tilec[:], tilei).then_inc(s_pset, 1)
            pool.affine_select(out=below_bf[:], in_=ones_bf[:], compare_op=ALU.is_gt, fill=0.0, base=0,
                               pattern=[[1, 128]], channel_multiplier=-1).then_inc(s_pset, 1)
            pool.tensor_copy(junk[:], junki).then_inc(s_pset, 1)
            pool.affine_select(out=ident[:], in_=ident[:], compare_op=ALU.not_equal, fill=1.0, base=0,
                               pattern=[[-1, 128]], channel_multiplier=1).then_inc(s_pset, 1)
            pool.affine_select(out=before[:], in_=ones[0:P, 0:P], compare_op=ALU.is_gt, fill=0.0, base=0,
                               pattern=[[-1, P]], channel_multiplier=1).then_inc(s_pset, 1)
            pool.wait_ge(s_pset, 18)
            pool.tensor_copy(ident_bf[:], ident[:]).then_inc(s_pset, 1)
            pool.wait_ge(s_pset, 19)
            pool.sem_inc(s_const, 1)
            for empty in (s_in, s_tT, s_tC, s_tO, s_tE, g_msg, g_widx, g_same, g_cp, g_sum,
                          o_read, o_tot, o_totc, o_rank, o_prod, o_pay, o_mul, o_mulv, o_slot, o_perm, o_S, o_turn, o_ST, o_cell, f_agg, l_agg):
                pool.sem_inc(empty, 2)
            for empty in (f_toN, f_toE, f_gat, f_hi, f_rest, f_mid, f_lo, f_sca, l_from, l_C, l_Cc, l_sum):
                pool.sem_inc(empty, BODY)
            for stored in o_store:
                pool.sem_inc(stored, 32)
            pool.memset(slots[:, :, NT, :], 0.0)
            pool.memset(selfs[:, 0:1], 0.0)
            sort_pool(pool)
            miss = load_flag(pool)
            stage_pool(pool, "enc", s_h, 1)
            for l in range(L0):
                if l == 0:
                    stage_pool(pool, "ab0", s_tE, STAGE0["enc"] + NT)
                else:
                    stage_pool(pool, f"ab{l}", s_h, l + 1)
                edge_pool(pool, l, miss)
                stage_pool(pool, f"upd{l}", s_agg, l + 1)
            stage_pool(pool, "out", s_h, L0 + 1)
            for l in range(L1):
                edge_pool(pool, L0 + l, miss)
                stage_pool(pool, f"lin{l}", s_agg, L0 + l + 1)

        @block.tensor
        def _(pe):
            pe.wait_ge(s_w, 16 * LOADS)
            pe.wait_ge(s_const, 1)
            for w in range(NW):
                if w >= 2:
                    pe.wait_ge(s_wTc, w - 1)
                pe.transpose(psT[w % 2][:, 0:D], wnat[:, w, :], ident[:]).then_inc(s_wT, 1)
            pe.wait_ge(s_wTc, NW)
            pe.wait_ge(s_b2, L0)
            for l in range(L0):
                pe.matmul(psO[l][:, 0:D], wnat[:, NW + l, :], wT[:, UPD_M + l, :], start=True, stop=True)
                pe.matmul(psO[l][0:P, D:2 * D], b2rep[:, l, :], wT[:, UPD_M + l, :], start=True, stop=True
                          ).then_inc(s_comp, 1)
            pe.wait_ge(s_compc, 2 * L0)
            sort_pe(pe)
            miss = load_flag(pe)
            stage_pe(pe, "enc", [(0, wT[:, ENC, :], 0, True)])
            for l in range(L0):
                stage_pe(pe, f"ab{l}", [(0, wT[:, MSG + 2 * l:MSG + 2 * l + 2, :].rearrange("k w d -> k (w d)"), 0, True)])
                edge_pe(pe, l, miss)
                stage_pe(pe, f"upd{l}", [(0, wT[:, UPD_H + l, :], 0, False), (1, wM[:, l, :], 0, True)])
            stage_pe(pe, "out", [(0, wT[:, OUT, :], 0, True)])
            for l in range(L1):
                edge_pe(pe, L0 + l, miss)
                stage_pe(pe, f"lin{l}", [(0, wT[:, LIN_R + l, :], D, True), (1, wT[:, LIN_L + l, :], 0, True)])

        @block.scalar
        def _(act):
            for w in range(NW):
                act.wait_ge(s_wT, w + 1)
                act.copy(wT[:, w, :], psT[w % 2][:, 0:D]).then_inc(s_wTc, 1)
            for l in range(L0):
                act.wait_ge(s_comp, l + 1)
                act.copy(wM[:, l, :], psO[l][:, 0:D]).then_inc(s_compc, 1)
                act.copy(b2upd[:, l, :], psO[l][0:P, D:2 * D]).then_inc(s_compc, 1)
            sort_act(act)
            miss = load_flag(act)
            norm_act(act, 0)
            stage_act(act, "enc")
            for l in range(L0):
                stage_act(act, f"ab{l}", split=l)
                edge_act(act, l, miss)
                stage_act(act, f"upd{l}")
                norm_act(act, l + 1)
            stage_act(act, "out")
            norm_act(act, L0 + 1)
            for l in range(L1):
                act.wait_ge(s_h, L0 + 2 + l)
                act.copy(TAB[:, 0, :, 0, :], H).then_inc(s_hi, 1)
                act.wait_ge(s_rest, 2 * NT + l + 1)
                act.copy(TAB[:, 0, :, 1, :], AGG[:, :, 0:D]).then_inc(s_mid, 1)
                edge_act(act, L0 + l, miss)
                stage_act(act, f"lin{l}")

        @block.vector
        def _(dve):
            step = Steps(dve, s_dve)
            gstep = Steps(dve, g_dve)
            dve.wait_ge(s_const, 1)
            dve.wait_ge(s_w, 16 * LOADS)
            for l in range(L0):
                dve.tensor_scalar(b2rep[:, l, :], ones[:, 0:P], b2col[:, l:l + 1], None, ALU.mult).then_inc(s_b2, 1)
                step.did(dve.tensor_copy(abias[:, l, 1, :], bias[:, B_1 + l, :]))
            sort_dve(dve)
            miss = load_flag(dve)
            dve.memset(Hs[:, 0, :], 0.0)
            dve.memset(AGGs[:, 0, :], 0.0)
            dve.wait_ge(s_x, 16)
            with dve.Fori(0, NT // 2) as i:
                step.enter(i, 2)
                for u in range(2):
                    step.did(dve.bn_stats(stats[:, bass.ds(i * 2 + u, 1), :], X[:, bass.ds(i * 2 + u, 1), :]))
                step.leave(NT // 2)
            norm_dve(dve, step, 0, X)
            step.last()
            dve.tensor_scalar(H, H, 0.0, None, ALU.max).then_inc(s_h, 1)
            with dve.Fori(0, NT // 2) as i:
                for u in range(2):
                    hold(dve, "dve", s_tO, i * 2 + (STAGE0["enc"] + u + 1))
                    dve.tensor_tensor(H[:, bass.ds(i * 2 + u, 1), :], psO[u][0:P, 0:D].rearrange("p (o d) -> p o d", o=1),
                                      bias[:, B_ENC:B_ENC + 1, :], ALU.add).then_inc(s_tE, 1)
            for l in range(L0):
                split_dve(dve, l)
                edge_dve(dve, gstep, l, miss)
                if l == 0:
                    dve.wait_ge(s_agg, 1)
                    step.did(dve.tensor_copy(degc[:], AGG[:, :, D]))
                    step.last()
                    step.did(dve.tensor_scalar(sq[:], degc[:], 1.0, None, ALU.max))
                    step.last()
                    step.did(dve.reciprocal(invdeg[:], sq[:]))
                update_dve(dve, step, l)
                norm_dve(dve, step, l + 1, H, l)
            dve.wait_ge(s_x, 32)
            with dve.Fori(0, NT // 2) as i:
                step.enter(i, 6)
                now = [0, 0]
                tile = [X[:, bass.ds(i * 2 + u, 1), :] for u in range(2)]
                for u in range(2):
                    hold(dve, "dve", s_tO, i * 2 + (STAGE0["out"] + u + 1))
                    now[u] = step.did(dve.tensor_tensor(tmp[:, u, 0, :], psO[u][0:P, 0:D], bias[:, B_OUT, :], ALU.add))
                for u in range(2):
                    hold(dve, "dve", s_dve, now[u])
                    now[u] = step.did(dve.tensor_tensor(tile[u], tmp[:, u, 0:1, :], tile[u], ALU.add))
                for u in range(2):
                    hold(dve, "dve", s_dve, now[u])
                    step.did(dve.bn_stats(stats[:, bass.ds(i * 2 + u, 1), :], tile[u]))
                    dve.sem_inc(s_tE, 1)
                step.leave(NT // 2)
            norm_dve(dve, step, L0 + 1, X)
            step.last()
            dve.tensor_scalar(H, H, 0.0, None, ALU.max).then_inc(s_h, 1)
            for l in range(L1):
                dve.wait_ge(s_h, L0 + 2 + l)
                dve.wait_ge(s_hi, 2 * NT + l + 1)
                dve.tensor_tensor(AGG[:, :, 0:D], H, TAB[:, 0, :, 0, :], ALU.subtract).then_inc(s_rest, 1)
                dve.wait_ge(s_rest, 2 * NT + l + 1)
                dve.wait_ge(s_mid, 2 * NT + l + 1)
                dve.tensor_tensor(TAB[:, 0, :, 2, :], AGG[:, :, 0:D], TAB[:, 0, :, 1, :], ALU.subtract).then_inc(s_tab, 1)
                dve.wait_ge(s_tab, l + 1)
                edge_dve(dve, gstep, L0 + l, miss)
                linear_dve(dve, step, l)


_INS = ["x", "src", "dst", "L0_gnn_W_enc", "L0_gnn_b_enc", "L0_gnn_msg_W1", "L0_gnn_msg_b1", "L0_gnn_msg_W2",
        "L0_gnn_msg_b2", "L0_gnn_upd_W", "L0_gnn_upd_b", "L0_gnn_ln_g", "L0_gnn_ln_b", "L0_gnn_W_out",
        "L0_gnn_b_out", "L1_gnn_Wl", "L1_gnn_bl", "L1_gnn_Wr"]


def kernel(**inputs):
    import numpy as np
    import concourse.bacc as bacc
    from concourse.bass_utils import run_bass_kernel_spmd as run

    nc = bacc.Bacc("TRN2", target_bir_lowering=False, num_devices=1)
    arrays, args = {}, []
    for name in _INS:
        a = np.ascontiguousarray(inputs[name])
        arrays[f"in_{name}"] = a
        args.append(nc.dram_tensor(f"in_{name}", a.shape, mybir.dt.from_np(a.dtype), kind="ExternalInput").ap())
    args.append(nc.dram_tensor("out_0", (N, D), F32, kind="ExternalOutput").ap())
    build(nc, *args)
    return run(nc, [arrays], core_ids=[0]).results[0]["out_0"]
```

```python
from contextlib import ExitStack

import concourse.bass as bass
from concourse import mybir

F32 = mybir.dt.float32
BF16 = mybir.dt.bfloat16
I32 = mybir.dt.int32
ALU = mybir.AluOpType
ACT = mybir.ActivationFunctionType
AX = mybir.AxisListType.X

N = 6250
E = 206250
D = 128
P = 125
NT = N // P
ET = E // P
PAIRS = ET // 2
L0 = 2
L1 = 3
EPS = 1e-5
PARTS = 3
ROW = PARTS * D
W = D + 1

CELL = 128
GROUP = 4
PAIRED = NT // 2
BODY = 2 * NT // GROUP
FIRST = [0, NT // GROUP]
LAST = [(NT - 1) // GROUP, BODY - 1]
RING = 5
CHUNKS = [(0, 3)] + [(g, 2) for g in range(3, BODY, 2)]
OWN = [0, 5]
PAY = 2 * NT + 2
SAMPLE = 33
COLS = 36
WIN = 128 * COLS
RG = 4
RK = COLS // RG
FOLD = NT // 4 * 2
MAGIC = 1.5 * 2.0 ** 23

assert RG * RK == COLS and ET % SAMPLE == 0 and sum(n for _, n in CHUNKS) == BODY and len(CHUNKS) % 2 == 0 and BODY % RING == 0

assert NT * P == N and ET * P == E and NT % 2 == 0 and ET % 2 == 0

ENC, MSG, UPD_H, UPD_M, OUT, LIN_L, LIN_R = 0, 1, 5, 7, 9, 10, 13
NW = 16
B_ENC, B_1, B_UPD, LN_G, LN_B, B_OUT, B_LIN = 0, 1, 3, 5, 7, 9, 10
NB = 13
LOADS = NW + 2 * L0 + NB
STAGES = ["enc", "ab0", "upd0", "ab1", "upd1", "out", "lin0", "lin1", "lin2"]
PB = 5
STAGE0 = {name: PB + NT * k for k, name in enumerate(STAGES)}
SPLITS = ["ab0", "ab1"]
EDGE = ["ab0", "ab1", "lin0", "lin1", "lin2"]
AGG_STAGES = ["upd0", "upd1", "lin0", "lin1", "lin2"]
TB = 10
NB_LOOPS = NT // TB
assert NB_LOOPS * TB == NT and TB % 2 == 0 and TB % PB == 0


class Steps:

    def __init__(self, eng, sem):
        self.eng, self.sem, self.base, self.k, self.i, self.per = eng, sem, 0, 0, None, 0

    def now(self):
        return self.base + self.k if self.i is None else self.i * self.per + (self.base + self.k)

    def did(self, ins):
        ins.then_inc(self.sem, 1)
        self.k += 1
        return self.now()

    def after(self, value):
        self.eng.wait_ge(self.sem, value)

    def last(self):
        self.after(self.now())

    def enter(self, i, per):
        self.base, self.k, self.i, self.per = self.base + self.k, 0, i, per

    def leave(self, times):
        assert self.k == self.per, (self.k, self.per)
        self.base, self.k, self.i = self.base + times * self.per, 0, None


def build(nc, x, src, dst, W_enc, b_enc, msg_W1, msg_b1, msg_W2, msg_b2, upd_W, upd_b, ln_g, ln_b,
          W_out, b_out, Wl, bl, Wr, out):
    with ExitStack() as ctx:
        def sb(name, shape, dt=F32):
            return ctx.enter_context(nc.sbuf_tensor(name, shape, dt))

        def sem(name):
            return ctx.enter_context(nc.semaphore(name))

        table_dram = [nc.dram_tensor(f"table_{n}", [N, ROW], BF16, kind="Internal").ap() for n in "ab"]
        sums_dram = [nc.dram_tensor(f"sums_{u}", [N + P, W], F32, kind="Internal").ap() for u in range(2)]

        slots_dram = nc.dram_tensor("slots_turned", [PAIRED, 2, 2 * NT, CELL], BF16, kind="Internal").ap()

        Hf = sb("Hf", [128, (NT + 1) * D])
        Hs = Hf[0:P, :].rearrange("p (t d) -> p t d", d=D)
        H = Hs[:, 1:NT + 1, :]
        AGGf = sb("AGGf", [128, (NT + 1) * W])
        AGGs = AGGf[0:P, :].rearrange("p (t d) -> p t d", d=W)
        AGG = AGGs[:, 1:NT + 1, :]
        selfs = sb("selfs", [128, NT + 1])
        half = NT * ROW // 2
        tabf = sb("tabf", [128, 2 * half])
        TAB = tabf[0:P, :].bitcast(BF16).rearrange("p (n t c d) -> p n t c d", n=2, t=NT, c=PARTS)
        wnat = tabf[:, 0:(NW + L0) * D].rearrange("p (w d) -> p w d", d=D)
        AGG1 = tabf[0:P, 0:NT * W].rearrange("p (t d) -> p t d", d=W)
        X = tabf[0:P, half:half + NT * D].rearrange("p (t d) -> p t d", d=D)
        wT = sb("wT", [D, NW, D])
        wM = sb("wM", [D, L0, D])
        bias = sb("bias", [P, NB, D])
        b2col = sb("b2col", [D, L0])
        b2upd = sb("b2upd", [P, L0, D])
        abias = sb("abias", [P, L0, 2, D])
        ident = sb("ident", [128, 128])
        before = sb("before", [P, P])
        ones = sb("ones", [128, 128])
        eps = sb("eps", [P, 1])
        stats = sb("stats", [P, NT, 6])
        mean = sb("mean", [P, NT])
        var = sb("var", [P, NT])
        std = sb("std", [P, NT])
        rstd = sb("rstd", [P, NT])
        sq = sb("sq", [P, NT])
        degc = sb("degc", [P, NT])
        invdeg = sb("invdeg", [P, NT])
        ones_bf = sb("ones_bf", [128, 128], BF16)
        ident_bf = sb("ident_bf", [128, 128], BF16)
        below_bf = sb("below_bf", [128, 128], BF16)
        col1 = sb("col1", [128, 128], BF16)
        row1 = sb("row1", [128, 1])
        tilec = sb("tilec", [128, 2, NT + 2])
        junk = sb("junk", [P, 1])
        zrow = sb("zrow", [P, W])
        slots = sb("slots", [128, 2, NT + 1, NT], BF16)
        lo = sb("lo", [1, NT + 2])
        loi = sb("loi", [1, NT + 2], I32)
        placed = sb("placed", [128, 2])
        missing = sb("missing", [1, 2])
        missingi = sb("missingi", [1, 1], I32)

        arena_words = 11790
        arena = sb("arena", [128, arena_words])

        def carver(memory, words):
            at = [0]

            def carve(shape, dt=F32):
                n = 1
                for k in shape[1:]:
                    n *= k
                size = (n + 1) // 2 if dt == BF16 else n
                a = memory[0:shape[0], at[0]:at[0] + size]
                at[0] += size
                assert at[0] <= words, (at[0], words)
                if dt != F32:
                    a = a.bitcast(dt)[:, 0:n]
                dims = " ".join(f"d{k}" for k in range(1, len(shape)))
                return a.rearrange(f"p ({dims}) -> p {dims}", **{f"d{k}": shape[k] for k in range(1, len(shape))})
            return carve

        carve = carver(arena, arena_words)
        tile_in = carve([P, PB, 2, D])
        hT = carve([128, 2, 2, 128])
        raw = carve([P, PB, 2, D])
        rest = carve([P, PB, 2, D])
        tmp = carve([P, PB, 2, D])
        carve = carver(arena, arena_words)
        srci = carve([P, ET], I32)
        dsti = carve([P, ET], I32)
        sidx = carve([P, 2], I32)
        didx = carve([P, 2], I32)
        widx = carve([P, 2], I32)
        dcol = carve([P, 2])
        drep = carve([P, 2, P])
        same = carve([P, 2, P])
        earlier = carve([P, 2, P])
        nearl = carve([P, 2])
        wsel = carve([P, 2, 2])
        rows = carve([P, 2, 2, PARTS, D], BF16)
        part = carve([P, 2, 2, D])
        msum = carve([P, 2, W])
        msg = carve([P, 2, W])
        carve = carver(arena, arena_words)
        slist = [carve([P, 2, n * GROUP * CELL], BF16) for _, n in (CHUNKS[0], CHUNKS[1])]
        toN = carve([P, RING, 2, GROUP * CELL], BF16)
        toE = carve([128, RING, GROUP, 126], BF16)
        mparts = carve([128, RING, GROUP, ROW + 2], BF16)
        mrest = carve([128, 2, GROUP, D])
        cur = carve([P, 2, ROW], BF16)
        curS = carve([128, 2 * NT, 2], BF16)
        carve = carver(arena, arena_words)
        oneE = carve([128, RING, GROUP, 2, 126], BF16)
        cells = carve([P, RING, GROUP, 126], BF16)
        curS2 = carve([128, 2 * NT, 2, 2], BF16)
        carve = carver(Hf, NT * D)
        one_cell = carve([128, 2, COLS, NT], BF16)
        payload = carve([128, 2, COLS, PAY], BF16)
        carve = carver(AGGf, NT * W)
        one_slot = carve([128, COLS, CELL], BF16)
        ranks_bf = carve([128, 2, RG, RK * NT], BF16)
        prod = carve([128, COLS, NT], BF16)
        carve = carver(Hf, NT * D)
        dstl = carve([P, ET], I32)
        samp = carve([P, NT])
        less = carve([P, NT + 1, NT])
        nless = carve([P, NT + 1])
        carve = carver(arena, arena_words)
        win = carve([128, 2, 2, COLS], I32)
        node = carve([128, 2, 2, COLS])
        off1 = carve([128, 2, 2, COLS])
        srct = carve([128, 2, 3, COLS])
        inside = carve([128, 2, 2, COLS])
        q1 = carve([128, 2, COLS, 2], BF16)
        rank = carve([128, 2, COLS])
        loops = carve([128, 2, COLS])
        selfe = carve([128, 2, COLS])
        others = carve([128, 2, COLS])
        selfto = carve([128, 2, COLS])
        slot0 = carve([128, 2, COLS])
        keep = carve([128, COLS])
        pay = carve([128, 2, COLS])
        pay2 = carve([128, 2, COLS, 2], BF16)
        slot1 = carve([128, 2, COLS, 2], BF16)
        rtot = carve([128, 2, RG, NT], BF16)
        Sb = carve([128, 2, 2 * NT], BF16)
        STb = carve([2 * NT, 2, CELL], BF16)
        filled = carve([128, NT, NT])
        b2rep = carve([D, L0, P])
        counti = carve([128, 128], I32)
        rowi = carve([128, 1], I32)
        tilei = carve([128, 2, NT + 2], I32)
        junki = carve([P, 1], I32)

        psum = ctx.enter_context(nc.psum_tensor("psum", [128, 8, 512], F32))
        bank = [psum[:, k, :] for k in range(8)]
        psRank = psum[:, 0:RG, 0:RK * NT]
        psTot, psSlot, psTurn, psCount = bank[4], bank[5], bank[6], bank[7]
        psMsg, psA = [bank[1]] + bank[4:8], bank[2:4]
        psT = [bank[0], bank[1]]
        psO = bank[2:2 + PB]
        psD = [bank[4], bank[5]]
        psM = [bank[6], bank[7]]

        s_w = sem("weights_loaded")
        s_x = sem("x_loaded")
        s_e = sem("edges_loaded")
        s_const = sem("constants_ready")
        s_wT = sem("weight_transposed")
        s_wTc = sem("weight_copied")
        s_b2 = sem("b2_spread")
        s_comp = sem("composed_ready")
        s_compc = sem("composed_copied")
        s_in = sem("tile_staged")
        s_agg_in = sem("aggregate_staged")
        s_tT = sem("tile_transposed")
        s_tC = sem("tile_copied")
        s_tO = sem("tile_product_ready")
        s_tE = sem("tile_finished")
        s_raw = sem("raw_ready")
        s_hi = sem("high_part_ready")
        s_rest = sem("rest_ready")
        s_mid = sem("middle_part_ready")
        s_dve = sem("vector_step")
        s_var = sem("variance_ready")
        s_std = sem("std_ready")
        s_h = sem("hidden_ready")
        s_relu = sem("hidden_rectified")
        s_tab = sem("linear_table_ready")
        s_agg = sem("aggregate_ready")
        s_fin = sem("result_ready")
        s_out = sem("result_stored")
        s_pset = sem("constant_step")
        gate = {e: sem(f"gate_{e}") for e in ("act", "dve", "pool")}
        g_tab = sem("general_table_stored")
        g_zero = sem("general_sums_cleared")
        g_idx = sem("general_indices_copied")
        g_rows = [[sem(f"general_rows_gathered{k}_{u}") for u in range(2)] for k in range(len(EDGE))]
        g_drep = sem("general_destinations_spread")
        g_dT = sem("general_destinations_turned")
        g_same = sem("general_equal_destinations_found")
        g_widx = sem("general_write_rows_ready")
        g_msg = sem("general_messages_ready")
        g_sum = sem("general_messages_summed")
        g_cp = sem("general_sums_copied")
        g_add = [[sem(f"general_sums_added{k}_{u}") for u in range(2)] for k in range(len(EDGE))]
        g_back = sem("general_sums_loaded")
        g_dve = sem("general_vector_step")

        o_dst = sem("sort_destinations_loaded")
        o_less = sem("sort_samples_counted")
        o_nless = sem("sort_starts_summed")
        o_lo = sem("sort_starts_ready")
        o_win = [sem(f"sort_window_loaded{u}") for u in range(2)]
        o_read = sem("sort_window_read")
        o_cell = sem("sort_cells_ready")
        o_tot = sem("sort_totals_ready")
        o_totc = sem("sort_totals_copied")
        o_rank = sem("sort_ranks_ready")
        o_rkc = sem("sort_ranks_copied")
        o_prod = sem("sort_ranks_picked")
        o_pay = sem("sort_payload_ready")
        o_mul = sem("sort_payload_placed")
        o_mulv = sem("sort_sources_placed")
        o_slot = sem("sort_slots_ready")
        o_perm = sem("sort_slots_filled")
        o_S = sem("sort_slots_copied")
        o_turn = sem("sort_slots_turned")
        o_ST = sem("sort_turned_copied")
        o_store = [sem(f"sort_slots_stored{u}") for u in range(2)]
        o_dve = sem("sort_vector_step")
        o_fill = sem("sort_fill_counted")
        o_sum = sem("sort_fill_summed")
        o_flag = sem("sort_flag_ready")
        f_list = [sem(f"cells_slot_list_loaded{b}") for b in range(2)]
        f_cur = [sem(f"cells_tile_rows_copied{u}") for u in range(2)]
        f_own = sem("cells_tile_slots_copied")
        f_one = sem("cells_count_column_set")
        f_toN = sem("cells_node_onehots_ready")
        f_toE = sem("cells_slot_onehots_ready")
        f_gat = sem("cells_rows_gathered")
        f_hi = sem("cells_high_part_ready")
        f_rest = sem("cells_rest_ready")
        f_mid = sem("cells_middle_part_ready")
        f_lo = sem("cells_low_part_ready")
        f_sca = sem("cells_messages_summed")
        f_add = sem("cells_part_added")
        f_agg = sem("cells_aggregate_copied")
        l_own = sem("linear_tile_slots_copied")
        l_from = sem("linear_onehots_ready")
        l_C = sem("linear_counts_ready")
        l_Cc = sem("linear_counts_copied")
        l_sum = sem("linear_rows_summed")
        l_add = sem("linear_part_added")
        l_agg = sem("linear_aggregate_copied")

        def hold(eng, name, s, value):
            eng.wait_ge(s, value)
            eng.sem_inc(gate[name], 1)

        def load_flag(eng):
            eng.wait_ge(o_flag, 1)
            return eng.value_load(missingi[0:1, 0:1], min_val=0, max_val=1)

        def edge_sp(sp, k, miss):
            with sp.If(miss < 1):
                if k < L0:
                    cells_sp(sp, k)
            with sp.If(miss > 0):
                general_sp(sp, k)

        def edge_pool(pool, k, miss):
            with pool.If(miss < 1):
                cells_pool(pool, k) if k < L0 else linear_pool(pool, k - L0)
            with pool.If(miss > 0):
                general_pool(pool, k)

        def edge_pe(pe, k, miss):
            with pe.If(miss < 1):
                cells_pe(pe, k) if k < L0 else linear_pe(pe, k - L0)
            with pe.If(miss > 0):
                general_pe(pe, k)

        def edge_act(act, k, miss):
            with act.If(miss < 1):
                cells_act(act, k) if k < L0 else linear_act(act, k - L0)
            with act.If(miss > 0):
                general_act(act, k)

        def edge_dve(dve, step, k, miss):
            with dve.If(miss < 1):
                cells_dve(dve, k) if k < L0 else counts_dve(dve, k - L0)
            with dve.If(miss > 0):
                general_dve(dve, step, k)

        def pairs(a):
            return a.rearrange("p c (n e) -> p c n e", e=2)

        def columns(numbers, width, count):
            a = numbers[:, 0:width].rearrange("p (o n e) -> p o n e", o=1, e=2)
            return a.to_broadcast([128, count, width // 2, 2])

        def along(values, width):
            c = values.shape[1]
            return values.rearrange("p c (o e) -> p c o e", o=1).to_broadcast([128, c, width // 2, 2])

        def twice(a):
            return a.rearrange("p (t o) -> p t o", o=1).to_broadcast([128, COLS, 2])

        def sort_sp(sp):
            sp.dma_start(dstl, dst.rearrange("(p t) -> p t", p=P)).then_inc(o_dst, 16)
            sp.wait_ge(o_lo, 1)

            def window(t, u):
                start = sp.value_load(loi[0:1, t], min_val=0, max_val=E - WIN)
                for n, ends in enumerate((src, dst)):
                    sp.dma_start(win[:, u, n, :], ends[bass.ds(start, WIN)].rearrange("(p t) -> p t", p=128)
                                 ).then_inc(o_win[u], 16)

            window(slice(0, 1), 0)
            with sp.Fori(0, NT // 2) as i:
                for u in range(2):
                    sp.wait_ge(o_read, i * 2 + (u + 2))
                    window(bass.ds(i * 2 + (u + 1), 1), 1 - u)

        def sort_pool(pool):
            with pool.Fori(0, NT // 2) as i:
                for u in range(2):
                    hold(pool, "pool", o_pay, i * 2 + (u + 3))
                    hold(pool, "pool", o_perm, i * 2 + (u + 1))
                    pool.tensor_tensor(payload[:, u, :, NT:2 * NT], one_cell[:, u],
                                       pay[:, u, :].rearrange("p (t o) -> p t o", o=1).to_broadcast([128, COLS, NT]),
                                       ALU.mult).then_inc(o_mul, 1)

        def sort_pe(pe):
            pe.wait_ge(o_less, 1)
            pe.matmul(psCount[0:1, 0:NT + 1], ones[0:P, 0:1], nless, start=True, stop=True).then_inc(o_nless, 1)

            def ranks(n, u):
                pe.wait_ge(o_cell, n + 3)
                pe.wait_ge(o_totc, n + 2)
                cell = one_cell[:, u].rearrange("p (g k) c -> p g k c", g=RG)
                for k in range(RK):
                    m = pe.matmul(psTot[:, 0:RG * NT].rearrange("p (g c) -> p g c", g=RG), ident_bf[:], cell[:, :, k, :],
                                  start=k == 0, stop=k == RK - 1)
                m.then_inc(o_tot, 1)
                pe.wait_ge(o_rkc, n + 2)
                pe.wait_ge(o_totc, n + 3)
                for g in range(RG):
                    bk = psRank[:, g, :].rearrange("p (k c) -> p k c", k=RK)
                    all_k = [128, RK, NT]
                    pe.matmul(bk, below_bf[:], rtot[:, u, g:g + 1, :].to_broadcast(all_k), start=True, stop=False)
                    for e in range(g):
                        pe.matmul(bk, ones_bf[:], rtot[:, u, e:e + 1, :].to_broadcast(all_k), start=False, stop=False)
                    for k in range(RK - 1):
                        m = pe.matmul(bk[:, k + 1:RK, :], ident_bf[:], cell[:, g, k:k + 1, :].to_broadcast([128, RK - 1 - k, NT]),
                                      start=False, stop=k == RK - 2)
                m.then_inc(o_rank, 1)

            def fill(n, u):
                pe.wait_ge(o_slot, n + 3)
                pe.wait_ge(o_mul, n + 3)
                pe.wait_ge(o_mulv, n + 3)
                pe.wait_ge(o_S, n + 2)
                for t in range(COLS):
                    m = pe.matmul(psSlot[:, 0:PAY], one_slot[:, t, :], payload[:, u, t, :], start=t == 0, stop=t == COLS - 1)
                m.then_inc(o_perm, 1)
                pe.wait_ge(o_ST, n + 2)
                pe.wait_ge(o_S, n + 3)
                pe.transpose(psTurn[0:2 * NT, 0:CELL // 2].bitcast(BF16), Sb[:, u, :], ident_bf[:]).then_inc(o_turn, 1)

            ranks(0, 0)
            with pe.Fori(0, NT // 2) as i:
                for u in range(2):
                    ranks(i * 2 + (u + 1), 1 - u)
                    fill(i * 2 + u, u)
            pe.wait_ge(o_fill, 1)
            for n in range(2):
                m = pe.matmul(psCount[0:1, 64:65], ones[:, 0:1], placed[:, n:n + 1], start=n == 0, stop=n == 1)
            m.then_inc(o_sum, 1)

        def sort_act(act):
            def totals(n, u):
                act.wait_ge(o_tot, n + 3)
                act.wait_ge(o_rank, n + 2)
                act.copy(rtot[:, u], psTot[:, 0:RG * NT].rearrange("p (g c) -> p g c", g=RG)).then_inc(o_totc, 1)

            def copy_ranks(n, u):
                act.wait_ge(o_rank, n + 3)
                act.wait_ge(o_prod, n + 1)
                act.copy(ranks_bf[:, u], psRank).then_inc(o_rkc, 1)

            totals(0, 0)
            copy_ranks(0, 0)
            with act.Fori(0, NT // 2) as i:
                for u in range(2):
                    totals(i * 2 + (u + 1), 1 - u)
                    copy_ranks(i * 2 + (u + 1), 1 - u)
                    hold(act, "act", o_turn, i * 2 + (u + 1))
                    hold(act, "act", o_perm, i * 2 + (u + 3))
                    act.copy(slots[:, :, bass.ds(i * 2 + u, 1), :], psSlot[:, 0:2 * NT].rearrange("p (n o c) -> p n o c", n=2, o=1))
                    act.copy(selfs[:, bass.ds(i * 2 + (u + 1), 1)], psSlot[:, 2 * NT:2 * NT + 1])
                    act.copy(Sb[:, u, :], psSlot[:, 0:2 * NT]).then_inc(o_S, 1)
                    act.wait_ge(o_turn, i * 2 + (u + 3))
                    act.wait_ge(o_store[u], i * 32 + 32)
                    act.copy(STb[:, u, :], psTurn[0:2 * NT, 0:CELL // 2].bitcast(BF16)).then_inc(o_ST, 1)
                    act.wait_ge(o_ST, i * 2 + (u + 3))
                    for n in range(2):
                        act.dma_start(slots_dram[bass.ds(i, 1), n, u * NT:(u + 1) * NT, :].rearrange("o c e -> (o c) e"),
                                      STb[n * NT:(n + 1) * NT, u, :]).then_inc(o_store[u], 16)
            for u in range(2):
                act.wait_ge(o_store[u], 32 + 32 * (NT // 2))

        def sort_dve(dve):
            step = Steps(dve, o_dve)
            dve.wait_ge(o_dst, 16)
            step.did(dve.tensor_copy(samp, dstl[:, 0:ET:SAMPLE]))
            step.last()
            grid = [P, NT + 1, NT]
            step.did(dve.tensor_tensor(less, samp.rearrange("p (o t) -> p o t", o=1).to_broadcast(grid),
                                       tilec[0:P, 0, 0:NT + 1].rearrange("p (t o) -> p t o", o=1).to_broadcast(grid), ALU.is_lt))
            step.last()
            dve.tensor_reduce(nless, less, AX, ALU.add).then_inc(o_less, 1)
            dve.wait_ge(o_nless, 1)
            step.did(dve.tensor_scalar(lo[:, 0:NT + 1], psCount[0:1, 0:NT + 1], float(SAMPLE), float(1 - SAMPLE), ALU.mult, ALU.add))
            step.last()
            dve.tensor_scalar(loi[:, 0:NT + 1], lo[:, 0:NT + 1], 0.0, float(E - WIN), ALU.max, ALU.min).then_inc(o_lo, 1)

            def find_cells(n, u, loaded, tile):
                dve.wait_ge(o_win[u], loaded)
                a = step.did(dve.tensor_copy(node[:, u], win[:, u]))
                step.after(a)
                dve.sem_inc(o_read, 1)
                t = [srct[:, u, k, :] for k in range(3)]
                to1 = off1[:, u, 1, :]
                a = step.did(dve.tensor_scalar(t[0], node[:, u, 0, :], 1.0 / P, -((P - 1) / 2) / P, ALU.mult, ALU.add))
                hold(dve, "dve", o_dve, a)
                b = step.did(dve.tensor_scalar(to1, node[:, u, 1, :], tilec[:, 1, tile], None, ALU.subtract))
                step.did(dve.tensor_tensor(loops[:, u], node[:, u, 0, :], node[:, u, 1, :], ALU.is_equal))
                a = step.did(dve.tensor_scalar(t[1], t[0], MAGIC, None, ALU.add))
                step.after(b)
                b = step.did(dve.tensor_scalar(inside[:, u, 0, :], to1, 1.0, None, ALU.is_ge))
                step.after(a)
                a = step.did(dve.tensor_scalar(t[2], t[1], MAGIC, None, ALU.subtract))
                step.after(b)
                b = step.did(dve.scalar_tensor_tensor(out=inside[:, u, 1, :], in0=to1, scalar=float(P),
                                                      in1=inside[:, u, 0, :], op0=ALU.is_le, op1=ALU.mult))
                step.after(b)
                b = step.did(dve.tensor_tensor(selfe[:, u], loops[:, u], inside[:, u, 1, :], ALU.mult))
                a = step.did(dve.scalar_tensor_tensor(out=t[0], in0=t[2], scalar=-float(P), in1=node[:, u, 0, :],
                                                      op0=ALU.mult, op1=ALU.add))
                step.after(b)
                b = step.did(dve.tensor_tensor(others[:, u], inside[:, u, 1, :], selfe[:, u], ALU.subtract))
                c = step.did(dve.tensor_tensor(selfto[:, u], selfe[:, u], to1, ALU.mult))
                step.after(a)
                step.did(dve.tensor_scalar(off1[:, u, 0, :], t[0], 1.0, None, ALU.add))
                step.after(b)
                step.did(dve.scalar_tensor_tensor(out=q1[:, u], in0=twice(t[2]), scalar=1.0, in1=twice(others[:, u]),
                                                  op0=ALU.add, op1=ALU.mult))
                step.after(c)
                a = step.did(dve.tensor_tensor(slot0[:, u], others[:, u], selfto[:, u], ALU.add))
                step.after(a)
                dve.wait_ge(o_mul, n + 1)
                dve.wait_ge(o_mulv, n + 1)
                dve.tensor_tensor(pairs(one_cell[:, u]), columns(col1, NT, COLS), along(q1[:, u], NT), ALU.is_equal).then_inc(o_cell, 1)

            def find_slots(n, u, tile):
                dve.wait_ge(o_rkc, n + 3)
                a = step.did(dve.tensor_tensor(pairs(prod), pairs(one_cell[:, u]),
                                               pairs(ranks_bf[:, u].rearrange("p g (k c) -> p (g k) c", c=NT)), ALU.mult))
                step.after(a)
                dve.sem_inc(o_prod, 1)
                a = step.did(dve.tensor_tensor(prod[:, :, 0:FOLD], prod[:, :, 0:FOLD], prod[:, :, NT - FOLD:NT], ALU.add))
                step.after(a)
                a = step.did(dve.tensor_reduce(rank[:, u, :], prod[:, :, 0:NT - FOLD], AX, ALU.add))
                step.after(a)
                step.did(dve.tensor_scalar(keep, rank[:, u, :], float(CELL), None, ALU.is_lt))
                a = step.did(dve.tensor_tensor(slot1[:, u], twice(rank[:, u, :]), twice(slot0[:, u]), ALU.add))
                step.after(a)
                a = step.did(dve.tensor_tensor(pay[:, u], keep, off1[:, u, 1, :], ALU.mult))
                b = step.did(dve.tensor_tensor(pay2[:, u], twice(keep), twice(off1[:, u, 0, :]), ALU.mult))
                step.after(a)
                dve.sem_inc(o_pay, 1)
                dve.wait_ge(o_perm, n + 2)
                step.did(dve.tensor_copy(payload[:, u, :, 2 * NT:PAY], twice(selfe[:, u])))
                dve.tensor_tensor(pairs(one_slot), columns(col1, CELL, COLS), along(slot1[:, u], CELL), ALU.is_equal).then_inc(o_slot, 1)
                step.after(b)
                dve.tensor_tensor(pairs(payload[:, u, :, 0:NT]), pairs(one_cell[:, u]), along(pay2[:, u], NT), ALU.mult
                                  ).then_inc(o_mulv, 1)

            find_cells(0, 0, 32, slice(0, 1))
            with dve.Fori(0, NT // 2) as i:
                step.enter(i, 2 * (15 + 8))
                for u in range(2):
                    find_cells(i * 2 + (u + 1), 1 - u, i * 32 + (32 if u == 0 else 64), bass.ds(i * 2 + (u + 1), 1))
                    find_slots(i * 2 + u, u, bass.ds(i * 2 + u, 1))
                step.leave(NT // 2)
            dve.wait_ge(o_S, NT + 2)
            step.did(dve.tensor_scalar(filled, slots[:, 1, 0:NT], 0.0, None, ALU.is_gt))
            step.last()
            step.did(dve.tensor_reduce(placed[:, 1:2], selfs[:, 1:NT + 1], AX, ALU.add))
            dve.tensor_reduce(placed[:, 0:1], filled.rearrange("p t c -> p (t c)"), AX, ALU.add).then_inc(o_fill, 1)
            dve.wait_ge(o_sum, 1)
            step.did(dve.tensor_scalar(missing[:, 0:1], psCount[0:1, 64:65], -1.0, float(E), ALU.mult, ALU.add))
            step.last()
            dve.tensor_scalar(missingi[:], missing[:, 0:1], 0.0, None, ALU.is_gt).then_inc(o_flag, 1)

        def group_done(i, k, pos, extra=0):
            return i * BODY + (BODY + k * (PAIRED * BODY + extra) + pos + 1)

        def before_it(i, k, pos, buffers, extra=0):
            at = pos % BODY
            last = at - buffers if at >= buffers else max(q for q in range(BODY) if q % buffers == at) - BODY
            return group_done(i, k, pos - at + last, extra)

        def cell(pos, c):
            return divmod(pos % BODY * GROUP + c, NT)

        def add_parts(i, k, u):
            return i * 4 + (k * (4 * PAIRED + 2) + (2 if u == 0 else 0) + 1)

        def part_sums(u, p, width):
            return psA[u][0:P, p * D:p * D + width].rearrange("p (o d) -> p o d", o=1)

        def cells_sp(sp, k):
            sp.wait_ge(s_tE, STAGE0[EDGE[k]] + NT)
            for u in range(2):
                sp.wait_ge(o_store[u], 32 + 32 * PAIRED)

            def load(i, pair, tile, c):
                g0, n = CHUNKS[c]
                g1, n1 = CHUNKS[c - 2]
                sp.wait_ge(f_toN, group_done(i, k, g1 + n1 - 1 - (BODY if c < 2 else 0), 3))
                for a in range(2):
                    sp.dma_start(slist[c % 2][:, a, 0:n * GROUP * CELL],
                                 slots_dram[pair, a, g0 * GROUP:(g0 + n) * GROUP, :]
                                 .rearrange("o c e -> o (c e)").to_broadcast([P, n * GROUP * CELL])).then_inc(f_list[c % 2], 16)
                if c in OWN:
                    u = OWN.index(c)
                    sp.wait_ge(f_gat, group_done(i, k, LAST[u] - BODY, 2))
                    sp.dma_start(cur[:, u], TAB[:, 1, tile(u)].rearrange("p o c d -> p (o c d)")).then_inc(f_cur[u], 16)

            with sp.Fori(0, PAIRED) as i:
                for c in range(len(CHUNKS)):
                    load(i, bass.ds(i, 1), lambda u: bass.ds(i * 2 + u, 1), c)
            load(PAIRED, slice(0, 1), lambda u: slice(u, u + 1), 0)

        def cells_pool(pool, k):
            hold(pool, "pool", s_tE, STAGE0[EDGE[k]] + NT)
            pool.memset(mparts[:, :, :, ROW:ROW + 1], 1.0).then_inc(f_one, 1)
            hold(pool, "pool", f_one, k + 1)

            def own_slots(tile, u):
                pool.tensor_copy(curS[:, u * NT:(u + 1) * NT], slots[:, 1, tile, :].rearrange("p o c -> p c o").to_broadcast([128, NT, 2])
                                 ).then_inc(f_own, 1)

            own_slots(slice(0, 1), 0)
            with pool.Fori(0, PAIRED) as i:
                hold(pool, "pool", f_toE, group_done(i, k, -1, 1))
                own_slots(bass.ds(i * 2 + 1, 1), 1)
                for pos in range(BODY):
                    hold(pool, "pool", f_mid, group_done(i, k, pos))
                    pool.tensor_tensor(mparts[:, pos % RING, :, 2 * D:ROW], mrest[:, pos % 2], mparts[:, pos % RING, :, D:2 * D], ALU.subtract
                                       ).then_inc(f_lo, 1)
                    if pos == LAST[0] + 4:
                        hold(pool, "pool", f_toE, group_done(i, k, LAST[0], 1))
                        own_slots(bass.ds(i * 2 + 2, 1), 0)

        def cells_pe(pe, k):
            def gather(i, pos):
                for u in range(2):
                    if pos % BODY == FIRST[u]:
                        pe.wait_ge(f_cur[u], i * 16 + (k * (PAIRED + 1 - u) + pos // BODY + 1) * 16)
                pe.wait_ge(f_toN, group_done(i, k, pos, 3))
                pe.wait_ge(f_rest, before_it(i, k, pos, RING))
                b = pos % BODY % RING
                for c in range(GROUP):
                    u, t = cell(pos, c)
                    to = psMsg[b][:, c * D:(c + 1) * D]
                    for p in range(PARTS):
                        pe.matmul(to, toN[:, b, 0, c * CELL:(c + 1) * CELL], TAB[:, 0, t, p, :], start=p == 0, stop=False)
                    for p in range(PARTS):
                        m = pe.matmul(to, toN[:, b, 1, c * CELL:(c + 1) * CELL], cur[:, u, p * D:(p + 1) * D],
                                      start=False, stop=p == PARTS - 1)
                m.then_inc(f_gat, 1)

            def scatter(i, pos):
                pe.wait_ge(f_toE, group_done(i, k, pos, 1))
                pe.wait_ge(f_lo, group_done(i, k, pos))
                for u in range(2):
                    if pos == FIRST[u]:
                        pe.wait_ge(f_agg, i * 2 + (k * (NT + 1) + u + 2))
                for c in range(GROUP):
                    u, t = cell(pos, c)
                    m = pe.matmul(psA[u][0:P, 0:ROW + 1], toE[:, pos % RING, c, 0:P], mparts[:, pos % RING, c, 0:ROW + 1],
                                  start=t == 0, stop=t == NT - 1, skip_group_check=True)
                m.then_inc(f_sca, 1)

            for pos in range(2):
                gather(0, pos)
            with pe.Fori(0, PAIRED) as i:
                for pos in range(BODY):
                    gather(i, pos + 2)
                    scatter(i, pos)

        def cells_act(act, k):
            with act.Fori(0, PAIRED) as i:
                def high(pos):
                    act.wait_ge(f_gat, group_done(i, k, pos, 2))
                    act.wait_ge(f_sca, before_it(i, k, pos, RING))
                    act.activation(mparts[:, pos % RING, :, 0:D], psMsg[pos % RING].rearrange("p (c d) -> p c d", d=D), ACT.Relu
                                   ).then_inc(f_hi, 1)

                def middle(pos):
                    act.wait_ge(f_rest, group_done(i, k, pos))
                    act.copy(mparts[:, pos % RING, :, D:2 * D], mrest[:, pos % 2]).then_inc(f_mid, 1)

                for pos in range(BODY):
                    if pos:
                        middle(pos - 1)
                    high(pos)
                middle(BODY - 1)

        def cells_dve(dve, k):
            def by_node(i, pos):
                g = pos % BODY
                c = max(n for n, (g0, _) in enumerate(CHUNKS) if g0 <= g)
                at = (g - CHUNKS[c][0]) * GROUP * CELL
                per = len(CHUNKS) // 2
                n = pos // BODY * per + c // 2
                dve.wait_ge(f_list[c % 2], i * (per * 32) + (k * (PAIRED * per + 1 - c % 2) * 32 + 32 * (n + 1)))
                dve.wait_ge(f_gat, before_it(i, k, pos, RING, 2))
                dve.tensor_scalar(toN[:, g % RING], slist[c % 2][:, :, at:at + GROUP * CELL], row1[0:P, :], None, ALU.is_equal
                                  ).then_inc(f_toN, 1)

            def by_slot(i, pos):
                g = pos % BODY
                for u in range(2):
                    if g == FIRST[u]:
                        dve.wait_ge(f_own, i * 2 + (k * (NT + 1) + pos // BODY * 2 + u + 1))
                dve.wait_ge(f_sca, before_it(i, k, pos, RING))
                dve.tensor_tensor(pairs(toE[:, g % RING]), columns(col1, 126, GROUP),
                                  along(curS[:, g * GROUP:(g + 1) * GROUP], 126), ALU.is_equal).then_inc(f_toE, 1)

            def rest_of(i, pos):
                dve.wait_ge(f_hi, group_done(i, k, pos))
                dve.wait_ge(f_lo, before_it(i, k, pos, 2))
                dve.scalar_tensor_tensor(out=mrest[:, pos % 2], in0=psMsg[pos % RING].rearrange("p (c d) -> p c d", d=D), scalar=0.0,
                                         in1=mparts[:, pos % RING, :, 0:D], op0=ALU.max, op1=ALU.subtract).then_inc(f_rest, 1)

            def sums(i, at, u, pos):
                hold(dve, "dve", f_sca, group_done(i, k, pos))
                add = add_parts(i, k, u)
                dve.tensor_tensor(AGGs[:, at, :], AGGs[:, at, :], part_sums(u, 2, W), ALU.add).then_inc(f_add, 1)
                hold(dve, "dve", f_add, add)
                dve.tensor_tensor(AGGs[:, at, 0:D], AGGs[:, at, 0:D], part_sums(u, 1, D), ALU.add).then_inc(f_add, 1)
                hold(dve, "dve", f_add, add + 1)
                dve.tensor_tensor(AGGs[:, at, 0:D], AGGs[:, at, 0:D], part_sums(u, 0, D), ALU.add).then_inc(f_agg, 1)

            for pos in range(3):
                by_node(0, pos)
            by_slot(0, 0)
            with dve.Fori(0, PAIRED) as i:
                for pos in range(BODY):
                    rest_of(i, pos)
                    by_node(i, pos + 3)
                    by_slot(i, pos + 1)
                    if pos == 2:
                        sums(i, bass.ds(i * 2, 1), 1, -1)
                    if pos == LAST[0] + 3:
                        sums(i, bass.ds(i * 2 + 1, 1), 0, LAST[0])
            sums(PAIRED, slice(NT, NT + 1), 1, -1)
            dve.wait_ge(f_agg, 2 + (NT + 1) * (k + 1))
            dve.sem_inc(s_agg, 1)

        def linear_pool(pool, l):
            hold(pool, "pool", s_tab, (l + 1) * NB_LOOPS)

            def own_slots(tile, u):
                for a in range(2):
                    o = pool.tensor_copy(curS2[:, u * NT:(u + 1) * NT, a, :],
                                         slots[:, a, tile, :].rearrange("p o c -> p c o").to_broadcast([128, NT, 2]))
                o.then_inc(l_own, 1)

            own_slots(slice(0, 1), 0)
            with pool.Fori(0, PAIRED) as i:
                hold(pool, "pool", l_from, group_done(i, l, -1, 2))
                own_slots(bass.ds(i * 2 + 1, 1), 1)
                hold(pool, "pool", l_from, group_done(i, l, LAST[0], 2))
                own_slots(bass.ds(i * 2 + 2, 1), 0)

        def linear_pe(pe, l):
            def count(i, pos):
                b = pos % BODY % RING
                pe.wait_ge(l_from, group_done(i, l, pos, 2))
                pe.wait_ge(l_Cc, before_it(i, l, pos, RING))
                for c in range(GROUP):
                    m = pe.matmul(psMsg[b][0:P, c * P:(c + 1) * P], oneE[:, b, c, 0, 0:P], oneE[:, b, c, 1, 0:P],
                                  start=True, stop=True, skip_group_check=True)
                m.then_inc(l_C, 1)

            def total(i, pos):
                pe.wait_ge(l_Cc, group_done(i, l, pos))
                for u in range(2):
                    if pos == FIRST[u]:
                        pe.wait_ge(l_agg, i * 2 + (l * (NT + 1) + u + 2))
                for c in range(GROUP):
                    u, t = cell(pos, c)
                    m = pe.matmul(psA[u][0:P, 0:ROW], cells[:, pos % RING, c, 0:P], TAB[:, 0, t].rearrange("p c d -> p (c d)"),
                                  start=t == 0, stop=t == NT - 1, skip_group_check=True)
                m.then_inc(l_sum, 1)

            for pos in range(2):
                count(0, pos)
            with pe.Fori(0, PAIRED) as i:
                for pos in range(BODY):
                    count(i, pos + 2)
                    total(i, pos)

        def linear_act(act, l):
            with act.Fori(0, PAIRED) as i:
                for pos in range(BODY):
                    act.wait_ge(l_C, group_done(i, l, pos, 2))
                    act.wait_ge(l_sum, before_it(i, l, pos, RING))
                    act.copy(cells[:, pos % RING, :, 0:P], psMsg[pos % RING][0:P, 0:GROUP * P].rearrange("p (c d) -> p c d", d=P)
                             ).then_inc(l_Cc, 1)

        def counts_dve(dve, l):
            def onehots(i, pos):
                for u in range(2):
                    if pos == FIRST[u]:
                        dve.wait_ge(l_own, i * 2 + (l * (NT + 1) + u + 1))
                dve.wait_ge(l_C, before_it(i, l, pos, RING, 2))
                dve.tensor_tensor(pairs(oneE[:, pos % RING].rearrange("p c a n -> p (c a) n")), columns(col1, 126, 2 * GROUP),
                                  along(curS2[:, pos * GROUP:(pos + 1) * GROUP].rearrange("p c a e -> p (c a) e"), 126),
                                  ALU.is_equal).then_inc(l_from, 1)

            def sums(i, at, u, pos):
                hold(dve, "dve", l_sum, group_done(i, l, pos))
                add = add_parts(i, l, u)
                dve.scalar_tensor_tensor(out=AGGs[:, at, 0:D], in0=Hs[:, at, :], scalar=selfs[0:P, at], in1=part_sums(u, 2, D),
                                         op0=ALU.mult, op1=ALU.add).then_inc(l_add, 1)
                hold(dve, "dve", l_add, add)
                dve.tensor_tensor(AGGs[:, at, 0:D], AGGs[:, at, 0:D], part_sums(u, 1, D), ALU.add).then_inc(l_add, 1)
                hold(dve, "dve", l_add, add + 1)
                dve.tensor_tensor(AGGs[:, at, 0:D], AGGs[:, at, 0:D], part_sums(u, 0, D), ALU.add).then_inc(l_agg, 1)

            with dve.Fori(0, PAIRED) as i:
                for pos in range(BODY):
                    onehots(i, pos)
                    if pos == 4:
                        sums(i, bass.ds(i * 2, 1), 1, -1)
                    if pos == LAST[0] + 5:
                        sums(i, bass.ds(i * 2 + 1, 1), 0, LAST[0])
            for pos in range(2):
                onehots(PAIRED, pos)
            sums(PAIRED, slice(NT, NT + 1), 1, -1)
            dve.wait_ge(l_agg, 2 + (NT + 1) * (l + 1))
            dve.sem_inc(s_agg, 1)

        def general_sp(sp, k):
            if k < L0:
                sp.wait_ge(s_tE, STAGE0[EDGE[k]] + NT)
            else:
                sp.wait_ge(s_tab, (k - L0 + 1) * NB_LOOPS)
            sp.dma_start(srci, src.rearrange("(p t) -> p t", p=P)).then_inc(s_e, 16)
            sp.dma_start(dsti, dst.rearrange("(p t) -> p t", p=P)).then_inc(s_e, 16)
            sp.wait_ge(s_const, 1)
            if k:
                sp.wait_ge(g_back, 32 * k)
            for u in range(2):
                sp.dma_start(sums_dram[u][0:N, :].rearrange("(t p) d -> p t d", p=P),
                             zrow[:].rearrange("p (o d) -> p o d", o=1).to_broadcast([P, NT, W])
                             ).then_inc(g_zero, 16)
            tables = 2 if k < L0 else 1
            for n in range(tables):
                sp.dma_start(table_dram[n].rearrange("(t p) d -> p t d", p=P),
                             TAB[:, n].rearrange("p t c d -> p t (c d)")).then_inc(g_tab, 16)
            for u in range(2):
                sp.wait_ge(g_add[k][u], 16 * PAIRS + 16)
            for u, to in enumerate((AGG, AGG1)):
                sp.dma_start(to, sums_dram[u][0:N, :].rearrange("(t p) d -> p t d", p=P)).then_inc(g_back, 16)

        def staged(name):
            return STAGE0[name] + 2 * STAGES.index(name)

        def stage_pool(pool, name, ready, value, source=H):
            base = staged(name)
            hold(pool, "pool", s_tT, base)
            hold(pool, "pool", ready, value)
            with pool.Fori(0, NB_LOOPS) as i:
                for t in range(TB):
                    hold(pool, "pool", s_tT, i * TB + (base + t + 1 - PB))
                    pool.tensor_copy(tile_in[:, t % PB, 0, :], source[:, bass.ds(i * TB + t, 1), :]).then_inc(s_in, 1)
            hold(pool, "pool", s_in, base + NT)
            pool.sem_inc(s_in, 2)

        def general_pool(pool, k):
            hold(pool, "pool", s_e, 32 * (k + 1))
            pool.memset(msg[:, :, D:W], 1.0)
            hold(pool, "pool", g_tab, 16 * (2 * min(k + 1, L0) + max(k + 1 - L0, 0)))
            hold(pool, "pool", g_zero, 32 * (k + 1))
            for u in range(2):
                pool.dma_start(sums_dram[u][N:N + P, :], zrow[:]).then_inc(g_add[k][u], 16)
            tables = 2 if k < L0 else 1
            done = 2 * PAIRS * k + 2
            with pool.Fori(0, PAIRS) as i:
                hold(pool, "pool", g_msg, i * 2 + done)
                hold(pool, "pool", g_widx, i * 2 + done)
                for u in range(2):
                    pool.tensor_copy(sidx[:, u:u + 1], srci[:, bass.ds(i * 2 + u, 1)])
                    pool.tensor_copy(didx[:, u:u + 1], dsti[:, bass.ds(i * 2 + u, 1)]).then_inc(g_idx, 1)
                hold(pool, "pool", g_idx, i * 2 + done)
                for u in range(2):
                    for n in range(tables):
                        pool.indirect_dma_start(rows[:, u, n].rearrange("p c d -> p (c d)"), None, table_dram[n],
                                                bass.IndirectOffsetOnAxis(ap=(sidx, didx)[n][:, u:u + 1], axis=0)
                                                ).then_inc(g_rows[k][u], 16)
                for u in range(2):
                    hold(pool, "pool", g_cp, i * 2 + (u + 1 + done))
                    hold(pool, "pool", g_add[k][u], i * 16 + 16)
                    pool.indirect_dma_start(sums_dram[u], bass.IndirectOffsetOnAxis(ap=widx[:, u:u + 1], axis=0),
                                            msum[:, u, :], None, compute_op=ALU.add).then_inc(g_add[k][u], 16)

        def stage_pe(pe, name, products):
            base, base_in = STAGE0[name], staged(name)
            used, base_used = (s_raw, PB + SPLITS.index(name) * NT) if name in SPLITS else (s_tE, base)

            def turn(i, t):
                u = t % 2
                pe.wait_ge(s_in, i * TB + (base_in + t + 1))
                m = pe.transpose(psT[u][:, 0:P], tile_in[:, t % PB, 0, :], ident[0:P, 0:P])
                if name in AGG_STAGES:
                    pe.wait_ge(s_agg_in, i * TB + (AGG_STAGES.index(name) * (NT + 1) + t + 1))
                    m = pe.transpose(psT[u][:, 128:128 + P], tile_in[:, t % PB, 1, :], ident[0:P, 0:P])
                m.then_inc(s_tT, 1)

            def multiply(i, t):
                u = t % 2
                pe.wait_ge(s_tC, i * TB + (base + t + 1))
                pe.wait_ge(used, i * TB + (base_used + t + 1 - PB))
                for n, (which, rhs, at, stop) in enumerate(products):
                    start = n == 0 or products[n - 1][3]
                    m = pe.matmul(psO[t % PB][0:P, at:at + rhs.shape[1]], hT[:, u, which, 0:P], rhs, start=start, stop=stop)
                m.then_inc(s_tO, 1)

            turn(0, 0)
            with pe.Fori(0, NB_LOOPS) as i:
                for t in range(TB):
                    turn(i, t + 1)
                    multiply(i, t)
            pe.wait_ge(s_tT, base_in + NT + 1)
            pe.sem_inc(s_tT, 1)

        def general_pe(pe, k):
            done = 2 * PAIRS * k + 2
            with pe.Fori(0, PAIRS) as i:
                for u in range(2):
                    pe.wait_ge(g_drep, i * 2 + (u - 1 + done))
                    pe.wait_ge(g_same, i * 2 + done)
                    pe.transpose(psD[u][0:P, 0:P], drep[:, u, :], ident[0:P, 0:P]).then_inc(g_dT, 1)
                for u in range(2):
                    pe.wait_ge(g_same, i * 2 + (u + 1 + done))
                    pe.wait_ge(g_msg, i * 2 + (u + 1 + done))
                    pe.wait_ge(g_cp, i * 2 + done)
                    pe.matmul(psM[u][0:P, 0:W], same[:, u, :], msg[:, u, :], start=True, stop=True).then_inc(g_sum, 1)

        def norm_act(act, n):
            act.wait_ge(s_var, n + 1)
            act.activation(std[:], var[:], ACT.Sqrt, bias=eps[:]).then_inc(s_std, 1)

        def stage_act(act, name, split=None):
            base, base_in = STAGE0[name], staged(name)
            n = 2 if name in AGG_STAGES else 1
            if n == 2:
                act.wait_ge(s_tT, base_in)
                hold(act, "act", s_agg, AGG_STAGES.index(name) + 1)
            with act.Fori(0, NB_LOOPS) as i:
                def copy(t):
                    act.wait_ge(s_tT, i * TB + (base_in + t + 1))
                    act.wait_ge(s_tO, i * TB + (base + t - 1))
                    act.copy(hT[:, t % 2, 0:n, 0:P], psT[t % 2][:, 0:n * 128].rearrange("k (n p) -> k n p", n=n)[:, :, 0:P]
                             ).then_inc(s_tC, 1)

                def high(t):
                    hold(act, "act", s_raw, i * TB + (PB + t + 1 + split * NT))
                    act.copy(TAB[:, :, bass.ds(i * TB + t, 1), 0, :], raw[:, t % PB].rearrange("p n (o d) -> p n o d", o=1)).then_inc(s_hi, 1)

                def middle(t):
                    hold(act, "act", s_rest, i * TB + (t + 1 + split * NT))
                    act.copy(TAB[:, :, bass.ds(i * TB + t, 1), 1, :], rest[:, t % PB].rearrange("p n (o d) -> p n o d", o=1)).then_inc(s_mid, 1)

                def stage(t):
                    act.copy(tile_in[:, t % PB, 1, :], AGG[:, bass.ds(i * TB + t, 1), 0:D]).then_inc(s_agg_in, 1)

                for t in range(TB):
                    if n == 2:
                        stage(t)
                        if t >= 1:
                            copy(t - 1)
                        continue
                    copy(t)
                    if split is not None:
                        if t >= 1:
                            high(t - 1)
                        if t >= 2:
                            middle(t - 2)
                if n == 2:
                    copy(TB - 1)
                if split is not None:
                    high(TB - 1)
                    middle(TB - 2)
                    middle(TB - 1)
            if n == 2:
                act.wait_ge(s_agg_in, AGG_STAGES.index(name) * (NT + 1) + NT)
                act.sem_inc(s_agg_in, 1)

        def general_act(act, k):
            done = 2 * PAIRS * k + 2
            with act.Fori(0, PAIRS) as i:
                for u in range(2):
                    act.wait_ge(g_sum, i * 2 + (u + 1 + done))
                    act.wait_ge(g_add[k][u], i * 16 + 16)
                    act.copy(msum[:, u, :], psM[u][0:P, 0:W]).then_inc(g_cp, 1)

        def norm_dve(dve, step, n, source, to, l=None):
            even, odd = stats[:, :, 0:3], stats[:, :, 3:6]
            step.last()
            a = step.did(dve.tensor_tensor(mean[:], even[:, :, 1], odd[:, :, 1], ALU.add))
            b = step.did(dve.tensor_tensor(sq[:], even[:, :, 1], odd[:, :, 1], ALU.subtract))
            c = step.did(dve.tensor_tensor(var[:], even[:, :, 2], odd[:, :, 2], ALU.add))
            step.after(c)
            d = step.did(dve.tensor_scalar(mean[:], mean[:], 0.5, None, ALU.mult))
            e = step.did(dve.tensor_tensor(sq[:], sq[:], sq[:], ALU.mult))
            f = step.did(dve.tensor_scalar(var[:], var[:], 1.0 / D, None, ALU.mult))
            step.after(f)
            dve.scalar_tensor_tensor(out=var[:], in0=sq[:], scalar=0.25, in1=var[:], op0=ALU.mult, op1=ALU.add
                                     ).then_inc(s_var, 1)
            per_tile = [P, NT, D]
            dve.wait_ge(s_std, n + 1)
            step.did(dve.reciprocal(rstd[:], std[:]))
            step.last()
            for t in range(NT):
                step.did(dve.tensor_scalar(to[:, t, :], source[:, t, :], mean[:, t:t + 1], rstd[:, t:t + 1], ALU.subtract, ALU.mult))
            if l is not None:
                step.last()
                step.did(dve.tensor_tensor(to, to, bias[:, LN_G + l:LN_G + l + 1, :].to_broadcast(per_tile), ALU.mult))
                step.last()
                dve.tensor_tensor(to, to, bias[:, LN_B + l:LN_B + l + 1, :].to_broadcast(per_tile), ALU.add).then_inc(s_h, 1)

        def split_dve(dve, l):
            base, done = STAGE0[f"ab{l}"], l * NT
            dve.tensor_copy(AGG[:, :, D], selfs[0:P, 1:NT + 1])
            with dve.Fori(0, NB_LOOPS) as i:
                for t in range(TB + 3):
                    if t >= 3:
                        r, u = t - 3, (t - 3) % PB
                        hold(dve, "dve", s_rest, i * TB + (done + r + 1))
                        hold(dve, "dve", s_mid, i * TB + (done + r + 1))
                        dve.tensor_scalar(AGG[:, bass.ds(i * TB + r, 1), 0:D], tmp[:, u, 0:1, :], 0.0,
                                          selfs[0:P, bass.ds(i * TB + (r + 1), 1)], ALU.max, ALU.mult)
                        dve.tensor_tensor(TAB[:, :, bass.ds(i * TB + r, 1), 2, :], rest[:, u].rearrange("p n (o d) -> p n o d", o=1),
                                          TAB[:, :, bass.ds(i * TB + r, 1), 1, :], ALU.subtract).then_inc(s_tE, 1)
                    if t < TB:
                        u = t % PB
                        dve.wait_ge(s_tO, i * TB + (base + t + 1))
                        dve.tensor_tensor(raw[:, u], psO[u][0:P, 0:2 * D].rearrange("p (n d) -> p n d", n=2), abias[:, l], ALU.add
                                          ).then_inc(s_raw, 1)
                    if 1 <= t <= TB:
                        r, u = t - 1, (t - 1) % PB
                        dve.wait_ge(s_tE, i * TB + (base + r - 2))
                        hold(dve, "dve", s_hi, i * TB + (done + r + 1))
                        dve.tensor_tensor(tmp[:, u, 0, :], raw[:, u, 0, :], raw[:, u, 1, :], ALU.add)
                        dve.tensor_tensor(rest[:, u].rearrange("p n (o d) -> p n o d", o=1), raw[:, u].rearrange("p n (o d) -> p n o d", o=1),
                                          TAB[:, :, bass.ds(i * TB + r, 1), 0, :], ALU.subtract).then_inc(s_rest, 1)

        def update_dve(dve, step, l):
            base = STAGE0[f"upd{l}"]
            with dve.Fori(0, NB_LOOPS) as i:
                step.enter(i, 4 * TB)
                now = {}
                for t in range(TB + 3):
                    if t < TB:
                        hold(dve, "dve", s_tO, i * TB + (base + t + 1))
                        now[t, 0] = step.did(dve.scalar_tensor_tensor(
                            out=tmp[:, t % PB, 0, :], in0=b2upd[:, l, :], scalar=degc[:, bass.ds(i * TB + t, 1)],
                            in1=psO[t % PB][0:P, 0:D], op0=ALU.mult, op1=ALU.add))
                    if 1 <= t <= TB:
                        r = t - 1
                        dve.wait_ge(s_dve, now[r, 0])
                        dve.sem_inc(s_tE, 1)
                        now[r, 1] = step.did(dve.tensor_tensor(tmp[:, r % PB, 1, :], tmp[:, r % PB, 0, :], bias[:, B_UPD + l, :], ALU.add))
                    if 2 <= t <= TB + 1:
                        r = t - 2
                        tile = H[:, bass.ds(i * TB + r, 1), :]
                        hold(dve, "dve", s_dve, now[r, 1])
                        now[r, 2] = step.did(dve.tensor_tensor(tile, tmp[:, r % PB, 1:2, :], tile, ALU.add))
                    if t >= 3:
                        r = t - 3
                        hold(dve, "dve", s_dve, now[r, 2])
                        step.did(dve.bn_stats(stats[:, bass.ds(i * TB + r, 1), :], H[:, bass.ds(i * TB + r, 1), :]))
                step.leave(NB_LOOPS)

        def linear_dve(dve, step, l):
            base, last = STAGE0[f"lin{l}"], l == L1 - 1
            with dve.Fori(0, NB_LOOPS) as i:
                step.enter(i, (3 if last else 2) * TB)
                now = {}
                for t in range(TB + 3):
                    if t >= 3:
                        dve.wait_ge(s_dve, now[t - 3, 1])
                        dve.sem_inc(s_tE, 1)
                    if t < TB:
                        dve.wait_ge(s_tO, i * TB + (base + t + 1))
                        now[t, 0] = step.did(dve.tensor_tensor(tmp[:, t % PB, 0, :], psO[t % PB][0:P, D:2 * D], bias[:, B_LIN + l, :], ALU.add))
                    if 1 <= t <= TB:
                        r = t - 1
                        to = raw[:, r % PB, 0:1, :] if last else H[:, bass.ds(i * TB + r, 1), :]
                        hold(dve, "dve", s_dve, now[r, 0])
                        now[r, 1] = step.did(dve.scalar_tensor_tensor(
                            out=to, in0=psO[r % PB][0:P, 0:D].rearrange("p (o d) -> p o d", o=1), scalar=invdeg[:, bass.ds(i * TB + r, 1)],
                            in1=tmp[:, r % PB, 0:1, :], op0=ALU.mult, op1=ALU.add))
                    if 2 <= t <= TB + 1 and last:
                        r = t - 2
                        hold(dve, "dve", s_dve, now[r, 1])
                        tile = X[:, bass.ds(i * TB + r, 1), :]
                        step.did(dve.tensor_tensor(tile, tile, raw[:, r % PB, 0:1, :], ALU.add))
                step.leave(NB_LOOPS)
            step.last()
            if last:
                dve.sem_inc(s_fin, 1)

        def table_act(act, l):
            for c in range(NB_LOOPS + 1):
                if c < NB_LOOPS:
                    act.wait_ge(s_relu, l * NB_LOOPS + c + 1)
                    act.copy(TAB[:, 0, c * TB:(c + 1) * TB, 0, :], H[:, c * TB:(c + 1) * TB, :]).then_inc(s_hi, 1)
                if c >= 1:
                    at = slice((c - 1) * TB, c * TB)
                    act.wait_ge(s_rest, 2 * NT + l * NB_LOOPS + c)
                    act.copy(TAB[:, 0, at, 1, :], AGG[:, at, 0:D]).then_inc(s_mid, 1)

        def table_dve(dve, step, l):
            step.last()
            done = 2 * NT + l * NB_LOOPS
            for c in range(NB_LOOPS + 2):
                if c < NB_LOOPS:
                    at = slice(c * TB, (c + 1) * TB)
                    dve.tensor_scalar(H[:, at, :], H[:, at, :], 0.0, None, ALU.max).then_inc(s_relu, 1)
                if 1 <= c <= NB_LOOPS:
                    at = slice((c - 1) * TB, c * TB)
                    dve.wait_ge(s_relu, l * NB_LOOPS + c)
                    dve.wait_ge(s_hi, done + c)
                    dve.tensor_tensor(AGG[:, at, 0:D], H[:, at, :], TAB[:, 0, at, 0, :], ALU.subtract).then_inc(s_rest, 1)
                if c >= 2:
                    at = slice((c - 2) * TB, (c - 1) * TB)
                    dve.wait_ge(s_rest, done + c - 1)
                    dve.wait_ge(s_mid, done + c - 1)
                    dve.tensor_tensor(TAB[:, 0, at, 2, :], AGG[:, at, 0:D], TAB[:, 0, at, 1, :], ALU.subtract).then_inc(s_tab, 1)

        def general_dve(dve, step, k):
            tables = 2 if k < L0 else 1
            done = 2 * PAIRS * k + 2
            with dve.Fori(0, PAIRS) as i:
                step.enter(i, 2 * (4 + (3 if k < L0 else 1)))
                now = [0, 0]
                for u in range(2):
                    dve.wait_ge(g_idx, i * 2 + (u - 1 + done))
                    dve.wait_ge(g_sum, i * 2 + done)
                    now[u] = step.did(dve.tensor_copy(dcol[:, u:u + 1], didx[:, u:u + 1]))
                for u in range(2):
                    dve.wait_ge(g_dve, now[u])
                    dve.tensor_scalar(drep[:, u, :], ones[0:P, 0:P], dcol[:, u:u + 1], None, ALU.mult).then_inc(g_drep, 1)
                for u in range(2):
                    dve.wait_ge(g_dT, i * 2 + (u - 1 + done))
                    dve.tensor_scalar(same[:, u, :], psD[u][0:P, 0:P], dcol[:, u:u + 1], None, ALU.is_equal).then_inc(g_same, 1)
                for u in range(2):
                    dve.wait_ge(g_same, i * 2 + (u + 1 + done))
                    now[u] = step.did(dve.tensor_tensor_reduce(earlier[:, u, :], same[:, u, :], before[:], 1.0, 0.0,
                                                               ALU.mult, ALU.add, nearl[:, u:u + 1]))
                for u in range(2):
                    dve.wait_ge(g_dve, now[u])
                    step.did(dve.tensor_scalar(wsel[:, u, 0:1], nearl[:, u:u + 1], 0.0, None, ALU.is_gt))
                    now[u] = step.did(dve.tensor_tensor(wsel[:, u, 1:2], junk[:], dcol[:, u:u + 1], ALU.subtract))
                for u in range(2):
                    dve.wait_ge(g_dve, now[u])
                    dve.wait_ge(g_add[k][u], i * 16 + 16)
                    dve.scalar_tensor_tensor(out=widx[:, u:u + 1], in0=wsel[:, u, 1:2], scalar=wsel[:, u, 0:1],
                                             in1=dcol[:, u:u + 1], op0=ALU.mult, op1=ALU.add).then_inc(g_widx, 1)
                for u in range(2):
                    dve.wait_ge(g_rows[k][u], i * (16 * tables) + 16 * tables)
                    r = rows[:, u, 0:tables]
                    now[u] = step.did(dve.tensor_tensor(part[:, u, 0:tables, :], r[:, :, 0, :], r[:, :, 1, :], ALU.add))
                for u in range(2):
                    dve.wait_ge(g_dve, now[u])
                    r = rows[:, u, 0:tables]
                    if k >= L0:
                        dve.tensor_tensor(msg[:, u, 0:D], part[:, u, 0, :], r[:, 0, 2, :], ALU.add).then_inc(g_msg, 1)
                    else:
                        now[u] = step.did(dve.tensor_tensor(part[:, u], part[:, u], r[:, :, 2, :], ALU.add))
                if k < L0:
                    for u in range(2):
                        dve.wait_ge(g_dve, now[u])
                        now[u] = step.did(dve.tensor_tensor(part[:, u, 0, :], part[:, u, 0, :], part[:, u, 1, :], ALU.add))
                    for u in range(2):
                        dve.wait_ge(g_dve, now[u])
                        dve.tensor_scalar(msg[:, u, 0:D], part[:, u, 0, :], 0.0, None, ALU.max).then_inc(g_msg, 1)
                step.leave(PAIRS)
            dve.wait_ge(g_back, 32 * (k + 1))
            dve.tensor_tensor(AGG[:], AGG, AGG1, ALU.add).then_inc(s_agg, 1)

        block = ctx.enter_context(nc.Block())

        @block.sync
        def _(sp):
            sp.dma_start(X, x.rearrange("(t p) d -> p t d", p=P)).then_inc(s_x, 16)
            loads = [(wnat[:, ENC, :], W_enc), (wnat[:, OUT, :], W_out)]
            for l in range(L0):
                loads += [(wnat[:, MSG + 2 * l, :], msg_W1[l, :, 0:D]),
                          (wnat[:, MSG + 2 * l + 1, :], msg_W1[l, :, D:2 * D]),
                          (wnat[:, UPD_H + l, :], upd_W[l, :, 0:D]),
                          (wnat[:, UPD_M + l, :], upd_W[l, :, D:2 * D]),
                          (wnat[:, NW + l, :], msg_W2[l]),
                          (b2col[:, l:l + 1], msg_b2[l].rearrange("(d o) -> d o", o=1))]
            for l in range(L1):
                loads += [(wnat[:, LIN_L + l, :], Wl[l]), (wnat[:, LIN_R + l, :], Wr[l])]
            rows_of = [b_enc] + [v[l] for v in (msg_b1, upd_b, ln_g, ln_b) for l in range(L0)] \
                + [b_out] + [bl[l] for l in range(L1)]
            for k, b in enumerate(rows_of):
                loads.append((bias[:, k, :], b.rearrange("(o d) -> o d", o=1).to_broadcast([P, D])))
            assert len(loads) == LOADS
            for to, fr in loads:
                sp.dma_start(to, fr).then_inc(s_w, 16)
            sort_sp(sp)
            miss = load_flag(sp)
            for k in range(L0):
                edge_sp(sp, k, miss)
            sp.wait_ge(s_agg, L0)
            sp.dma_start(X, x.rearrange("(t p) d -> p t d", p=P)).then_inc(s_x, 16)
            for k in range(L0, L0 + L1):
                edge_sp(sp, k, miss)
            sp.wait_ge(s_fin, 1)
            sp.dma_start(out.rearrange("(t p) d -> p t d", p=P), X).then_inc(s_out, 16)
            sp.wait_ge(s_out, 16)

        @block.gpsimd
        def _(pool):
            pool.memset(ones[:], 1.0).then_inc(s_pset, 1)
            pool.memset(ident[:], 0.0).then_inc(s_pset, 1)
            pool.memset(zrow[:], 0.0).then_inc(s_pset, 1)
            pool.memset(eps[:], EPS).then_inc(s_pset, 1)
            pool.memset(abias[:], 0.0).then_inc(s_pset, 1)
            pool.iota(junki, pattern=[[0, 1]], base=N, channel_multiplier=1).then_inc(s_pset, 1)
            pool.iota(counti, pattern=[[1, 128]], base=0, channel_multiplier=0).then_inc(s_pset, 1)
            pool.iota(rowi, pattern=[[0, 1]], base=1, channel_multiplier=1).then_inc(s_pset, 1)
            pool.iota(tilei[:, 0, :], pattern=[[P, NT + 2]], base=0, channel_multiplier=0).then_inc(s_pset, 1)
            pool.iota(tilei[:, 1, :], pattern=[[P, NT + 2]], base=-1, channel_multiplier=0).then_inc(s_pset, 1)
            pool.memset(ones_bf[:], 1.0).then_inc(s_pset, 1)
            pool.wait_ge(s_pset, 11)
            pool.tensor_scalar(col1[:], counti, 1.0, None, ALU.add).then_inc(s_pset, 1)
            pool.tensor_copy(row1[:], rowi).then_inc(s_pset, 1)
            pool.tensor_copy(tilec[:], tilei).then_inc(s_pset, 1)
            pool.affine_select(out=below_bf[:], in_=ones_bf[:], compare_op=ALU.is_gt, fill=0.0, base=0,
                               pattern=[[1, 128]], channel_multiplier=-1).then_inc(s_pset, 1)
            pool.tensor_copy(junk[:], junki).then_inc(s_pset, 1)
            pool.affine_select(out=ident[:], in_=ident[:], compare_op=ALU.not_equal, fill=1.0, base=0,
                               pattern=[[-1, 128]], channel_multiplier=1).then_inc(s_pset, 1)
            pool.affine_select(out=before[:], in_=ones[0:P, 0:P], compare_op=ALU.is_gt, fill=0.0, base=0,
                               pattern=[[-1, P]], channel_multiplier=1).then_inc(s_pset, 1)
            pool.wait_ge(s_pset, 18)
            pool.tensor_copy(ident_bf[:], ident[:]).then_inc(s_pset, 1)
            pool.wait_ge(s_pset, 19)
            pool.sem_inc(s_const, 1)
            for empty in (s_in, s_tT, s_tC, s_tO, s_tE, s_raw):
                pool.sem_inc(empty, PB)
            for empty in (g_msg, g_widx, g_same, g_cp, g_sum,
                          o_read, o_tot, o_totc, o_rank, o_rkc, o_prod, o_pay, o_mul, o_mulv, o_slot, o_perm, o_S, o_turn, o_ST, o_cell, f_agg, l_agg):
                pool.sem_inc(empty, 2)
            for empty in (f_toN, f_toE, f_gat, f_hi, f_rest, f_mid, f_lo, f_sca, l_from, l_C, l_Cc, l_sum):
                pool.sem_inc(empty, BODY)
            for stored in o_store:
                pool.sem_inc(stored, 32)
            pool.memset(slots[:, :, NT, :], 0.0)
            pool.memset(selfs[:, 0:1], 0.0)
            sort_pool(pool)
            miss = load_flag(pool)
            stage_pool(pool, "enc", s_h, 1, X)
            for l in range(L0):
                if l == 0:
                    stage_pool(pool, "ab0", s_tE, STAGE0["enc"] + NT)
                else:
                    stage_pool(pool, f"ab{l}", s_h, l + 1)
                edge_pool(pool, l, miss)
                stage_pool(pool, f"upd{l}", s_agg, l + 1)
            stage_pool(pool, "out", s_h, L0 + 1)
            for l in range(L1):
                edge_pool(pool, L0 + l, miss)
                stage_pool(pool, f"lin{l}", s_agg, L0 + l + 1)

        @block.tensor
        def _(pe):
            pe.wait_ge(s_w, 16 * LOADS)
            pe.wait_ge(s_const, 1)
            for w in range(NW):
                if w >= 2:
                    pe.wait_ge(s_wTc, w - 1)
                pe.transpose(psT[w % 2][:, 0:D], wnat[:, w, :], ident[:]).then_inc(s_wT, 1)
            pe.wait_ge(s_wTc, NW)
            pe.wait_ge(s_b2, L0)
            for l in range(L0):
                pe.matmul(psO[l][:, 0:D], wnat[:, NW + l, :], wT[:, UPD_M + l, :], start=True, stop=True)
                pe.matmul(psO[l][0:P, D:2 * D], b2rep[:, l, :], wT[:, UPD_M + l, :], start=True, stop=True
                          ).then_inc(s_comp, 1)
            pe.wait_ge(s_compc, 2 * L0)
            sort_pe(pe)
            miss = load_flag(pe)
            stage_pe(pe, "enc", [(0, wT[:, ENC, :], 0, True)])
            for l in range(L0):
                stage_pe(pe, f"ab{l}", [(0, wT[:, MSG + 2 * l:MSG + 2 * l + 2, :].rearrange("k w d -> k (w d)"), 0, True)])
                edge_pe(pe, l, miss)
                stage_pe(pe, f"upd{l}", [(0, wT[:, UPD_H + l, :], 0, False), (1, wM[:, l, :], 0, True)])
            stage_pe(pe, "out", [(0, wT[:, OUT, :], 0, True)])
            for l in range(L1):
                edge_pe(pe, L0 + l, miss)
                stage_pe(pe, f"lin{l}", [(0, wT[:, LIN_R + l, :], D, True), (1, wT[:, LIN_L + l, :], 0, True)])

        @block.scalar
        def _(act):
            act.wait_ge(s_const, 1)
            norm_act(act, 0)
            for w in range(NW):
                act.wait_ge(s_wT, w + 1)
                act.copy(wT[:, w, :], psT[w % 2][:, 0:D]).then_inc(s_wTc, 1)
            for l in range(L0):
                act.wait_ge(s_comp, l + 1)
                act.copy(wM[:, l, :], psO[l][:, 0:D]).then_inc(s_compc, 1)
                act.copy(b2upd[:, l, :], psO[l][0:P, D:2 * D]).then_inc(s_compc, 1)
            sort_act(act)
            miss = load_flag(act)
            stage_act(act, "enc")
            for l in range(L0):
                stage_act(act, f"ab{l}", split=l)
                edge_act(act, l, miss)
                stage_act(act, f"upd{l}")
                norm_act(act, l + 1)
            stage_act(act, "out")
            norm_act(act, L0 + 1)
            for l in range(L1):
                table_act(act, l)
                edge_act(act, L0 + l, miss)
                stage_act(act, f"lin{l}")

        @block.vector
        def _(dve):
            step = Steps(dve, s_dve)
            gstep = Steps(dve, g_dve)
            dve.wait_ge(s_x, 16)
            for t in range(NT):
                step.did(dve.bn_stats(stats[:, t, :], X[:, t, :]))
            norm_dve(dve, step, 0, X, X)
            step.last()
            dve.tensor_scalar(X, X, 0.0, None, ALU.max).then_inc(s_h, 1)
            dve.wait_ge(s_const, 1)
            dve.wait_ge(s_w, 16 * LOADS)
            for l in range(L0):
                dve.tensor_scalar(b2rep[:, l, :], ones[:, 0:P], b2col[:, l:l + 1], None, ALU.mult).then_inc(s_b2, 1)
                step.did(dve.tensor_copy(abias[:, l, 1, :], bias[:, B_1 + l, :]))
            sort_dve(dve)
            miss = load_flag(dve)
            dve.memset(Hs[:, 0, :], 0.0)
            dve.memset(AGGs[:, 0, :], 0.0)
            with dve.Fori(0, NB_LOOPS) as i:
                for t in range(TB):
                    hold(dve, "dve", s_tO, i * TB + (STAGE0["enc"] + t + 1))
                    dve.tensor_tensor(H[:, bass.ds(i * TB + t, 1), :], psO[t % PB][0:P, 0:D].rearrange("p (o d) -> p o d", o=1),
                                      bias[:, B_ENC:B_ENC + 1, :], ALU.add).then_inc(s_tE, 1)
            for l in range(L0):
                split_dve(dve, l)
                edge_dve(dve, gstep, l, miss)
                if l == 0:
                    dve.wait_ge(s_agg, 1)
                    step.did(dve.tensor_copy(degc[:], AGG[:, :, D]))
                    step.last()
                    step.did(dve.tensor_scalar(sq[:], degc[:], 1.0, None, ALU.max))
                    step.last()
                    step.did(dve.reciprocal(invdeg[:], sq[:]))
                update_dve(dve, step, l)
                norm_dve(dve, step, l + 1, H, H, l)
            dve.wait_ge(s_x, 32)
            with dve.Fori(0, NB_LOOPS) as i:
                step.enter(i, 3 * TB)
                now = {}
                for t in range(TB + 2):
                    if t < TB:
                        dve.wait_ge(s_tO, i * TB + (STAGE0["out"] + t + 1))
                        now[t, 0] = step.did(dve.tensor_tensor(tmp[:, t % PB, 0, :], psO[t % PB][0:P, 0:D], bias[:, B_OUT, :], ALU.add))
                    if 1 <= t <= TB:
                        r = t - 1
                        tile = X[:, bass.ds(i * TB + r, 1), :]
                        hold(dve, "dve", s_dve, now[r, 0])
                        dve.sem_inc(s_tE, 1)
                        now[r, 1] = step.did(dve.tensor_tensor(tile, tile, tmp[:, r % PB, 0:1, :], ALU.add))
                    if t >= 2:
                        r = t - 2
                        hold(dve, "dve", s_dve, now[r, 1])
                        step.did(dve.bn_stats(stats[:, bass.ds(i * TB + r, 1), :], X[:, bass.ds(i * TB + r, 1), :]))
                step.leave(NB_LOOPS)
            norm_dve(dve, step, L0 + 1, X, H)
            for l in range(L1):
                table_dve(dve, step, l)
                dve.wait_ge(s_tab, (l + 1) * NB_LOOPS)
                edge_dve(dve, gstep, L0 + l, miss)
                linear_dve(dve, step, l)


_INS = ["x", "src", "dst", "L0_gnn_W_enc", "L0_gnn_b_enc", "L0_gnn_msg_W1", "L0_gnn_msg_b1", "L0_gnn_msg_W2",
        "L0_gnn_msg_b2", "L0_gnn_upd_W", "L0_gnn_upd_b", "L0_gnn_ln_g", "L0_gnn_ln_b", "L0_gnn_W_out",
        "L0_gnn_b_out", "L1_gnn_Wl", "L1_gnn_bl", "L1_gnn_Wr"]


def kernel(**inputs):
    import numpy as np
    import concourse.bacc as bacc
    from concourse.bass_utils import run_bass_kernel_spmd as run

    nc = bacc.Bacc("TRN2", target_bir_lowering=False, num_devices=1)
    arrays, args = {}, []
    for name in _INS:
        a = np.ascontiguousarray(inputs[name])
        arrays[f"in_{name}"] = a
        args.append(nc.dram_tensor(f"in_{name}", a.shape, mybir.dt.from_np(a.dtype), kind="ExternalInput").ap())
    args.append(nc.dram_tensor("out_0", (N, D), F32, kind="ExternalOutput").ap())
    build(nc, *args)
    return run(nc, [arrays], core_ids=[0]).results[0]["out_0"]
```
